# Optimizing a Trainium2 kernel written in Bass

```python
import numpy as np
import jax
import jax.numpy as jnp

def _softmax(x, axis=-1):
    return jax.nn.softmax(x, axis=axis)

def _gelu(x):
    return jax.nn.gelu(x, approximate=True)

def _silu(x):
    return jax.nn.silu(x)

def _sigmoid(x):
    return jax.nn.sigmoid(x)

def _layernorm(x, axis=-1, eps=1e-05):
    m = jnp.mean(x, axis=axis, keepdims=True)
    v = jnp.var(x, axis=axis, keepdims=True)
    return (x - m) / jnp.sqrt(v + eps)

def _scatter_add(tgt, idx, src, axis=0):
    return tgt.at[idx].add(src)

def _segment_sum(src, seg, n):
    return jax.ops.segment_sum(src, seg, n)
kernel_name = 'mk_gps_d1_gnn_r8_a391cb'

def setup_inputs(seed: int=0):
    np.random.seed(seed)
    _w = jnp.asarray

    def _rec_inputs():
        import jax
        import jax.numpy as jnp
        _gk = jax.random.key(seed)
        x = -5.39e-05 + 0.9998 * jax.random.normal(jax.random.fold_in(_gk, 1), (12500, 256), jnp.float32)
        _s = jax.random.randint(jax.random.fold_in(_gk, 2), (100000,), 0, 12500, jnp.int32)
        _d = jax.random.randint(jax.random.fold_in(_gk, 3), (100000,), 0, 12500, jnp.int32)
        _loop = jnp.arange(12500, dtype=jnp.int32)
        src = jnp.concatenate([_s, _d, _loop])
        dst = jnp.concatenate([_d, _s, _loop])
        _o = jnp.argsort(dst, stable=True)
        src = src[_o]
        dst = dst[_o]
        return (x, src, dst)
    x, src, dst = _rec_inputs()

    def _L0_gnn_setup():
        import jax, jax.numpy as jnp
        import numpy as np
        NUM_NODES = 12500
        IN_CH = 256
        HIDDEN = 128
        OUT_CH = 256
        NUM_EDGES = 400000

        def gcn_conv(x, W, b, src, dst, num_nodes):
            h = x @ W
            loop = jnp.arange(num_nodes, dtype=src.dtype)
            s = jnp.concatenate([src, loop])
            d = jnp.concatenate([dst, loop])
            deg = jax.ops.segment_sum(jnp.ones_like(d, dtype=h.dtype), d, num_segments=num_nodes)
            dinv = jnp.where(deg > 0, jax.lax.rsqrt(deg), 0.0)
            norm = dinv[s] * dinv[d]
            msg = h[s] * norm[:, None]
            out = jax.ops.segment_sum(msg, d, num_segments=num_nodes)
            return out + b
        key = jax.random.key(seed)
        k1, k2, k3, k4 = jax.random.split(key, 4)
        edge_index = jax.random.randint(k1, (2, NUM_EDGES), 0, NUM_NODES, dtype=jnp.int64)
        node_features = jax.random.normal(k2, (NUM_NODES, IN_CH), dtype=jnp.float32)
        W1 = jax.random.normal(k3, (IN_CH, HIDDEN), dtype=jnp.float32) * (1.0 / np.sqrt(IN_CH))
        b1 = jnp.zeros((HIDDEN,), dtype=jnp.float32)
        W2 = jax.random.normal(k4, (HIDDEN, OUT_CH), dtype=jnp.float32) * (1.0 / np.sqrt(HIDDEN))
        b2 = jnp.zeros((OUT_CH,), dtype=jnp.float32)
        return {'node_features': node_features, 'W1': W1, 'b1': b1, 'W2': W2, 'b2': b2, 'edge_index': edge_index}
    _L0_gnn_all = _L0_gnn_setup()
    _L0_gnn_in = {k: v for k, v in _L0_gnn_all.items() if k in ('W1', 'b1', 'W2', 'b2')}
    del _L0_gnn_all

    def _L0_mix_setup():
        import jax, jax.numpy as jnp
        import numpy as np
        N, F, C, H = (32, 512, 256, 8)
        D = C // H
        EPS_ATTN = 1e-06
        EPS_LN = 1e-05

        def layer_norm(x, g, b):
            mu = jnp.mean(x, axis=-1, keepdims=True)
            var = jnp.var(x, axis=-1, keepdims=True)
            return (x - mu) * jax.lax.rsqrt(var + EPS_LN) * g + b
        key = jax.random.key(seed)
        ks = jax.random.split(key, 8)
        s = 1.0 / np.sqrt(C)
        return {'x': jax.random.normal(ks[0], (N, F, C), jnp.float32), 'Wqkv': jax.random.uniform(ks[1], (3 * C, C), jnp.float32, -s, s), 'ln1_g': jnp.ones((C,), jnp.float32), 'ln1_b': jnp.zeros((C,), jnp.float32), 'W1': jax.random.uniform(ks[2], (C, C), jnp.float32, -s, s), 'b1': jax.random.uniform(ks[3], (C,), jnp.float32, -s, s), 'W2': jax.random.uniform(ks[4], (C, C), jnp.float32, -s, s), 'b2': jax.random.uniform(ks[5], (C,), jnp.float32, -s, s), 'ln2_g': jnp.ones((C,), jnp.float32), 'ln2_b': jnp.zeros((C,), jnp.float32)}
    _L0_mix_all = _L0_mix_setup()
    _L0_mix_in = {k: v for k, v in _L0_mix_all.items() if k in ('Wqkv', 'ln1_g', 'ln1_b', 'W1', 'b1', 'W2', 'b2', 'ln2_g', 'ln2_b')}
    del _L0_mix_all

    def _L0_ffn_setup():
        import jax, jax.numpy as jnp
        import numpy as np
        B, S, D, E, H, K = (4, 512, 256, 8, 512, 2)
        key = jax.random.key(seed)
        ks = jax.random.split(key, 6)
        x = jax.random.normal(ks[0], (B, S, D), jnp.float32)
        Wg = jax.random.normal(ks[1], (D, E), jnp.float32) * 0.02
        bg = jnp.zeros((E,), jnp.float32)
        W1 = jax.random.normal(ks[2], (E, D, H), jnp.float32) * 0.02
        b1 = jnp.zeros((E, H), jnp.float32)
        W2 = jax.random.normal(ks[3], (E, H, D), jnp.float32) * 0.02
        b2 = jnp.zeros((E, D), jnp.float32)
        return {'x': x, 'Wg': Wg, 'bg': bg, 'W1': W1, 'b1': b1, 'W2': W2, 'b2': b2}
    _L0_ffn_all = _L0_ffn_setup()
    _L0_ffn_in = {k: v for k, v in _L0_ffn_all.items() if k in ('Wg', 'bg', 'W1', 'b1', 'W2', 'b2')}
    del _L0_ffn_all
    return {'x': x, 'src': src, 'dst': dst, 'L0_gnn_W1': _L0_gnn_in['W1'], 'L0_gnn_b1': _L0_gnn_in['b1'], 'L0_gnn_W2': _L0_gnn_in['W2'], 'L0_gnn_b2': _L0_gnn_in['b2'], 'L0_mix_Wqkv': _L0_mix_in['Wqkv'], 'L0_mix_ln1_g': _L0_mix_in['ln1_g'], 'L0_mix_ln1_b': _L0_mix_in['ln1_b'], 'L0_mix_W1': _L0_mix_in['W1'], 'L0_mix_b1': _L0_mix_in['b1'], 'L0_mix_W2': _L0_mix_in['W2'], 'L0_mix_b2': _L0_mix_in['b2'], 'L0_mix_ln2_g': _L0_mix_in['ln2_g'], 'L0_mix_ln2_b': _L0_mix_in['ln2_b'], 'L0_ffn_Wg': _L0_ffn_in['Wg'], 'L0_ffn_bg': _L0_ffn_in['bg'], 'L0_ffn_W1': _L0_ffn_in['W1'], 'L0_ffn_b1': _L0_ffn_in['b1'], 'L0_ffn_W2': _L0_ffn_in['W2'], 'L0_ffn_b2': _L0_ffn_in['b2']}

def reference(x, src, dst, L0_gnn_W1, L0_gnn_b1, L0_gnn_W2, L0_gnn_b2, L0_mix_Wqkv, L0_mix_ln1_g, L0_mix_ln1_b, L0_mix_W1, L0_mix_b1, L0_mix_W2, L0_mix_b2, L0_mix_ln2_g, L0_mix_ln2_b, L0_ffn_Wg, L0_ffn_bg, L0_ffn_W1, L0_ffn_b1, L0_ffn_W2, L0_ffn_b2):
    import jax
    import jax.numpy as jnp

    def _L0_gnn_ref(node_features, W1, b1, W2, b2, edge_index):
        import jax, jax.numpy as jnp
        import numpy as np
        NUM_NODES = 12500
        IN_CH = 256
        HIDDEN = 128
        OUT_CH = 256
        NUM_EDGES = 400000

        def gcn_conv(x, W, b, src, dst, num_nodes):
            h = x @ W
            loop = jnp.arange(num_nodes, dtype=src.dtype)
            s = jnp.concatenate([src, loop])
            d = jnp.concatenate([dst, loop])
            deg = jax.ops.segment_sum(jnp.ones_like(d, dtype=h.dtype), d, num_segments=num_nodes)
            dinv = jnp.where(deg > 0, jax.lax.rsqrt(deg), 0.0)
            norm = dinv[s] * dinv[d]
            msg = h[s] * norm[:, None]
            out = jax.ops.segment_sum(msg, d, num_segments=num_nodes)
            return out + b
        src, dst = (edge_index[0], edge_index[1])
        x = gcn_conv(node_features, W1, b1, src, dst, NUM_NODES)
        x = jax.nn.relu(x)
        x = gcn_conv(x, W2, b2, src, dst, NUM_NODES)
        return x

    def _L0_mix_ref(x, Wqkv, ln1_g, ln1_b, W1, b1, W2, b2, ln2_g, ln2_b):
        import jax, jax.numpy as jnp
        import numpy as np
        N, F, C, H = (32, 512, 256, 8)
        D = C // H
        EPS_ATTN = 1e-06
        EPS_LN = 1e-05

        def layer_norm(x, g, b):
            mu = jnp.mean(x, axis=-1, keepdims=True)
            var = jnp.var(x, axis=-1, keepdims=True)
            return (x - mu) * jax.lax.rsqrt(var + EPS_LN) * g + b
        n, f, c = x.shape
        qkv = jnp.einsum('nfc,oc->nfo', x, Wqkv)
        q, k, v = jnp.split(qkv, 3, axis=-1)
        q = q.reshape(n, f, H, D)
        k = k.reshape(n, f, H, D)
        v = v.reshape(n, f, H, D)
        q = jax.nn.elu(q) + 1.0
        k = jax.nn.elu(k) + 1.0
        kv = jnp.einsum('nshd,nshm->nhmd', k, v)
        ksum = jnp.sum(k, axis=1)
        z = 1.0 / (jnp.einsum('nlhd,nhd->nlh', q, ksum) + EPS_ATTN)
        t = jnp.einsum('nlhd,nhmd,nlh->nlhm', q, kv, z)
        t = t.reshape(n, f, c)
        x1 = layer_norm(t + x, ln1_g, ln1_b)
        h = jax.nn.gelu(jnp.einsum('nfc,oc->nfo', x1, W1) + b1, approximate=False)
        y = jnp.einsum('nfc,oc->nfo', h, W2) + b2
        return layer_norm(y + x1, ln2_g, ln2_b)

    def _L0_ffn_ref(x, Wg, bg, W1, b1, W2, b2):
        import jax, jax.numpy as jnp
        import numpy as np
        B, S, D, E, H, K = (4, 512, 256, 8, 512, 2)
        Bv, Sv, Dv = x.shape
        gate_scores = x @ Wg + bg
        _, idx = jax.lax.top_k(gate_scores, K)
        mask = jax.nn.one_hot(idx, E, dtype=x.dtype).sum(axis=-2)
        xf = x.reshape(-1, Dv)
        mf = mask.reshape(-1, E)
        h = jax.nn.gelu(jnp.einsum('td,edh->teh', xf, W1) + b1[None], approximate=False)
        y = jnp.einsum('teh,ehd->ted', h, W2) + b2[None]
        out = jnp.einsum('ted,te->td', y, mf)
        return out.reshape(Bv, Sv, Dv)
    edge_index = jnp.stack([src, dst])
    xn = _layernorm(x, axis=-1)
    x = x + _L0_gnn_ref(xn, L0_gnn_W1, L0_gnn_b1, L0_gnn_W2, L0_gnn_b2, edge_index) + _L0_mix_ref(xn[None], L0_mix_Wqkv, L0_mix_ln1_g, L0_mix_ln1_b, L0_mix_W1, L0_mix_b1, L0_mix_W2, L0_mix_b2, L0_mix_ln2_g, L0_mix_ln2_b)[0]
    x = x + _L0_ffn_ref(_layernorm(x, axis=-1)[None], L0_ffn_Wg, L0_ffn_bg, L0_ffn_W1, L0_ffn_b1, L0_ffn_W2, L0_ffn_b2)[0]
    return x

_drawn_inputs = setup_inputs


def setup_inputs(seed=0):
    import zlib

    import numpy as np

    out = dict(_drawn_inputs(seed))
    spreads = {'L0_gnn_b1': (0.0, 0.279),
     'L0_gnn_b2': (0.0, 0.1),
     'L0_mix_ln1_g': (1.0, 0.2),
     'L0_mix_ln1_b': (0.0, 0.1),
     'L0_mix_ln2_g': (1.0, 0.2),
     'L0_mix_ln2_b': (0.0, 0.1),
     'L0_ffn_bg': (0.0, 0.1),
     'L0_ffn_b1': (0.0, 0.456),
     'L0_ffn_b2': (0.0, 0.1)}
    factors = {'L0_mix_Wqkv': 7.707, 'L0_mix_b1': 6.372, 'L0_mix_b2': 2.686}
    for name, (base, spread) in spreads.items():
        noise = np.random.default_rng([zlib.crc32(name.encode()), seed]).standard_normal(out[name].shape)
        drawn = base * np.exp(spread * noise) if base else spread * noise
        out[name] = jnp.asarray(drawn.astype(out[name].dtype))
    for name, factor in factors.items():
        out[name] = (out[name] * factor).astype(out[name].dtype)
    return out
```

```python
from contextlib import ExitStack

import concourse.bass as bass
from concourse import mybir

F32 = mybir.dt.float32
BF16 = mybir.dt.bfloat16
I32 = mybir.dt.int32
ALU = mybir.AluOpType
ACT = mybir.ActivationFunctionType
AX = mybir.AxisListType
DVE_ONLY = (mybir.EngineType.DVE,)
PE_ONLY = (mybir.EngineType.PE,)
ds = bass.ds

P = 125
ROWS16 = 112
EPS_LN = 1e-5
EPS_ATTN = 1e-6


class Steps:

    def __init__(self, eng, sem, base, per_body):
        self.eng, self.sem, self.base, self.n, self.per_body = eng, sem, base, 0, per_body

    def did(self, ins):
        ins.then_inc(self.sem, 1)
        self.n += 1

    def settle(self):
        self.eng.wait_ge(self.sem, self.base + self.n)

    def end(self):
        assert self.per_body is None or self.n == self.per_body, (self.n, self.per_body)


def spread(ap, dim, n):
    ap = ap.unsqueeze(dim)
    return ap.broadcast_to(tuple(n if i == dim else d for i, d in enumerate(ap.shape)))


def row_pieces(dst, src):
    yield dst[0:ROWS16], src[0:ROWS16]
    yield dst[ROWS16:P], src[ROWS16:P]


def move_rows(eng, dst, src, sem):
    for d, s in row_pieces(dst, src):
        eng.dma_start(d, s).then_inc(sem, 16)


class Kernel:
    def __init__(self, nc, ctx, t):
        self.nc, self.ctx, self.t, self.phase_sems = nc, ctx, t, []
        self.N, self.C = t["x"].shape
        self.NT = self.N // P
        self.E = t["src"].shape[0]
        self.ET = self.E // P
        self.EPT = self.ET // self.NT
        self.F = t["gnn_W1"].shape[1]
        assert self.N == self.NT * P and self.ET == self.EPT * self.NT and self.NT % 4 == 0
        assert self.F == 128 and self.C == 256

    def sb(self, name, shape, dt=F32):
        return self.ctx.enter_context(self.nc.sbuf_tensor(name, shape, dt))

    def sem(self, name):
        self.phase_sems.append(self.nc.alloc_semaphore(name=name))
        return self.phase_sems[-1]

    def end_phase(self):
        self.nc.all_engine_barrier()
        self.nc.clear_and_free_semaphores(self.phase_sems)
        self.nc.all_engine_barrier()
        self.phase_sems = []

    def dram(self, name, shape, dt=F32):
        return self.nc.dram_tensor(name, shape, dt, kind="Internal").ap()

    def carve(self, flat):
        at = [0]

        def take(n):
            at[0] += n
            assert at[0] <= flat.shape[1], (at[0], flat.shape)
            return flat[:, at[0] - n:at[0]]
        return take

    def inverse_std(self, act, out, var, ln_done, count, done):
        self.nc.scalar.activation(out, var, ACT.Ln, bias=self.epsc[:, 0:1]).then_inc(ln_done, 1)
        act.wait_ge(ln_done, count)
        self.nc.scalar.activation(out, out, ACT.Exp, scale=-0.5).then_inc(done, 1)

    def pipeline(self, eng, stages, tiles, ring=2):
        deepest = max(lag for lag, _ in stages)
        first = -(-(deepest + ring) // ring) * ring
        last = tiles - tiles % ring

        def step(i, h):
            for lag, stage in stages:
                n = ring * i + h - lag if isinstance(i, int) else i * ring + (h - lag)
                if isinstance(n, int) and not 0 <= n < tiles:
                    continue
                stage(n, (h - lag) % ring, i + (h - lag) // ring)
        for k in range(first):
            step(k // ring, k % ring)
        with eng.Fori(first // ring, last // ring) as i:
            for h in range(ring):
                step(i, h)
        for k in range(last, tiles + deepest):
            step(k // ring, k % ring)

    def allocate(self):
        NT, ET, EPT, F, C = self.NT, self.ET, self.EPT, self.F, self.C
        self.bank = [self.ctx.enter_context(self.nc.psum_tensor(f"bank{i}", [128, 512], F32)) for i in range(8)]
        self.nodes1 = self.sb("nodes1", [128, NT * F])
        self.aggT = self.sb("aggT", [128, (NT + 1) * P])
        self.SLOTS = 2 * EPT
        self.rows_flat = self.sb("gathered_rows", [128, self.SLOTS * F])
        self.rows = self.rows_flat[0:P, :].rearrange("p (a f) -> p a f", f=F)
        self.srcT = self.sb("srcT", [P, ET], I32)
        self.dstT = self.sb("dstT", [P, ET])
        self.DPAD = 20
        self.winstart = self.sb("window_start", [1, NT * self.DPAD], I32)
        self.dinv = self.sb("dinv", [P, NT])
        self.ident = self.sb("ident", [128, 128])
        self.iota = self.sb("iota", [P, 128])
        self.ones = self.sb("ones", [128, 128])
        self.kvbd = self.sb("kv_blockdiag", [128, 2, 132])
        self.gW1 = self.sb("gnn_W1", [128, 2, F])
        self.Wqkv = self.sb("Wqkv", [128, 2, 3 * C])
        self.mW1 = self.sb("mix_W1", [128, 2, C])
        self.mW2 = self.sb("mix_W2", [128, 2, C])
        self.gW2 = self.sb("gnn_W2", [128, C])
        self.mb1 = self.sb("mix_b1", [128, 2])
        self.brow = {k: self.sb("row_" + k, [P, C]) for k in ("mix_b2", "ln1_g", "ln1_b", "ln2_g", "ln2_b", "gnn_b2")}
        self.gb1 = self.sb("gnn_b1", [P, F])
        NE, H = self.t["ffn_W1"].shape[1], self.t["ffn_W1"].shape[3]
        self.NE, self.H = NE, H
        self.Wg, self.bg = self.sb("ffn_Wg", [128, 2, NE]), self.sb("ffn_bg", [P, NE])
        self.slots = self.sb("slots", [P, 2, NT], I32)
        self.WE = 2 * H + H // 128
        self.W1e = self.nodes1[:, 0:NE * self.WE]
        self.b2e = self.nodes1[0:1, NE * self.WE:NE * (self.WE + C)]
        self.W2e = self.aggT[:, 0:NE * (H // 128) * C]
        self.gates = self.rows_flat[0:P, :][:, 0:NT * NE]
        self.W1s = [self.rows_flat[:, b * self.WE:(b + 1) * self.WE] for b in range(2)]
        self.W1_in = self.sem("W1_in")
        self.idx = [self.sb(f"idx{b}", [P, EPT], I32) for b in range(2)]
        self.onehot = [self.sb(f"onehot{b}", [P, EPT, P]) for b in range(2)]
        self.zeros = self.sb("zeros", [P, C])
        self.held = self.sb("held", [1, 2])
        self.zeros_made, self.slots_zeroed = self.sem("zeros_made"), self.sem("slots_zeroed")
        self.epsc = self.sb("eps_ln", [P, 1])
        self.work = self.sb("work", [128, 4200])
        self.t_g1 = self.dram("g1_table", [self.N, F])
        self.t_g2 = self.dram("g2_table", [self.N, F])
        self.d_xn = self.dram("xn_rows", [self.N, C])
        self.d_xnT = self.dram("xnT_tiles", [NT, 128, 2 * P])
        self.d_xmix = self.dram("xmix_rows", [self.N, C])
        self.d_x2 = self.dram("x2_rows", [self.N, C])
        self.d_xm = self.dram("xm_rows", [self.N, C])
        self.ST = 2 * NT + 8
        self.eid = self.sb("tile_expert", [1, (self.ST // 2) * 4], I32)
        self.d_xs = self.dram("expert_in_rows", [self.ST * P, C])
        self.d_ys = self.dram("expert_out_rows", [self.ST * P, C])
        self.phase_sems = []

    def tile_rows(self, ap, n):
        return ap[ds(n * P, P), :]

    def setup(self):
        nc, t, NT, ET, EPT = self.nc, self.t, self.NT, self.ET, self.EPT
        weights_in, raw_in = self.sem("weights_in"), self.sem("raw_in")
        made, idn = self.sem("constants_made"), self.sem("identity_made")
        floated, turned, taken = self.sem("raw_floated"), self.sem("blocks_turned"), self.sem("blocks_taken")
        starts_out, chain = self.sem("starts_spread"), self.sem("setup_chain")
        NBLK = ET // 100
        raw = self.nodes1[0:100, 0:2 * NBLK * P].bitcast(I32).rearrange("p (a b e) -> p a b e", a=2, b=NBLK)
        flt = self.nodes1[0:100, 2 * NBLK * P:4 * NBLK * P].rearrange("p (a b e) -> p a b e", a=2, b=NBLK)
        take = self.carve(self.aggT)
        exact = lambda *shape: take(-(-shape[0] * shape[1] // 2))[0:P].bitcast(BF16)[:, 0:shape[0] * shape[1]]
        self.lo, self.hi = exact(NT, EPT), exact(NT, EPT)
        self.lo_is = exact(P, EPT).rearrange("p (m e) -> p m e", e=EPT)
        self.hi_is = exact(NT, EPT).rearrange("p (m e) -> p m e", e=EPT)
        self.ohl = [exact(P, EPT).rearrange("p (m e) -> p m e", e=EPT) for _ in range(2)]
        self.ohh = [exact(NT, EPT).rearrange("p (m e) -> p m e", e=EPT) for _ in range(2)]
        self.xnT = [take(2 * P).rearrange("p (k n) -> p k n", k=2) for _ in range(2)]
        self.zer = take(260)
        whole, tmp = take(ET)[0:P], take(ET)[0:P]
        loads = [
            (self.gW1[:, :, :], t["gnn_W1"].rearrange("(k p) f -> p k f", p=128)),
            (self.Wqkv[:, :, :], t["mix_WqkvT"].rearrange("(k p) f -> p k f", p=128)),
            (self.mW1[:, :, :], t["mix_W1T"].rearrange("(k p) f -> p k f", p=128)),
            (self.mW2[:, :, :], t["mix_W2T"].rearrange("(k p) f -> p k f", p=128)),
            (self.gW2[:, :], t["gnn_W2"]),
            (self.mb1[:, :], t["mix_b1"]),
            (self.gb1[:, :], spread(t["gnn_b1"], 0, P)),
            (self.Wg[:, :, :], t["ffn_Wg"].rearrange("(k p) e -> p k e", p=128)),
            (self.bg[:, :], spread(t["ffn_bg"], 0, P)),
        ] + [(self.brow[k][:, :], spread(t[k], 0, P)) for k in self.brow]

        with nc.Block() as block:
            @block.sync
            def _(sp):
                for a, name in enumerate(("src", "dst")):
                    sp.dma_start(raw[:, a, :, :], t[name].rearrange("(b p e) -> p b e", p=100, e=P)).then_inc(raw_in, 16)
                for dst, src in loads:
                    sp.dma_start(dst, src).then_inc(weights_in, 16)
                sp.wait_ge(weights_in, 16 * len(loads))

            @block.gpsimd
            def _(pool):
                nc.gpsimd.memset(self.ident[:, :], 0.0).then_inc(idn, 1)
                pool.wait_ge(idn, 1)
                nc.gpsimd.affine_select(out=self.ident[:, :], in_=self.ident[:, :], compare_op=ALU.not_equal, fill=1.0,
                                        base=0, pattern=[[-1, 128]], channel_multiplier=1).then_inc(idn, 1)
                nc.gpsimd.iota(self.iota[:, :], pattern=[[1, 128]], base=0, channel_multiplier=0,
                               allow_small_or_imprecise_dtypes=True).then_inc(made, 1)
                for out, m in ((self.lo_is, P), (self.hi_is, NT)):
                    nc.gpsimd.iota(out, pattern=[[1, m], [0, EPT]], base=0, channel_multiplier=0,
                                   allow_small_or_imprecise_dtypes=True).then_inc(made, 1)
                nc.gpsimd.memset(self.ones[:, :], 1.0).then_inc(made, 1)
                nc.gpsimd.memset(self.kvbd[:, :, :], 0.0).then_inc(made, 1)
                pool.wait_ge(idn, 2)
                nc.gpsimd.memset(self.held[:, :], 0.0).then_inc(made, 1)
                pool.wait_ge(made, 6)

            @block.tensor
            def _(pe):
                pe.wait_ge(idn, 2)
                pe.wait_ge(floated, 2)
                n = 0
                for a in range(2):
                    for b0 in range(0, NBLK, 4):
                        if n >= 4:
                            pe.wait_ge(taken, n - 3)
                        for b in range(b0, min(b0 + 4, NBLK)):
                            mm = nc.tensor.transpose(self.bank[n % 4][0:P, (b - b0) * 100:(b - b0 + 1) * 100],
                                                     flt[:, a, b, :], self.ident[0:100, 0:100])
                        mm.then_inc(turned, 1)
                        n += 1
                pe.wait_ge(made, 5)
                pe.wait_ge(taken, n)
                for c in range(4):
                    w = ET // 4
                    mm = nc.tensor.matmul(self.bank[4 + c][0:P, 0:w], self.ones[0:1, 0:P],
                                          self.dstT[0:1, c * w:(c + 1) * w], start=True, stop=True)
                    mm.then_inc(starts_out, 1)

            @block.vector
            def _(dve):
                dve.wait_ge(raw_in, 32)
                for a in range(2):
                    nc.vector.tensor_copy(flt[:, a, :, :], raw[:, a, :, :]).then_inc(floated, 1)
                n = 0
                for a, out in enumerate((self.srcT, self.dstT)):
                    for b0 in range(0, NBLK, 4):
                        k = min(4, NBLK - b0) * 100
                        dve.wait_ge(turned, n + 1)
                        nc.vector.tensor_copy(out[:, b0 * 100:b0 * 100 + k], self.bank[n % 4][0:P, 0:k]).then_inc(taken, 1)
                        n += 1
                dve.wait_ge(taken, n)
                c = Steps(dve, chain, 0, 7)
                c.did(nc.vector.tensor_scalar(tmp, self.dstT[:, :], 1.0 / P, 0.5 / P - 0.5, ALU.mult, ALU.add))
                c.settle()
                c.did(nc.vector.tensor_scalar(whole, tmp, 12582912.0, None, ALU.add))
                c.settle()
                c.did(nc.vector.tensor_scalar(tmp, whole, 12582912.0, None, ALU.subtract))
                c.settle()
                c.did(nc.vector.tensor_copy(self.hi, tmp))
                c.did(nc.vector.scalar_tensor_tensor(out=self.lo, in0=tmp, scalar=-float(P), in1=self.dstT[:, :],
                                                     op0=ALU.mult, op1=ALU.add))
                start = self.winstart[0:1, :].rearrange("a (n d) -> a n d", d=self.DPAD)
                c.did(nc.vector.memset(self.winstart[0:1, :], 0))
                c.settle()
                c.did(nc.vector.tensor_scalar(start[:, :, 0:EPT], self.dstT[0:1, :].rearrange("a (n e) -> a n e", e=EPT),
                                              0.0, float(self.N), ALU.max, ALU.min))
                c.settle()
                c.end()
                nc.vector.memset(self.epsc[:, :], EPS_LN).then_inc(taken, 1)
                nc.vector.memset(self.zeros[:, :], 0.0).then_inc(self.zeros_made, 1)
                dve.wait_ge(weights_in, 16 * len(loads))
                nc.vector.tensor_tensor(self.brow["ln2_b"][:, :], self.brow["ln2_b"][:, :], self.brow["gnn_b2"][:, :],
                                        ALU.add).then_inc(taken, 1)
                n += 2
                for k in range(4):
                    w = ET // 4
                    dve.wait_ge(starts_out, 4)
                    nc.vector.tensor_tensor(self.dstT[:, k * w:(k + 1) * w], self.dstT[:, k * w:(k + 1) * w],
                                            self.bank[4 + k][0:P, 0:w], ALU.subtract).then_inc(taken, 1)
                dve.wait_ge(taken, n + 4)

    def project(self):
        nc, t, NT, EPT, F, C = self.nc, self.t, self.NT, self.EPT, self.F, self.C
        s = {k: self.sem("p1_" + k) for k in (
            "stats", "var", "ln", "rstd", "xn", "xn_turned", "xnT", "h", "h1", "hot", "hist", "zeroed", "counted")}
        RX = 4
        x_in = [self.sem(f"p1_x_in{b}") for b in range(RX)]
        xn_st, xT_st = ([self.sem(f"p1_{k}{b}") for b in range(2)] for k in ("xn_stored", "xnT_stored"))
        take = self.carve(self.work)
        xb, xn = [take(C)[0:P] for _ in range(RX)], [take(C)[0:P] for _ in range(2)]
        small = take(40)[0:P]
        st = [small[:, 8 * b:8 * b + 6] for b in range(2)]
        mv = [small[:, 16 + 4 * b:18 + 4 * b] for b in range(2)]
        rstd = [small[:, 24 + b:25 + b] for b in range(2)]
        xnT, zer, ohl, ohh = self.xnT, self.zer, self.ohl, self.ohh
        turn, hbank, hist = self.bank[0:2], self.bank[2:4], self.bank[4]

        with nc.Block() as block:
            @block.sync
            def _(sp):
                def load(n, slot, r):
                    if not isinstance(n, int) or n >= RX:
                        sp.wait_ge(s["xn"], n - (RX - 1))
                    move_rows(sp, xb[slot], self.tile_rows(t["x"], n), x_in[slot])

                def store(n, slot, r):
                    sp.wait_ge(s["xn"], n + 1)
                    move_rows(sp, self.tile_rows(self.d_xn, n), xn[slot % 2], xn_st[slot % 2])

                def store_turned(n, slot, r):
                    sp.wait_ge(s["xnT"], n + 1)
                    sp.dma_start(self.d_xnT[ds(n, 1), :, :].rearrange("a p f -> (a p) f"),
                                 xnT[slot % 2].rearrange("p k n -> p (k n)")).then_inc(xT_st[slot % 2], 16)

                self.pipeline(sp, [(0, load), (RX - 1, store), (RX, store_turned)], NT, RX)
                for par in range(2):
                    sp.wait_ge(xn_st[par], 32 * (NT // 2))
                    sp.wait_ge(xT_st[par], 16 * (NT // 2))

            @block.vector
            def _(dve):
                nc.vector.memset(zer, 0.0).then_inc(s["zeroed"], 1)
                dve.sem_inc(s["hist"], 2)

                def stats(n, slot, r):
                    par = slot % 2
                    dve.wait_ge(x_in[slot], r * 32 + 32)
                    nc.vector.bn_stats(st[par], xb[slot]).then_inc(s["stats"], 1)
                    dve.wait_ge(s["hist"], n + 1)
                    nc.vector.tensor_tensor(ohl[par], spread(self.lo[:, ds(n * EPT, EPT)], 1, P), self.lo_is,
                                            ALU.is_equal).then_inc(s["hot"], 1)
                    dve.wait_ge(s["stats"], n + 1)
                    nc.vector.tensor_tensor(ohh[par], spread(self.hi[:, ds(n * EPT, EPT)], 1, NT), self.hi_is,
                                            ALU.is_equal).then_inc(s["hot"], 1)
                    nc.vector.bn_aggr(mv[par], st[par]).then_inc(s["var"], 1)

                def norm(n, slot, r):
                    par = slot % 2
                    dve.wait_ge(s["rstd"], n + 1)
                    if not isinstance(n, int) or n > 1:
                        dve.wait_ge(s["xn_turned"], n - 1)
                        dve.wait_ge(xn_st[par], (r * 2 + slot // 2) * 32)
                    nc.vector.tensor_scalar(xn[par], xb[slot], mv[par][:, 0:1], rstd[par], ALU.subtract,
                                            ALU.mult).then_inc(s["xn"], 1)

                self.pipeline(dve, [(0, stats), (1, norm)], NT, RX)
                dve.wait_ge(s["hist"], NT + 2)
                nc.vector.tensor_scalar(self.dinv[:, :], hist[0:P, 0:NT], 1.0, None, ALU.add).then_inc(s["counted"], 1)
                dve.wait_ge(s["counted"], 1)

            @block.tensor
            def _(pe):
                pe.wait_ge(s["zeroed"], 1)
                nc.tensor.matmul(hist[0:P, 0:NT], zer[:, 0:P], zer[:, 0:NT], start=True, stop=False, skip_group_check=True)

                def turned(n, par, r):
                    pe.wait_ge(s["xn"], n + 1)
                    for k in range(2):
                        mm = nc.tensor.transpose(turn[par][:, k * P:(k + 1) * P], xn[par][:, k * 128:(k + 1) * 128],
                                                 self.ident[0:P, 0:P])
                    mm.then_inc(s["xn_turned"], 1)

                def counts(n, par, r):
                    pe.wait_ge(s["hot"], n * 2 + 2)
                    for e in range(EPT):
                        mm = nc.tensor.matmul(hist[0:P, 0:NT], ohl[par][:, :, e], ohh[par][:, :, e], start=False,
                                              stop=False, skip_group_check=True)
                    mm.then_inc(s["hist"], 1)

                def h1(n, par, r):
                    pe.wait_ge(s["xnT"], n + 1)
                    for k in range(2):
                        mm = nc.tensor.matmul(hbank[par][0:P, 0:F], xnT[par][:, k, :], self.gW1[:, k, :],
                                              start=(k == 0), stop=(k == 1))
                    mm.then_inc(s["h"], 1)

                self.pipeline(pe, [(0, counts), (1, turned), (2, h1)], NT)

            @block.scalar
            def _(act):
                nc.scalar.preload_act_table_set("natural_log_exp_and_others")

                def inverse(n, par, r):
                    act.wait_ge(s["var"], n + 1)
                    self.inverse_std(act, rstd[par], mv[par][:, 1:2], s["ln"], n + 1, s["rstd"])

                def keep_turned(n, par, r):
                    act.wait_ge(s["xn_turned"], n + 1)
                    if not isinstance(n, int) or n > 1:
                        act.wait_ge(xT_st[par], r * 16)
                        act.wait_ge(s["h"], n - 1)
                    nc.scalar.activation(xnT[par], turn[par][:, 0:2 * P].rearrange("p (k n) -> p k n", k=2),
                                         ACT.Copy).then_inc(s["xnT"], 1)

                def keep_h1(n, par, r):
                    act.wait_ge(s["h"], n + 1)
                    nc.scalar.activation(self.nodes1[0:P, ds(n * F, F)], hbank[par][0:P, 0:F], ACT.Copy).then_inc(s["h1"], 1)

                self.pipeline(act, [(0, inverse), (1, keep_turned), (2, keep_h1)], NT)
                act.wait_ge(s["h1"], NT)

    def scale_nodes(self):
        nc, NT, F = self.nc, self.NT, self.F
        dinv_made, cleared, scaled, stored = self.sem("dinv_made"), self.sem("aggT_cleared"), self.sem("g1_scaled"), self.sem("g1_stored")
        CH = 10
        W = NT // CH
        g1 = self.nodes1[0:P, :].rearrange("p (n f) -> p n f", f=F)
        table = self.t_g1.rearrange("(n p) f -> p n f", p=P)

        def scale(eng, c):
            w = slice(c * W, (c + 1) * W)
            eng.tensor_tensor(g1[:, w, :], g1[:, w, :], spread(self.dinv[:, w], 2, F),
                              ALU.mult).then_inc(scaled, 1)

        with nc.Block() as block:
            @block.gpsimd
            def _(pool):
                nc.gpsimd.memset(self.aggT[:, :], 0.0).then_inc(cleared, 1)
                pool.wait_ge(cleared, 1)

            @block.scalar
            def _(act):
                nc.scalar.activation(self.dinv[:, :], self.dinv[:, :], ACT.Sqrt).then_inc(dinv_made, 1)

            @block.vector
            def _(dve):
                dve.wait_ge(dinv_made, 1)
                nc.vector.reciprocal(self.dinv[:, :], self.dinv[:, :]).then_inc(dinv_made, 1)
                dve.wait_ge(dinv_made, 2)
                for c in range(CH):
                    scale(nc.vector, c)

            @block.sync
            def _(sp):
                for c in range(CH):
                    w = slice(c * W, (c + 1) * W)
                    sp.wait_ge(scaled, c + 1)
                    for a, b in ((0, ROWS16), (ROWS16, P)):
                        sp.dma_start(table[a:b, w, :], g1[a:b, w, :]).then_inc(stored, 16)
                sp.wait_ge(stored, 32 * CH)

    def aggregate(self, name, table, beside=None):
        nc, NT, EPT = self.nc, self.NT, self.EPT
        SL, WB = self.SLOTS, 2
        idx, onehot, window = self.idx, self.onehot, self.bank[0:WB]
        got = [self.sem(f"{name}_row{k}") for k in range(SL)]
        indexed, hot, summed, added = (self.sem(f"{name}_{k}") for k in ("indexed", "hot", "summed", "added"))

        with self.nc.Block() as block:
            @block.gpsimd
            def _(pool):
                with pool.Fori(0, NT // 2) as i:
                    for par in range(2):
                        n = i * 2 + par
                        pool.wait_ge(summed, n * EPT + EPT)
                        nc.gpsimd.tensor_copy(idx[par][:, :], self.srcT[:, ds(n * EPT, EPT)]).then_inc(indexed, 1)
                        pool.wait_ge(indexed, n * 2 + 1)
                        nc.gpsimd.tensor_tensor(self.held[:, 0:1], self.held[:, 1:2], self.held[:, 1:2],
                                                ALU.add).then_inc(indexed, 1)
                        for e in range(EPT):
                            k = par * EPT + e
                            nc.gpsimd.indirect_dma_start(
                                self.rows[:, k, :], None, table,
                                bass.IndirectOffsetOnAxis(ap=idx[par][:, e:e + 1], axis=0)).then_inc(got[k], 16)

            @block.tensor
            def _(pe):
                if beside:
                    beside.pe_start(pe)
                with pe.Fori(0, NT // 2) as i:
                    for par in range(2):
                        n = i * 2 + par
                        pe.wait_ge(hot, n + 1)
                        for e in range(EPT):
                            k = par * EPT + e
                            pe.wait_ge(got[k], (i + 1) * 16)
                            pe.wait_ge(added, n * EPT + (e + 1))
                            nc.tensor.matmul(window[k % WB][:, 0:P], self.rows[:, k, :], onehot[par][:, e, :],
                                             start=True, stop=True).then_inc(summed, 1)
                            if beside:
                                beside.pe(pe, n, par, i, e)

            @block.vector
            def _(dve):
                dve.sem_inc(summed, SL)
                dve.sem_inc(added, WB)

                def hots(n, par):
                    nc.vector.tensor_tensor(onehot[par][:, :, :], spread(self.iota[:, 0:P], 1, EPT),
                                            spread(self.dstT[:, ds(n * EPT, EPT)], 2, P),
                                            ALU.is_equal).then_inc(hot, 1)

                def group(n, par, r, more):
                    _, starts = nc.values_load_multi_w_load_instructions(
                        self.winstart[0:1, ds(n * self.DPAD, self.DPAD)], engines=DVE_ONLY, min_val=0, max_val=self.N,
                        skip_runtime_bounds_check_because="clamped to [0, N] when made")
                    if more:
                        dve.wait_ge(summed, n * EPT + SL)
                        hots(n + 1, 1 - par)
                    for e in range(EPT):
                        k = par * EPT + e
                        dve.wait_ge(summed, n * EPT + (e + 1 + SL))
                        dve.wait_ge(added, n * EPT + (e + WB))
                        at = self.aggT[:, ds(starts[e], P)]
                        nc.vector.tensor_tensor(at, at, window[k % WB][:, 0:P], ALU.add).then_inc(added, 1)
                        if beside:
                            beside.dve(dve, n, par, r, e)

                if beside:
                    beside.dve_start(dve)
                hots(0, 0)
                with dve.Fori(0, NT // 2 - 1) as i:
                    group(i * 2, 0, i, True)
                    group(i * 2 + 1, 1, i, True)
                group(NT - 2, 0, NT // 2 - 1, True)
                group(NT - 1, 1, NT // 2 - 1, False)
                dve.wait_ge(added, self.ET + WB)
                if beside:
                    beside.dve_end(dve)

            if beside:
                @block.sync
                def _(sp):
                    beside.sync(sp)

                @block.scalar
                def _(act):
                    beside.scalar(act)

    def load_experts(self, sp):
        t, NE, H, C = self.t, self.NE, self.H, self.C
        W = self.W1e.rearrange("p (e w) -> p e w", e=NE)
        sp.dma_start(W[:, :, 0:2 * H], t["ffn_W1"].rearrange("p e k h -> p e (k h)")).then_inc(self.W1_in, 16)
        sp.dma_start(W[:, :, 2 * H:self.WE], t["ffn_b1"]).then_inc(self.W1_in, 16)
        sp.dma_start(self.b2e, t["ffn_b2"].rearrange("(a e) c -> a (e c)", a=1)).then_inc(self.W1_in, 16)

    def zero_slots(self, sp):
        self.zero_dmas = 4
        w = self.ST // self.zero_dmas
        rows = self.d_xs.rearrange("(j p) c -> p j c", p=P)
        sp.wait_ge(self.zeros_made, 1)
        for z in range(self.zero_dmas):
            sp.dma_start(rows[:, z * w:(z + 1) * w, :],
                         spread(self.zeros[0:P, :], 1, w)).then_inc(self.slots_zeroed, 16)

    def between(self):
        nc, NT, F = self.nc, self.NT, self.F
        G = 4
        joined, biased, ready, turned, kept, brought = (self.sem("p3_" + k) for k in (
            "joined", "biased", "ready", "turned", "kept", "brought"))
        stored = [self.sem(f"p3_stored{b}") for b in range(2)]
        chain = self.sem("p3_chain")
        flat = self.rows_flat[0:P, :]
        a1 = [flat[:, b * G * F:(b + 1) * G * F].rearrange("p (g f) -> p g f", g=G) for b in range(2)]
        g2 = [flat[:, (2 + b) * G * F:(3 + b) * G * F].rearrange("p (g f) -> p g f", g=G) for b in range(2)]
        take = self.carve(self.work)
        agg = [take(G * P) for _ in range(2)]
        table = self.t_g2.rearrange("(n p) f -> p n f", p=P)
        NG = NT // G
        sums, turns = self.bank[0:2], self.bank[2:4]

        def over(eng, A, B):
            A(0, 0, 0)
            with eng.Fori(0, (NG - 1) // 2) as i:
                A(i * 2 + 1, 1, i)
                B(i * 2, 0, i)
                A(i * 2 + 2, 0, i + 1)
                B(i * 2 + 1, 1, i)
            B(NG - 1, 0, (NG - 1) // 2)

        with nc.Block() as block:
            @block.tensor
            def _(pe):
                def A(g, par, r):
                    pe.wait_ge(biased, g + 1)
                    pe.wait_ge(brought, g + 1)
                    for k in range(G):
                        nc.tensor.matmul(sums[par][0:P, k * F:(k + 1) * F], agg[par][:, k * P:(k + 1) * P],
                                         self.ident[:, :], start=True, stop=False, skip_group_check=True)
                        mm = nc.tensor.matmul(sums[par][0:P, k * F:(k + 1) * F], self.ident[0:P, 0:P],
                                              self.nodes1[0:P, ds((g * G + k) * F, F)], start=False, stop=True,
                                              skip_group_check=True)
                    mm.then_inc(joined, 1)

                def B(g, par, r):
                    pe.wait_ge(ready, g + 1)
                    pe.wait_ge(kept, g + 1)
                    for k in range(G):
                        mm = nc.tensor.transpose(turns[par][:, k * P:(k + 1) * P], g2[par][:, k, :], self.ident[0:P, 0:P])
                    mm.then_inc(turned, 1)
                over(pe, A, B)

            @block.vector
            def _(dve):
                dve.sem_inc(biased, 2)
                dve.sem_inc(kept, 2)

                def group(g, par, r, first):
                    d = spread(self.dinv[:, ds(g * G, G)], 2, F)
                    dve.wait_ge(joined, g + 1)
                    nc.vector.tensor_tensor(a1[par], sums[par][0:P, 0:G * F].rearrange("p (g f) -> p g f", g=G), d,
                                            ALU.mult).then_inc(biased, 1)
                    dve.wait_ge(biased, g + 3)
                    nc.vector.tensor_tensor(a1[par], a1[par], spread(self.gb1[:, :], 1, G),
                                            ALU.add).then_inc(chain, 1)
                    dve.wait_ge(chain, g + 1)
                    if not first:
                        dve.wait_ge(stored[par], r * 32)
                        dve.wait_ge(turned, g - 1)
                    nc.vector.scalar_tensor_tensor(out=g2[par], in0=a1[par], scalar=0.0, in1=d, op0=ALU.max,
                                                   op1=ALU.mult).then_inc(ready, 1)
                group(0, 0, 0, True)
                group(1, 1, 0, True)
                with dve.Fori(1, (NG - 1) // 2) as i:
                    group(i * 2, 0, i, False)
                    group(i * 2 + 1, 1, i, False)
                group(NG - 1, 0, (NG - 1) // 2, False)

            @block.scalar
            def _(act):
                def bring(g, par, r):
                    if not isinstance(g, int) or g > 1:
                        act.wait_ge(joined, g - 1)
                    nc.scalar.activation(agg[par], self.aggT[:, ds(g * (G * P), G * P)], ACT.Copy).then_inc(brought, 1)

                def keep(g, par, r):
                    act.wait_ge(turned, g + 1)
                    act.wait_ge(brought, g + 1)
                    nc.scalar.activation(self.aggT[:, ds(g * (G * P), G * P)], turns[par][:, 0:G * P],
                                         ACT.Copy).then_inc(kept, 1)
                self.pipeline(act, [(0, bring), (2, keep)], NG)
                act.wait_ge(kept, NG + 2)

            @block.sync
            def _(sp):
                def store(g, par):
                    sp.wait_ge(ready, g + 1)
                    for a, b in ((0, ROWS16), (ROWS16, P)):
                        sp.dma_start(table[a:b, ds(g * G, G), :], g2[par][a:b, :, :]).then_inc(stored[par], 16)
                with sp.Fori(0, (NG - 1) // 2) as i:
                    for par in range(2):
                        store(i * 2 + par, par)
                store(NG - 1, 0)
                sp.wait_ge(stored[0], 32 * ((NG + 1) // 2))
                sp.wait_ge(stored[1], 32 * (NG // 2))


    def gate(self):
        nc, NT, C, NE = self.nc, self.NT, self.C, self.NE
        s = {k: self.sem("p5_" + k) for k in (
            "brought", "gnn", "x2", "stats", "var", "ln", "rstd", "xm", "xm_turned", "xmT", "score", "scored")}
        RX = 4
        x_in = [self.sem(f"p5_x_in{b}") for b in range(RX)]
        x2_st, xm_st = ([self.sem(f"p5_{k}{b}") for b in range(2)] for k in ("x2_stored", "xm_stored"))
        take = self.carve(self.work)
        xb, x2, xm = ([take(C)[0:P] for _ in range(k)] for k in (RX, 2, 2))
        agg = [take(P) for _ in range(2)]
        xmT = [take(2 * P).rearrange("p (k n) -> p k n", k=2) for _ in range(2)]
        small = take(40)[0:P]
        st = [small[:, 8 * b:8 * b + 6] for b in range(2)]
        mv = [small[:, 16 + 4 * b:18 + 4 * b] for b in range(2)]
        rstd = [small[:, 24 + b:25 + b] for b in range(2)]
        scratch = small[0:1, 26:27]
        gbank, turn, sbank = self.bank[0:2], self.bank[2:4], self.bank[4:6]

        with nc.Block() as block:
            @block.sync
            def _(sp):
                def load(n, slot, r):
                    if not isinstance(n, int) or n >= RX:
                        sp.wait_ge(s["x2"], n - (RX - 1))
                    move_rows(sp, xb[slot], self.tile_rows(self.d_xmix, n), x_in[slot])

                def store(n, slot, r):
                    sp.wait_ge(s["x2"], n + 1)
                    move_rows(sp, self.tile_rows(self.d_x2, n), x2[slot % 2], x2_st[slot % 2])
                    sp.wait_ge(s["xm"], n + 1)
                    move_rows(sp, self.tile_rows(self.d_xm, n), xm[slot % 2], xm_st[slot % 2])

                self.pipeline(sp, [(0, load), (RX - 1, store)], NT, RX)
                for par in range(2):
                    sp.wait_ge(x2_st[par], 32 * (NT // 2))
                    sp.wait_ge(xm_st[par], 32 * (NT // 2))

            @block.scalar
            def _(act):
                nc.scalar.preload_act_table_set("natural_log_exp_and_others")

                def bring(n, par, r):
                    if not isinstance(n, int) or n > 1:
                        act.wait_ge(s["gnn"], n - 1)
                    nc.scalar.activation(agg[par], self.aggT[:, ds(n * P, P)], ACT.Copy).then_inc(s["brought"], 1)

                def inverse(n, par, r):
                    act.wait_ge(s["var"], n + 1)
                    self.inverse_std(act, rstd[par], mv[par][:, 1:2], s["ln"], n + 1, s["rstd"])

                def keep_turned(n, par, r):
                    act.wait_ge(s["xm_turned"], n + 1)
                    if not isinstance(n, int) or n > 1:
                        act.wait_ge(s["score"], n - 1)
                    nc.scalar.activation(xmT[par], turn[par][:, 0:2 * P].rearrange("p (k n) -> p k n", k=2),
                                         ACT.Copy).then_inc(s["xmT"], 1)
                self.pipeline(act, [(0, bring), (1, inverse), (3, keep_turned)], NT)

            @block.tensor
            def _(pe):
                def gnn(n, par, r):
                    pe.wait_ge(s["brought"], n + 1)
                    if not isinstance(n, int) or n > 1:
                        pe.wait_ge(s["x2"], n - 1)
                    nc.tensor.matmul(gbank[par][0:P, 0:C], agg[par], self.gW2[:, :], start=True,
                                     stop=True).then_inc(s["gnn"], 1)

                def turned(n, par, r):
                    pe.wait_ge(s["xm"], n + 1)
                    for k in range(2):
                        mm = nc.tensor.transpose(turn[par][:, k * P:(k + 1) * P], xm[par][:, k * 128:(k + 1) * 128],
                                                 self.ident[0:P, 0:P])
                    mm.then_inc(s["xm_turned"], 1)

                def score(n, par, r):
                    pe.wait_ge(s["xmT"], n + 1)
                    if not isinstance(n, int) or n > 1:
                        pe.wait_ge(s["scored"], n - 1)
                    for k in range(2):
                        mm = nc.tensor.matmul(sbank[par][0:P, 0:NE], xmT[par][:, k, :], self.Wg[:, k, :],
                                              start=(k == 0), stop=(k == 1))
                    mm.then_inc(s["score"], 1)
                self.pipeline(pe, [(0, gnn), (2, turned), (3, score)], NT)

            @block.vector
            def _(dve):
                def x2_stats(n, slot, r):
                    par = slot % 2
                    dve.wait_ge(x_in[slot], r * 32 + 32)
                    if not isinstance(n, int) or n > 1:
                        dve.wait_ge(x2_st[par], (r * 2 + slot // 2) * 32)
                        dve.wait_ge(s["xm"], n - 1)
                    dve.wait_ge(s["gnn"], n + 1)
                    nc.vector.scalar_tensor_tensor(out=x2[par], in0=gbank[par][0:P, 0:C], scalar=self.dinv[:, ds(n, 1)],
                                                   in1=xb[slot], op0=ALU.mult, op1=ALU.add).then_inc(s["x2"], 1)
                    dve.wait_ge(s["x2"], n + 1)
                    nc.vector.bn_stats(st[par], x2[par]).then_inc(s["stats"], 1)
                    dve.wait_ge(s["stats"], n + 1)
                    nc.vector.memset(scratch, 0.0)
                    nc.vector.bn_aggr(mv[par], st[par]).then_inc(s["var"], 1)

                def norm(n, slot, r):
                    par = slot % 2
                    dve.wait_ge(s["rstd"], n + 1)
                    if not isinstance(n, int) or n > 1:
                        dve.wait_ge(s["xm_turned"], n - 1)
                        dve.wait_ge(xm_st[par], (r * 2 + slot // 2) * 32)
                    nc.vector.tensor_scalar(xm[par], x2[par], mv[par][:, 0:1], rstd[par], ALU.subtract,
                                            ALU.mult).then_inc(s["xm"], 1)

                def scored(n, slot, r):
                    dve.wait_ge(s["score"], n + 1)
                    nc.vector.tensor_tensor(self.gates[:, ds(n * NE, NE)], sbank[slot % 2][0:P, 0:NE], self.bg[:, :],
                                            ALU.add).then_inc(s["scored"], 1)
                self.pipeline(dve, [(0, x2_stats), (1, norm), (3, scored)], NT, RX)
                dve.wait_ge(s["scored"], NT)

    def route(self):
        nc, NT, NE, ST = self.nc, self.NT, self.NE, self.ST
        chain, made, counted, W2_in = (self.sem("p6_" + k) for k in ("chain", "made", "counted", "W2_in"))
        take = self.carve(self.rows_flat[0:P, :])
        grid = lambda flat: flat.rearrange("p (n e) -> p n e", e=NE)
        take(NT * NE)
        gates = grid(self.gates)
        first, second, upto, tmp = (grid(take(NT * NE)) for _ in range(4))
        best, ones8 = take(NT), take(NT)
        more = self.carve(self.work)
        mark = grid(more(NT * NE)[0:P])
        fits = more(NE * NT)[0:P].rearrange("p (e j) -> p e j", e=NE)
        past = more(ST * NE)[0:1]
        tile_no, tiles125 = more(ST)[0:1], more(NT)[0:P]
        rank8, per, total, ntile, upto8, base, own = (more(NE)[0:P] for _ in range(7))
        low, eidf = more(128), more(ST)[0:1]
        sums = self.bank[0]

        with nc.Block() as block:
            @block.sync
            def _(sp):
                sp.dma_start(self.W2e, self.t["ffn_W2"].rearrange("p e c d -> p (e c d)")).then_inc(W2_in, 16)
                sp.wait_ge(W2_in, 16)

            @block.gpsimd
            def _(pool):
                nc.gpsimd.affine_select(out=low, in_=self.ones[:, :], compare_op=ALU.is_gt, fill=0.0, base=0,
                                        pattern=[[1, 128]], channel_multiplier=-1).then_inc(made, 1)
                nc.gpsimd.iota(tile_no, pattern=[[1, ST]], base=0, channel_multiplier=0,
                               allow_small_or_imprecise_dtypes=True).then_inc(made, 1)
                nc.gpsimd.iota(tiles125, pattern=[[P, NT]], base=0, channel_multiplier=0,
                               allow_small_or_imprecise_dtypes=True).then_inc(made, 1)
                pool.wait_ge(made, 3)

            @block.tensor
            def _(pe):
                pe.wait_ge(made, 3)
                pe.wait_ge(counted, 1)
                nc.tensor.matmul(sums[0:P, 0:NE], low[0:P, 0:P], per, start=True, stop=True)
                nc.tensor.matmul(sums[0:P, NE:2 * NE], self.ones[0:P, 0:P], per, start=True, stop=True).then_inc(counted, 1)

            @block.vector
            def _(dve):
                c = Steps(dve, chain, 0, None)
                v = nc.vector

                def step(ins):
                    c.did(ins)
                    c.settle()
                step(v.tensor_scalar(rank8, self.iota[:, 0:NE], -1.0, float(NE), ALU.mult, ALU.add))
                step(v.memset(ones8, 1.0))

                def pick(scores, chosen):
                    step(v.tensor_reduce(best, scores, AX.X, ALU.max))
                    step(v.tensor_tensor(tmp, scores, spread(best, 2, NE), ALU.is_equal))
                    step(v.tensor_tensor(mark, tmp, spread(rank8, 1, NT), ALU.mult))
                    step(v.tensor_reduce(best, mark, AX.X, ALU.max))
                    step(v.tensor_tensor(chosen, mark, spread(best, 2, NE), ALU.is_equal))
                pick(gates, first)
                step(v.scalar_tensor_tensor(out=gates, in0=first, scalar=-3.0e38, in1=gates, op0=ALU.mult, op1=ALU.add))
                pick(gates, second)
                step(v.tensor_tensor(mark, first, second, ALU.add))
                for e in range(NE):
                    c.did(v.tensor_tensor_scan(out=upto[:, :, e], data0=ones8, data1=mark[:, :, e], initial=0.0,
                                               op0=ALU.mult, op1=ALU.add))
                c.settle()
                v.tensor_copy(per, upto[:, NT - 1, :]).then_inc(counted, 1)
                dve.wait_ge(counted, 2)
                step(v.tensor_copy(total, sums[0:P, NE:2 * NE]))
                step(v.tensor_copy(own, sums[0:P, 0:NE]))
                dve.wait_ge(made, 3)
                step(v.tensor_tensor(fits, spread(total, 2, NT), spread(tiles125, 1, NE), ALU.is_gt))
                step(v.tensor_reduce(ntile, fits, AX.X, ALU.add))
                step(v.tensor_tensor_scan(out=upto8, data0=ones8[:, 0:NE], data1=ntile, initial=0.0, op0=ALU.mult,
                                          op1=ALU.add))
                step(v.tensor_tensor(base, upto8, ntile, ALU.subtract))
                step(v.tensor_scalar(base, base, float(P), -1.0, ALU.mult, ALU.add))
                step(v.tensor_tensor(base, base, own, ALU.add))
                step(v.tensor_tensor(upto, upto, spread(base, 1, NT), ALU.add))
                for k, chosen in enumerate((first, second)):
                    step(v.tensor_tensor(tmp, upto, chosen, ALU.mult))
                    step(v.tensor_reduce(best, tmp, AX.X, ALU.add))
                    step(v.tensor_copy(self.slots[:, k, :], best))
                pastv = past.rearrange("a (j e) -> a j e", e=NE)
                step(v.tensor_tensor(pastv, spread(tile_no, 2, NE), spread(upto8[0:1, :], 1, ST), ALU.is_ge))
                step(v.tensor_reduce(eidf, pastv, AX.X, ALU.add))
                step(v.memset(self.eid[:, :], 0))
                step(v.tensor_scalar(self.eid[0:1, :].rearrange("a (j k) -> a j k", k=4)[:, :, 0:2],
                                     eidf.rearrange("a (j k) -> a j k", k=2), float(NE - 1), None, ALU.min))

    def scatter(self):
        nc, NT, C = self.nc, self.NT, self.C
        RX = 4
        x_in, sent = ([self.sem(f"p7_{k}{b}") for b in range(RX)] for k in ("x_in", "sent"))
        indexed = self.sem("p7_indexed")
        take = self.carve(self.work)
        xm = [take(C)[0:P] for _ in range(RX)]
        idx = [take(2)[0:P].bitcast(I32) for _ in range(RX)]

        with nc.Block() as block:
            @block.sync
            def _(sp):
                def load(n, slot, r):
                    if not isinstance(n, int) or n >= RX:
                        sp.wait_ge(sent[slot], r * 32)
                    move_rows(sp, xm[slot], self.tile_rows(self.d_xm, n), x_in[slot])
                self.pipeline(sp, [(0, load)], NT, RX)

            @block.gpsimd
            def _(pool):
                def send(n, slot, r):
                    pool.wait_ge(x_in[slot], r * 32 + 32)
                    nc.gpsimd.tensor_copy(idx[slot], self.slots[:, :, ds(n, 1)].rearrange("p k n -> p (k n)"))\
                        .then_inc(indexed, 1)
                    pool.wait_ge(indexed, n * 2 + 1)
                    nc.gpsimd.tensor_tensor(self.held[:, 0:1], self.held[:, 1:2], self.held[:, 1:2],
                                            ALU.add).then_inc(indexed, 1)
                    for k in range(2):
                        nc.gpsimd.indirect_dma_start(self.d_xs, bass.IndirectOffsetOnAxis(ap=idx[slot][:, k:k + 1], axis=0),
                                                     xm[slot], None).then_inc(sent[slot], 16)
                self.pipeline(pool, [(0, send)], NT, RX)
                for b in range(RX):
                    pool.wait_ge(sent[b], 32 * (NT // RX))

    def experts(self):
        nc, C, ST, NE, H = self.nc, self.C, self.ST, self.NE, self.H
        HC = H // 128
        s = {k: self.sem("p8_" + k) for k in ("turned", "xT", "W1", "h", "hT", "y", "kept")}
        RX = 4
        x_in = [self.sem(f"p8_x_in{b}") for b in range(RX)]
        y_st = [self.sem(f"p8_y_stored{b}") for b in range(2)]
        take = self.carve(self.work)
        xb, yb = ([take(C)[0:P] for _ in range(k)] for k in (RX, 2))
        xT = [take(2 * P).rearrange("p (k n) -> p k n", k=2) for _ in range(2)]
        hT = [take(HC * P) for _ in range(2)]
        W1s = self.W1s
        turn, hbank, ybank = self.bank[0:2], self.bank[2:4], self.bank[4:6]
        WE = self.WE

        def expert_ids(engines, r):
            return nc.values_load_multi_w_load_instructions(
                self.eid[0:1, ds(r * 4, 4)], engines=engines, min_val=0, max_val=NE - 1,
                skip_runtime_bounds_check_because="a count of experts, held below their number when made")[1]

        with nc.Block() as block:
            @block.sync
            def _(sp):
                def load(n, slot, r):
                    if not isinstance(n, int) or n >= RX:
                        sp.wait_ge(s["turned"], n - (RX - 1))
                    move_rows(sp, xb[slot], self.tile_rows(self.d_xs, n), x_in[slot])

                def store(n, slot, r):
                    sp.wait_ge(s["kept"], n + 1)
                    move_rows(sp, self.tile_rows(self.d_ys, n), yb[slot % 2], y_st[slot % 2])
                self.pipeline(sp, [(0, load), (RX - 1, store)], ST, RX)
                for par in range(2):
                    sp.wait_ge(y_st[par], 32 * (ST // 2))

            @block.tensor
            def _(pe):
                def turned(n, slot, r):
                    par = slot % 2
                    pe.wait_ge(x_in[slot], r * 32 + 32)
                    if not isinstance(n, int) or n > 1:
                        pe.wait_ge(s["xT"], n - 1)
                    for k in range(2):
                        mm = nc.tensor.transpose(turn[par][:, k * P:(k + 1) * P], xb[slot][:, k * 128:(k + 1) * 128],
                                                 self.ident[0:P, 0:P])
                    mm.then_inc(s["turned"], 1)

                def hidden(n, slot, r):
                    par = slot % 2
                    pe.wait_ge(s["xT"], n + 1)
                    pe.wait_ge(s["W1"], n + 1)
                    if not isinstance(n, int) or n > 1:
                        pe.wait_ge(s["hT"], (n - 1) * HC)
                    for c in range(HC):
                        for k in range(2):
                            mm = nc.tensor.matmul(hbank[par][:, c * P:(c + 1) * P],
                                                  W1s[par][:, k * H + c * 128:k * H + (c + 1) * 128], xT[par][:, k, :],
                                                  start=(k == 0), stop=(k == 1))
                    mm.then_inc(s["h"], 1)

                def output(n, slot, r):
                    par = slot % 2
                    if par == 0:
                        self.ids = expert_ids(PE_ONLY, r * (RX // 2) + slot // 2)
                    e = self.ids[par]
                    pe.wait_ge(s["hT"], (n + 1) * HC)
                    if not isinstance(n, int) or n > 1:
                        pe.wait_ge(s["kept"], n - 1)
                    out = ybank[par][0:P, 0:C]
                    for c in range(HC):
                        nc.tensor.matmul(out, hT[par][:, c * P:(c + 1) * P], self.W2e[:, ds(e * (HC * C) + c * C, C)],
                                         start=(c == 0), stop=False)
                    nc.tensor.matmul(out, self.ones[0:1, 0:P], self.b2e[0:1, ds(e * C, C)], start=False,
                                     stop=True).then_inc(s["y"], 1)
                self.pipeline(pe, [(0, turned), (1, hidden), (2, output)], ST, RX)

            @block.scalar
            def _(act):
                def keep_turned(n, par, r):
                    act.wait_ge(s["turned"], n + 1)
                    if not isinstance(n, int) or n > 1:
                        act.wait_ge(s["h"], n - 1)
                    nc.scalar.activation(xT[par], turn[par][:, 0:2 * P].rearrange("p (k n) -> p k n", k=2),
                                         ACT.Copy).then_inc(s["xT"], 1)

                def gelu(n, par, r):
                    act.wait_ge(s["h"], n + 1)
                    if not isinstance(n, int) or n > 1:
                        act.wait_ge(s["y"], n - 1)
                    for c in range(HC):
                        nc.scalar.activation(hT[par][:, c * P:(c + 1) * P], hbank[par][:, c * P:(c + 1) * P], ACT.Gelu,
                                             bias=W1s[par][:, 2 * H + c:2 * H + c + 1]).then_inc(s["hT"], 1)
                nc.scalar.preload_act_table(ACT.Gelu)
                self.pipeline(act, [(0, keep_turned), (1, gelu)], ST)

            @block.vector
            def _(dve):
                def weights(n, par, r):
                    if par == 0:
                        self.ids = expert_ids(DVE_ONLY, r)
                    if not isinstance(n, int) or n > 1:
                        dve.wait_ge(s["h"], n - 1)
                        dve.wait_ge(s["hT"], (n - 1) * HC)
                    nc.vector.tensor_copy(W1s[par], self.W1e[:, ds(self.ids[par] * WE, WE)]).then_inc(s["W1"], 1)

                def keep(n, par, r):
                    dve.wait_ge(s["y"], n + 1)
                    if not isinstance(n, int) or n > 1:
                        dve.wait_ge(y_st[par], r * 32)
                    nc.vector.tensor_copy(yb[par], ybank[par][0:P, 0:C]).then_inc(s["kept"], 1)
                self.pipeline(dve, [(0, weights), (2, keep)], ST)

    def combine(self, out):
        nc, NT, C = self.nc, self.NT, self.C
        RX = 4
        x_in, got, out_st = ([self.sem(f"p9_{k}{b}") for b in range(RX)] for k in ("x_in", "got", "stored"))
        indexed, summed, done = (self.sem("p9_" + k) for k in ("indexed", "summed", "done"))
        take = self.carve(self.work)
        x2, ya = ([take(C)[0:P] for _ in range(RX)] for _ in range(2))
        yb = [take(C)[0:P] for _ in range(RX)]
        idx = [take(2)[0:P].bitcast(I32) for _ in range(RX)]

        with nc.Block() as block:
            @block.sync
            def _(sp):
                def load(n, slot, r):
                    if not isinstance(n, int) or n >= RX:
                        sp.wait_ge(out_st[slot], r * 32)
                    move_rows(sp, x2[slot], self.tile_rows(self.d_x2, n), x_in[slot])

                def store(n, slot, r):
                    sp.wait_ge(done, n + 1)
                    move_rows(sp, self.tile_rows(out, n), x2[slot], out_st[slot])
                self.pipeline(sp, [(0, load), (2, store)], NT, RX)
                for b in range(RX):
                    sp.wait_ge(out_st[b], 32 * (NT // RX))

            @block.gpsimd
            def _(pool):
                def fetch(n, slot, r):
                    if not isinstance(n, int) or n >= RX:
                        pool.wait_ge(done, n - (RX - 1))
                    nc.gpsimd.tensor_copy(idx[slot], self.slots[:, :, ds(n, 1)].rearrange("p k n -> p (k n)"))\
                        .then_inc(indexed, 1)
                    pool.wait_ge(indexed, n * 2 + 1)
                    nc.gpsimd.tensor_tensor(self.held[:, 0:1], self.held[:, 1:2], self.held[:, 1:2],
                                            ALU.add).then_inc(indexed, 1)
                    for k, y in enumerate((ya, yb)):
                        nc.gpsimd.indirect_dma_start(y[slot], None, self.d_ys,
                                                     bass.IndirectOffsetOnAxis(ap=idx[slot][:, k:k + 1], axis=0))\
                            .then_inc(got[slot], 16)
                self.pipeline(pool, [(0, fetch)], NT, RX)

            @block.vector
            def _(dve):
                def add(n, slot, r):
                    dve.wait_ge(got[slot], r * 32 + 32)
                    nc.vector.tensor_tensor(ya[slot], ya[slot], yb[slot], ALU.add).then_inc(summed, 1)
                    dve.wait_ge(x_in[slot], r * 32 + 32)
                    dve.wait_ge(summed, n + 1)
                    nc.vector.tensor_tensor(x2[slot], x2[slot], ya[slot], ALU.add).then_inc(done, 1)
                self.pipeline(dve, [(0, add)], NT, RX)


class KeyValueSums:

    def __init__(self, k):
        self.k = k
        self.s = {n: k.sem("kv_" + n) for n in ("k", "v", "kmin", "kexp", "kf", "v_kept", "summed", "ready", "kept")}
        self.ins = [k.sem(f"kv_in{b}") for b in range(2)]
        take = k.carve(k.work)
        self.xnT = [take(2 * P).rearrange("p (a n) -> p a n", a=2) for _ in range(2)]
        self.kmin, self.kf = take(k.C)[0:P], take(k.C)[0:P]
        self.v = take(2 * 129)[0:P].rearrange("p (a m) -> p a m", a=2)
        self.zero = take(260)
        self.kb, self.vb, self.acc = k.bank[2:5]

    def sync(self, sp):
        k = self.k

        def load(n, par):
            sp.dma_start(self.xnT[par].rearrange("p a n -> p (a n)"),
                         k.d_xnT[ds(n, 1), :, :].rearrange("a p f -> (a p) f")).then_inc(self.ins[par], 16)
        load(0, 0)
        load(1, 1)
        k.zero_slots(sp)
        with sp.Fori(0, k.NT // 2 - 1) as i:
            for par in range(2):
                sp.wait_ge(self.s["v"], i * 2 + (par + 1))
                load(i * 2 + (par + 2), par)
        sp.wait_ge(k.slots_zeroed, 16 * k.zero_dmas)

    def pe_start(self, pe):
        pe.wait_ge(self.s["ready"], 2)
        self.k.nc.tensor.matmul(self.acc[:, 0:258], self.zero[:, 0:128], self.zero[:, 0:258], start=True, stop=False,
                                skip_group_check=True)

    def pe(self, pe, n, par, r, e):
        k, s, mm = self.k, self.s, self.k.nc.tensor.matmul
        if e == 1:
            pe.wait_ge(self.ins[par], r * 16 + 16)
            for w0, out, name in ((k.C, self.kb, "k"), (2 * k.C, self.vb, "v")):
                for c in range(2):
                    last = mm(out[0:P, 0:k.C], self.xnT[par][:, c, :], k.Wqkv[:, c, w0:w0 + k.C],
                              start=(c == 0), stop=(c == 1))
                last.then_inc(s[name], 1)
        if e == 9:
            pe.wait_ge(s["kf"], n + 1)
            pe.wait_ge(s["v_kept"], n + 1)
            for a in range(2):
                last = mm(self.acc[:, a * 129:(a + 1) * 129], self.kf[:, a * 128:(a + 1) * 128], self.v[:, a, :],
                          start=False, stop=False, skip_group_check=True)
            last.then_inc(s["summed"], 1)

    def scalar(self, act):
        k, s, nc = self.k, self.s, self.k.nc
        nc.scalar.preload_act_table_set("exp_and_others")
        act.wait_ge(s["ready"], 2)

        def tile(n):
            act.wait_ge(s["kmin"], n + 1)
            nc.scalar.activation(self.kmin, self.kmin, ACT.Exp).then_inc(s["kexp"], 1)
            act.wait_ge(s["v"], n + 1)
            if not isinstance(n, int):
                act.wait_ge(s["summed"], n)
            nc.scalar.activation(self.v[:, :, 0:128], self.vb[0:P, 0:k.C].rearrange("p (a m) -> p a m", a=2),
                                 ACT.Copy).then_inc(s["v_kept"], 1)
        tile(0)
        with act.Fori(1, k.NT) as n:
            tile(n)

    def dve(self, dve, n, par, r, e):
        k, s, nc = self.k, self.s, self.k.nc
        if e == 3:
            dve.wait_ge(s["k"], n + 1)
            nc.vector.tensor_scalar(self.kmin, self.kb[0:P, 0:k.C], 0.0, None, ALU.min).then_inc(s["kmin"], 1)
        if e == 6:
            dve.wait_ge(s["kexp"], n + 1)
            nc.vector.scalar_tensor_tensor(out=self.kf, in0=self.kb[0:P, 0:k.C], scalar=0.0, in1=self.kmin,
                                           op0=ALU.max, op1=ALU.add).then_inc(s["kf"], 1)

    def dve_start(self, dve):
        self.k.nc.vector.memset(self.zero, 0.0).then_inc(self.s["ready"], 1)
        self.k.nc.vector.memset(self.v[:, :, 128:129], 1.0).then_inc(self.s["ready"], 1)

    def dve_end(self, dve):
        k, nc = self.k, self.k.nc
        dve.wait_ge(self.s["summed"], k.NT)
        for a in range(2):
            for h in range(4):
                q = slice(32 * h, 32 * h + 32)
                for to, of, w in ((32 * h, a * 129 + 32 * h, 32), (128 + h, a * 129 + 128, 1)):
                    nc.vector.tensor_copy(k.kvbd[q, a, to:to + w], self.acc[q, of:of + w]).then_inc(self.s["kept"], 1)
        dve.wait_ge(self.s["kept"], 16)


class Mixer:

    def __init__(self, k):
        self.k = k
        nc, C = k.nc, k.C
        self.s = {n: k.sem("mix_" + n) for n in (
            "q", "qmin", "qexp", "qf", "t", "var1", "std1", "x1", "x1_turned", "x1T", "h", "hT", "y", "var2", "std2",
            "res", "chain", "ln")}
        self.ins = [k.sem(f"mix_in{b}") for b in range(2)]
        self.stored = [k.sem(f"mix_stored{b}") for b in range(2)]
        take = k.carve(k.work)
        rows = lambda: take(C)[0:P]
        cols = lambda: take(2 * P).rearrange("p (a n) -> p a n", a=2)
        self.x, self.xn = [rows() for _ in range(2)], [rows() for _ in range(2)]
        self.xnT = [cols() for _ in range(2)]
        self.res = [rows() for _ in range(2)]
        self.qm, self.qf, self.x1T, self.hT = cols(), cols(), cols(), cols()
        self.r, self.x1 = rows(), rows()
        small = take(40)[0:P]
        self.den, self.rden = small[:, 0:8].rearrange("p (a h) -> p a h", a=2), small[:, 8:16].rearrange("p (a h) -> p a h", a=2)
        self.st, self.mv, self.std, self.rstd = small[:, 16:22], small[:, 22:24], small[:, 24:25], small[:, 25:26]
        self.scratch = small[0:1, 26:27]
        self.qb, self.tb, self.turnb, self.hb, self.yb = k.bank[2:7]
        self.CH = 13

    def sync(self, sp):
        k = self.k

        def load(n, par):
            move_rows(sp, self.xn[par], k.tile_rows(k.d_xn, n), self.ins[par])
            sp.dma_start(self.xnT[par].rearrange("p a n -> p (a n)"),
                         k.d_xnT[ds(n, 1), :, :].rearrange("a p f -> (a p) f")).then_inc(self.ins[par], 16)
            move_rows(sp, self.x[par], k.tile_rows(k.t["x"], n), self.ins[par])

        def store(n, par):
            sp.wait_ge(self.s["res"], n + 1)
            move_rows(sp, k.tile_rows(k.d_xmix, n), self.res[par], self.stored[par])

        load(0, 0)
        load(1, 1)
        k.load_experts(sp)
        with sp.Fori(0, k.NT // 2 - 1) as i:
            for par in range(2):
                store(i * 2 + par, par)
                load(i * 2 + par + 2, par)
        for par in range(2):
            store(k.NT - 2 + par, par)
            sp.wait_ge(self.stored[par], 32 * (k.NT // 2) + 32)
        sp.wait_ge(k.W1_in, 48)

    def pe_start(self, pe):
        pass

    def dve_start(self, dve):
        for par in range(2):
            dve.sem_inc(self.stored[par], 32)

    def dve_end(self, dve):
        pass

    def pe(self, pe, n, par, r, e):
        k, s, mm = self.k, self.s, self.k.nc.tensor.matmul
        if e == 0:
            pe.wait_ge(self.ins[par], (r + 1) * 80)
            for a in range(2):
                for c in range(2):
                    last = mm(self.qb[:, a * P:(a + 1) * P], k.Wqkv[:, c, a * 128:(a + 1) * 128], self.xnT[par][:, c, :],
                              start=(c == 0), stop=(c == 1))
            last.then_inc(s["q"], 1)
        if e == 3:
            pe.wait_ge(s["qf"], n + 1)
            for a in range(2):
                last = mm(self.tb[0:P, a * 132:(a + 1) * 132], self.qf[:, a, :], k.kvbd[:, a, :], start=True, stop=True)
            last.then_inc(s["t"], 1)
        if e == 8:
            pe.wait_ge(s["x1"], n + 1)
            for a in range(2):
                last = k.nc.tensor.transpose(self.turnb[:, a * P:(a + 1) * P], self.x1[:, a * 128:(a + 1) * 128],
                                             k.ident[0:P, 0:P])
            last.then_inc(s["x1_turned"], 1)
        if e == 10:
            pe.wait_ge(s["x1T"], n + 1)
            for a in range(2):
                for c in range(2):
                    last = mm(self.hb[:, a * P:(a + 1) * P], k.mW1[:, c, a * 128:(a + 1) * 128], self.x1T[:, c, :],
                              start=(c == 0), stop=(c == 1))
            last.then_inc(s["h"], 1)
        if e == 12:
            pe.wait_ge(s["hT"], n * 2 + 2)
            for c in range(2):
                last = mm(self.yb[0:P, 0:k.C], self.hT[:, c, :], k.mW2[:, c, :], start=(c == 0), stop=(c == 1))
            last.then_inc(s["y"], 1)

    def scalar(self, act):
        k, s, nc = self.k, self.s, self.k.nc
        with act.Fori(0, k.NT) as n:
            nc.scalar.preload_act_table_set("natural_log_exp_and_others")
            act.wait_ge(s["qmin"], n + 1)
            nc.scalar.activation(self.qm, self.qm, ACT.Exp).then_inc(s["qexp"], 1)
            act.wait_ge(s["var1"], n + 1)
            k.inverse_std(act, self.rstd, self.mv[:, 1:2], s["ln"], n * 2 + 1, s["std1"])
            act.wait_ge(s["x1_turned"], n + 1)
            nc.scalar.activation(self.x1T, self.turnb[:, 0:2 * P].rearrange("p (a n) -> p a n", a=2),
                                 ACT.Copy).then_inc(s["x1T"], 1)
            act.wait_ge(s["h"], n + 1)
            for a in range(2):
                nc.scalar.activation(self.hT[:, a, :], self.hb[:, a * P:(a + 1) * P], ACT.Gelu,
                                     bias=k.mb1[:, a:a + 1]).then_inc(s["hT"], 1)
            nc.scalar.preload_act_table_set("natural_log_exp_and_others")
            act.wait_ge(s["var2"], n + 1)
            k.inverse_std(act, self.rstd, self.mv[:, 1:2], s["ln"], n * 2 + 2, s["std2"])

    def dve(self, dve, n, par, r, e):
        k, s, nc, C = self.k, self.s, self.k.nc, self.k.C
        if e == 0:
            self.c = Steps(dve, s["chain"], n * self.CH, self.CH)
        c = self.c
        both = lambda b, w: b.rearrange("p (a n) -> p a n", a=2)

        def stats(var):
            c.did(nc.vector.bn_stats(self.st, self.r))
            c.settle()
            nc.vector.memset(self.scratch, 0.0)
            nc.vector.bn_aggr(self.mv, self.st).then_inc(s[var], 1)

        def norm(std, out, g):
            dve.wait_ge(s[std], n + 1)
            c.did(nc.vector.tensor_scalar(self.r, self.r, self.mv[:, 0:1], self.rstd, ALU.subtract, ALU.mult))
            c.settle()
            c.did(nc.vector.tensor_tensor(out, self.r, k.brow[g][:, :], ALU.mult))
            c.settle()

        if e == 1:
            dve.wait_ge(s["q"], n + 1)
            nc.vector.tensor_scalar(self.qm, both(self.qb[:, 0:2 * P], P), 0.0, None, ALU.min).then_inc(s["qmin"], 1)
        if e == 2:
            dve.wait_ge(s["qexp"], n + 1)
            nc.vector.scalar_tensor_tensor(out=self.qf, in0=both(self.qb[:, 0:2 * P], P), scalar=0.0, in1=self.qm,
                                           op0=ALU.max, op1=ALU.add).then_inc(s["qf"], 1)
        if e == 4:
            dve.wait_ge(s["t"], n + 1)
            t = self.tb[0:P, 0:264].rearrange("p (a m) -> p a m", a=2)
            c.did(nc.vector.tensor_scalar(self.den, t[:, :, 128:132], EPS_ATTN, None, ALU.add))
            c.settle()
            c.did(nc.vector.reciprocal(self.rden, self.den))
            c.settle()
            c.did(nc.vector.tensor_tensor(self.r.rearrange("p (a h m) -> p a h m", a=2, h=4),
                                          t[:, :, 0:128].rearrange("p a (h m) -> p a h m", h=4),
                                          spread(self.rden, 3, 32), ALU.mult))
            c.settle()
        if e == 5:
            c.did(nc.vector.tensor_tensor(self.r, self.r, self.xn[par], ALU.add))
            c.settle()
            stats("var1")
        if e == 7:
            norm("std1", self.x1, "ln1_g")
            nc.vector.tensor_tensor(self.x1, self.x1, k.brow["ln1_b"][:, :], ALU.add).then_inc(s["x1"], 1)
        if e == 13:
            dve.wait_ge(s["y"], n + 1)
            dve.wait_ge(s["x1"], n + 1)
            c.did(nc.vector.tensor_tensor(self.r, self.yb[0:P, 0:C], self.x1, ALU.add))
            c.settle()
            c.did(nc.vector.tensor_tensor(self.r, self.r, k.brow["mix_b2"][:, :], ALU.add))
            c.settle()
            stats("var2")
        if e == 15:
            norm("std2", self.r, "ln2_g")
            c.did(nc.vector.tensor_tensor(self.r, self.r, k.brow["ln2_b"][:, :], ALU.add))
            c.settle()
            dve.wait_ge(self.stored[par], r * 32 + 32)
            nc.vector.tensor_tensor(self.res[par], self.r, self.x[par], ALU.add).then_inc(s["res"], 1)
        if e == 16:
            c.end()


def run_layer(nc, t, out):
    with ExitStack() as ctx:
        k = Kernel(nc, ctx, t)
        k.allocate()
        k.setup()
        k.end_phase()
        k.project()
        k.scale_nodes()
        k.end_phase()
        k.aggregate("agg1", k.t_g1, KeyValueSums(k))
        k.end_phase()
        k.between()
        k.aggregate("agg2", k.t_g2, Mixer(k))
        k.end_phase()
        k.gate()
        k.route()
        k.scatter()
        k.end_phase()
        k.experts()
        k.combine(out)


_NAMES = {"x": "x", "src": "src", "dst": "dst", "gnn_W1": "L0_gnn_W1", "gnn_b1": "L0_gnn_b1", "gnn_W2": "L0_gnn_W2",
          "gnn_b2": "L0_gnn_b2", "mix_WqkvT": "L0_mix_Wqkv", "ln1_g": "L0_mix_ln1_g", "ln1_b": "L0_mix_ln1_b",
          "mix_W1T": "L0_mix_W1", "mix_b1": "L0_mix_b1", "mix_W2T": "L0_mix_W2", "mix_b2": "L0_mix_b2",
          "ln2_g": "L0_mix_ln2_g", "ln2_b": "L0_mix_ln2_b", "ffn_Wg": "L0_ffn_Wg", "ffn_bg": "L0_ffn_bg",
          "ffn_W1": "L0_ffn_W1", "ffn_b1": "L0_ffn_b1", "ffn_W2": "L0_ffn_W2", "ffn_b2": "L0_ffn_b2"}


def _laid_out(name, a):
    if name in ("mix_WqkvT", "mix_W1T", "mix_W2T"):
        return a.T
    if name == "mix_b1":
        return a.reshape(-1, 128).T
    if name == "ffn_W1":
        e, d, h = a.shape
        return a.reshape(e, d // 128, 128, h).transpose(2, 0, 1, 3)
    if name == "ffn_W2":
        e, h, d = a.shape
        return a.reshape(e, h // 128, 128, d).transpose(2, 0, 1, 3)
    if name == "ffn_b1":
        return a.reshape(a.shape[0], -1, 128).transpose(2, 0, 1)
    return a


def kernel(**inputs):
    import numpy as _np
    import concourse.bacc as _bacc
    from concourse.bass_utils import run_bass_kernel_spmd as _run

    nc = _bacc.Bacc("TRN2", target_bir_lowering=False, num_devices=1)
    arrays, t = {}, {}
    for name, given in _NAMES.items():
        a = _np.ascontiguousarray(_laid_out(name, _np.asarray(inputs[given])))
        arrays[f"in_{name}"] = a
        t[name] = nc.dram_tensor(f"in_{name}", a.shape, mybir.dt.from_np(a.dtype), kind="ExternalInput").ap()
    out = nc.dram_tensor("out_0", arrays["in_x"].shape, F32, kind="ExternalOutput").ap()
    run_layer(nc, t, out)
    r = _run(nc, [arrays], core_ids=[0])
    return r.results[0]["out_0"]
```

```python
from contextlib import ExitStack

import concourse.bass as bass
from concourse import mybir

F32 = mybir.dt.float32
BF16 = mybir.dt.bfloat16
I32 = mybir.dt.int32
ALU = mybir.AluOpType
ACT = mybir.ActivationFunctionType
AX = mybir.AxisListType
DVE_ONLY = (mybir.EngineType.DVE,)
PE_ONLY = (mybir.EngineType.PE,)
ds = bass.ds

P = 125
ROWS16 = 112
EPS_LN = 1e-5
EPS_ATTN = 1e-6


class Steps:

    def __init__(self, eng, sem, base, per_body):
        self.eng, self.sem, self.base, self.n, self.per_body = eng, sem, base, 0, per_body

    def did(self, ins):
        ins.then_inc(self.sem, 1)
        self.n += 1

    def settle(self):
        self.eng.wait_ge(self.sem, self.base + self.n)

    def end(self):
        assert self.per_body is None or self.n == self.per_body, (self.n, self.per_body)


def spread(ap, dim, n):
    ap = ap.unsqueeze(dim)
    return ap.broadcast_to(tuple(n if i == dim else d for i, d in enumerate(ap.shape)))


def row_pieces(dst, src):
    yield dst[0:ROWS16], src[0:ROWS16]
    yield dst[ROWS16:P], src[ROWS16:P]


def move_rows(eng, dst, src, sem):
    for d, s in row_pieces(dst, src):
        eng.dma_start(d, s).then_inc(sem, 16)


class Kernel:
    def __init__(self, nc, ctx, t):
        self.nc, self.ctx, self.t, self.phase_sems = nc, ctx, t, []
        self.N, self.C = t["x"].shape
        self.NT = self.N // P
        self.E = t["src"].shape[0]
        self.ET = self.E // P
        self.EPT = self.ET // self.NT
        self.F = t["gnn_W1"].shape[1]
        assert self.N == self.NT * P and self.ET == self.EPT * self.NT and self.NT % 4 == 0
        assert self.F == 128 and self.C == 256

    def sb(self, name, shape, dt=F32):
        return self.ctx.enter_context(self.nc.sbuf_tensor(name, shape, dt))

    def sem(self, name):
        self.phase_sems.append(self.nc.alloc_semaphore(name=name))
        return self.phase_sems[-1]

    def end_phase(self):
        self.nc.all_engine_barrier()
        self.nc.clear_and_free_semaphores(self.phase_sems)
        self.nc.all_engine_barrier()
        self.phase_sems = []

    def dram(self, name, shape, dt=F32):
        return self.nc.dram_tensor(name, shape, dt, kind="Internal").ap()

    def carve(self, flat):
        at = [0]

        def take(n):
            at[0] += n
            assert at[0] <= flat.shape[1], (at[0], flat.shape)
            return flat[:, at[0] - n:at[0]]
        return take

    def inverse_std(self, act, out, var, ln_done, count, done):
        self.nc.scalar.activation(out, var, ACT.Ln, bias=self.epsc[:, 0:1]).then_inc(ln_done, 1)
        act.wait_ge(ln_done, count)
        self.nc.scalar.activation(out, out, ACT.Exp, scale=-0.5).then_inc(done, 1)

    def pipeline(self, eng, stages, tiles, ring=2):
        deepest = max(lag for lag, _ in stages)
        first = -(-(deepest + ring) // ring) * ring
        last = tiles - tiles % ring

        def step(i, h):
            for lag, stage in stages:
                n = ring * i + h - lag if isinstance(i, int) else i * ring + (h - lag)
                if isinstance(n, int) and not 0 <= n < tiles:
                    continue
                stage(n, (h - lag) % ring, i + (h - lag) // ring)
        for k in range(first):
            step(k // ring, k % ring)
        with eng.Fori(first // ring, last // ring) as i:
            for h in range(ring):
                step(i, h)
        for k in range(last, tiles + deepest):
            step(k // ring, k % ring)

    def allocate(self):
        NT, ET, EPT, F, C = self.NT, self.ET, self.EPT, self.F, self.C
        self.bank = [self.ctx.enter_context(self.nc.psum_tensor(f"bank{i}", [128, 512], F32)) for i in range(8)]
        self.nodes1 = self.sb("nodes1", [128, NT * F])
        self.aggT = self.sb("aggT", [128, (NT + 1) * P])
        self.SLOTS = 2 * EPT
        self.rows_flat = self.sb("gathered_rows", [128, self.SLOTS * F])
        self.rows = self.rows_flat[0:P, :].rearrange("p (a f) -> p a f", f=F)
        self.srcT = self.sb("srcT", [P, ET], I32)
        self.dstT = self.sb("dstT", [P, ET])
        self.DPAD = 20
        self.winstart = self.sb("window_start", [1, NT * self.DPAD], I32)
        self.dinv = self.sb("dinv", [P, NT])
        self.ident = self.sb("ident", [128, 128])
        self.iota = self.sb("iota", [P, 128])
        self.ones = self.sb("ones", [128, 128])
        self.kvbd = self.sb("kv_blockdiag", [128, 2, 132])
        self.gW1 = self.sb("gnn_W1", [128, 2, F])
        self.Wqkv = self.sb("Wqkv", [128, 2, 3 * C])
        self.mW1 = self.sb("mix_W1", [128, 2, C])
        self.mW2 = self.sb("mix_W2", [128, 2, C])
        self.gW2 = self.sb("gnn_W2", [128, C])
        self.mb1 = self.sb("mix_b1", [128, 2])
        self.brow = {k: self.sb("row_" + k, [P, C]) for k in ("mix_b2", "ln1_g", "ln1_b", "ln2_g", "ln2_b", "gnn_b2")}
        self.gb1 = self.sb("gnn_b1", [P, F])
        NE, H = self.t["ffn_W1"].shape[1], self.t["ffn_W1"].shape[3]
        self.NE, self.H = NE, H
        self.Wg, self.bg = self.sb("ffn_Wg", [128, 2, NE]), self.sb("ffn_bg", [P, NE])
        self.slots = self.sb("slots", [P, 2, NT], I32)
        self.WE = 2 * H + H // 128
        self.W1e = self.nodes1[:, 0:NE * self.WE]
        self.b2e = self.nodes1[0:P, NE * self.WE:NE * (self.WE + C)]
        self.W2e = self.aggT[:, 0:NE * (H // 128) * C]
        self.gates = self.rows_flat[0:P, :][:, 0:NT * NE]
        self.W1s = [self.rows_flat[:, b * self.WE:(b + 1) * self.WE] for b in range(2)]
        self.W1_in = self.sem("W1_in")
        self.idx = [self.sb(f"idx{b}", [P, EPT], I32) for b in range(2)]
        self.onehot = [self.sb(f"onehot{b}", [P, EPT, P]) for b in range(2)]
        self.zeros = self.sb("zeros", [P, C])
        self.held = self.sb("held", [1, 2])
        self.zeros_made, self.slots_zeroed = self.sem("zeros_made"), self.sem("slots_zeroed")
        self.epsc = self.sb("eps_ln", [P, 1])
        self.work = self.sb("work", [128, 4200])
        self.t_g1 = self.dram("g1_table", [self.N, F])
        self.t_g2 = self.dram("g2_table", [self.N, F])
        self.d_xn = self.dram("xn_rows", [self.N, C])
        self.d_xnT = self.dram("xnT_tiles", [NT, 128, 2 * P])
        self.d_xmix = self.dram("xmix_rows", [self.N, C])
        self.d_x2 = self.dram("x2_rows", [self.N, C])
        self.d_xm = self.dram("xm_rows", [self.N, C])
        self.ST = 2 * NT + 8
        self.eid = self.sb("tile_expert", [1, (self.ST // 2) * 4], I32)
        self.d_xs = self.dram("expert_in_rows", [self.ST * P, C])
        self.d_ys = self.dram("expert_out_rows", [self.ST * P, C])
        self.phase_sems = []

    def pair_rows(self, ap, n):
        return ap[ds(n * P, 2 * P), :].rearrange("(b p) c -> p b c", p=P)

    def tile_rows(self, ap, n):
        return ap[ds(n * P, P), :]

    def setup(self):
        nc, t, NT, ET, EPT = self.nc, self.t, self.NT, self.ET, self.EPT
        weights_in, raw_in = self.sem("weights_in"), self.sem("raw_in")
        made, idn = self.sem("constants_made"), self.sem("identity_made")
        floated, turned, taken = self.sem("raw_floated"), self.sem("blocks_turned"), self.sem("blocks_taken")
        starts_out, chain = self.sem("starts_spread"), self.sem("setup_chain")
        NBLK = ET // 100
        raw = self.nodes1[0:100, 0:2 * NBLK * P].bitcast(I32).rearrange("p (a b e) -> p a b e", a=2, b=NBLK)
        flt = self.nodes1[0:100, 2 * NBLK * P:4 * NBLK * P].rearrange("p (a b e) -> p a b e", a=2, b=NBLK)
        take = self.carve(self.aggT)
        exact = lambda *shape: take(-(-shape[0] * shape[1] // 2))[0:P].bitcast(BF16)[:, 0:shape[0] * shape[1]]
        self.lo, self.hi = exact(NT, EPT), exact(NT, EPT)
        self.lo_is = exact(P, EPT).rearrange("p (m e) -> p m e", e=EPT)
        self.hi_is = exact(NT, EPT).rearrange("p (m e) -> p m e", e=EPT)
        self.ohl = [exact(P, EPT).rearrange("p (m e) -> p m e", e=EPT) for _ in range(2)]
        self.ohh = [exact(NT, EPT).rearrange("p (m e) -> p m e", e=EPT) for _ in range(2)]
        self.xnT = [take(2 * P).rearrange("p (k n) -> p k n", k=2) for _ in range(2)]
        self.zer = take(260)
        whole, tmp = take(ET)[0:P], take(ET)[0:P]
        loads = [
            (self.gW1[:, :, :], t["gnn_W1"].rearrange("(k p) f -> p k f", p=128)),
            (self.Wqkv[:, :, :], t["mix_WqkvT"].rearrange("(k p) f -> p k f", p=128)),
            (self.mW1[:, :, :], t["mix_W1T"].rearrange("(k p) f -> p k f", p=128)),
            (self.mW2[:, :, :], t["mix_W2T"].rearrange("(k p) f -> p k f", p=128)),
            (self.gW2[:, :], t["gnn_W2"]),
            (self.mb1[:, :], t["mix_b1"]),
            (self.gb1[:, :], spread(t["gnn_b1"], 0, P)),
            (self.Wg[:, :, :], t["ffn_Wg"].rearrange("(k p) e -> p k e", p=128)),
            (self.bg[:, :], spread(t["ffn_bg"], 0, P)),
        ] + [(self.brow[k][:, :], spread(t[k], 0, P)) for k in self.brow]

        with nc.Block() as block:
            @block.sync
            def _(sp):
                for a, name in enumerate(("src", "dst")):
                    sp.dma_start(raw[:, a, :, :], t[name].rearrange("(b p e) -> p b e", p=100, e=P)).then_inc(raw_in, 16)
                for dst, src in loads:
                    sp.dma_start(dst, src).then_inc(weights_in, 16)
                sp.wait_ge(weights_in, 16 * len(loads))

            @block.gpsimd
            def _(pool):
                nc.gpsimd.memset(self.ident[:, :], 0.0).then_inc(idn, 1)
                pool.wait_ge(idn, 1)
                nc.gpsimd.affine_select(out=self.ident[:, :], in_=self.ident[:, :], compare_op=ALU.not_equal, fill=1.0,
                                        base=0, pattern=[[-1, 128]], channel_multiplier=1).then_inc(idn, 1)
                nc.gpsimd.iota(self.iota[:, :], pattern=[[1, 128]], base=0, channel_multiplier=0,
                               allow_small_or_imprecise_dtypes=True).then_inc(made, 1)
                for out, m in ((self.lo_is, P), (self.hi_is, NT)):
                    nc.gpsimd.iota(out, pattern=[[1, m], [0, EPT]], base=0, channel_multiplier=0,
                                   allow_small_or_imprecise_dtypes=True).then_inc(made, 1)
                nc.gpsimd.memset(self.ones[:, :], 1.0).then_inc(made, 1)
                nc.gpsimd.memset(self.kvbd[:, :, :], 0.0).then_inc(made, 1)
                pool.wait_ge(idn, 2)
                nc.gpsimd.memset(self.held[:, :], 0.0).then_inc(made, 1)
                pool.wait_ge(made, 6)

            @block.tensor
            def _(pe):
                pe.wait_ge(idn, 2)
                pe.wait_ge(floated, 2)
                n = 0
                for a in range(2):
                    for b0 in range(0, NBLK, 4):
                        if n >= 4:
                            pe.wait_ge(taken, n - 3)
                        for b in range(b0, min(b0 + 4, NBLK)):
                            mm = nc.tensor.transpose(self.bank[n % 4][0:P, (b - b0) * 100:(b - b0 + 1) * 100],
                                                     flt[:, a, b, :], self.ident[0:100, 0:100])
                        mm.then_inc(turned, 1)
                        n += 1
                pe.wait_ge(made, 5)
                pe.wait_ge(taken, n)
                for c in range(4):
                    w = ET // 4
                    mm = nc.tensor.matmul(self.bank[4 + c][0:P, 0:w], self.ones[0:1, 0:P],
                                          self.dstT[0:1, c * w:(c + 1) * w], start=True, stop=True)
                    mm.then_inc(starts_out, 1)

            @block.vector
            def _(dve):
                dve.wait_ge(raw_in, 32)
                for a in range(2):
                    nc.vector.tensor_copy(flt[:, a, :, :], raw[:, a, :, :]).then_inc(floated, 1)
                n = 0
                for a, out in enumerate((self.srcT, self.dstT)):
                    for b0 in range(0, NBLK, 4):
                        k = min(4, NBLK - b0) * 100
                        dve.wait_ge(turned, n + 1)
                        nc.vector.tensor_copy(out[:, b0 * 100:b0 * 100 + k], self.bank[n % 4][0:P, 0:k]).then_inc(taken, 1)
                        n += 1
                dve.wait_ge(taken, n)
                c = Steps(dve, chain, 0, 7)
                c.did(nc.vector.tensor_scalar(tmp, self.dstT[:, :], 1.0 / P, 0.5 / P - 0.5, ALU.mult, ALU.add))
                c.settle()
                c.did(nc.vector.tensor_scalar(whole, tmp, 12582912.0, None, ALU.add))
                c.settle()
                c.did(nc.vector.tensor_scalar(tmp, whole, 12582912.0, None, ALU.subtract))
                c.settle()
                c.did(nc.vector.tensor_copy(self.hi, tmp))
                c.did(nc.vector.scalar_tensor_tensor(out=self.lo, in0=tmp, scalar=-float(P), in1=self.dstT[:, :],
                                                     op0=ALU.mult, op1=ALU.add))
                start = self.winstart[0:1, :].rearrange("a (n d) -> a n d", d=self.DPAD)
                c.did(nc.vector.memset(self.winstart[0:1, :], 0))
                c.settle()
                c.did(nc.vector.tensor_scalar(start[:, :, 0:EPT], self.dstT[0:1, :].rearrange("a (n e) -> a n e", e=EPT),
                                              0.0, float(self.N), ALU.max, ALU.min))
                c.settle()
                c.end()
                nc.vector.memset(self.epsc[:, :], EPS_LN).then_inc(taken, 1)
                nc.vector.memset(self.zeros[:, :], 0.0).then_inc(self.zeros_made, 1)
                dve.wait_ge(weights_in, 16 * len(loads))
                nc.vector.tensor_tensor(self.brow["ln2_b"][:, :], self.brow["ln2_b"][:, :], self.brow["gnn_b2"][:, :],
                                        ALU.add).then_inc(taken, 1)
                n += 2
                for k in range(4):
                    w = ET // 4
                    dve.wait_ge(starts_out, 4)
                    nc.vector.tensor_tensor(self.dstT[:, k * w:(k + 1) * w], self.dstT[:, k * w:(k + 1) * w],
                                            self.bank[4 + k][0:P, 0:w], ALU.subtract).then_inc(taken, 1)
                dve.wait_ge(taken, n + 4)

    def project(self):
        nc, t, NT, EPT, F, C = self.nc, self.t, self.NT, self.EPT, self.F, self.C
        s = {k: self.sem("p1_" + k) for k in (
            "stats", "var", "ln", "rstd", "xn", "xn_turned", "xnT", "h", "h1", "hot", "hist", "zeroed", "counted")}
        RX = 4
        x_in = [self.sem(f"p1_x_in{b}") for b in range(RX)]
        xn_st, xT_st = ([self.sem(f"p1_{k}{b}") for b in range(2)] for k in ("xn_stored", "xnT_stored"))
        take = self.carve(self.work)
        xb, xn = [take(C)[0:P] for _ in range(RX)], [take(C)[0:P] for _ in range(2)]
        small = take(40)[0:P]
        st = [small[:, 8 * b:8 * b + 6] for b in range(2)]
        mv = [small[:, 16 + 4 * b:18 + 4 * b] for b in range(2)]
        rstd = [small[:, 24 + b:25 + b] for b in range(2)]
        xnT, zer, ohl, ohh = self.xnT, self.zer, self.ohl, self.ohh
        turn, hbank, hist = self.bank[0:2], self.bank[2:4], self.bank[4]

        with nc.Block() as block:
            @block.sync
            def _(sp):
                def load(n, slot, r):
                    if not isinstance(n, int) or n >= RX:
                        sp.wait_ge(s["xn"], n - (RX - 1))
                    move_rows(sp, xb[slot], self.tile_rows(t["x"], n), x_in[slot])

                def store(n, slot, r):
                    sp.wait_ge(s["xn"], n + 1)
                    move_rows(sp, self.tile_rows(self.d_xn, n), xn[slot % 2], xn_st[slot % 2])

                def store_turned(n, slot, r):
                    sp.wait_ge(s["xnT"], n + 1)
                    sp.dma_start(self.d_xnT[ds(n, 1), :, :].rearrange("a p f -> (a p) f"),
                                 xnT[slot % 2].rearrange("p k n -> p (k n)")).then_inc(xT_st[slot % 2], 16)

                self.pipeline(sp, [(0, load), (RX - 1, store), (RX, store_turned)], NT, RX)
                for par in range(2):
                    sp.wait_ge(xn_st[par], 32 * (NT // 2))
                    sp.wait_ge(xT_st[par], 16 * (NT // 2))

            @block.vector
            def _(dve):
                nc.vector.memset(zer, 0.0).then_inc(s["zeroed"], 1)
                dve.sem_inc(s["hist"], 2)

                def stats(n, slot, r):
                    par = slot % 2
                    dve.wait_ge(x_in[slot], r * 32 + 32)
                    nc.vector.bn_stats(st[par], xb[slot]).then_inc(s["stats"], 1)
                    dve.wait_ge(s["hist"], n + 1)
                    nc.vector.tensor_tensor(ohl[par], spread(self.lo[:, ds(n * EPT, EPT)], 1, P), self.lo_is,
                                            ALU.is_equal).then_inc(s["hot"], 1)
                    dve.wait_ge(s["stats"], n + 1)
                    nc.vector.tensor_tensor(ohh[par], spread(self.hi[:, ds(n * EPT, EPT)], 1, NT), self.hi_is,
                                            ALU.is_equal).then_inc(s["hot"], 1)
                    nc.vector.bn_aggr(mv[par], st[par]).then_inc(s["var"], 1)

                def norm(n, slot, r):
                    par = slot % 2
                    dve.wait_ge(s["rstd"], n + 1)
                    if not isinstance(n, int) or n > 1:
                        dve.wait_ge(s["xn_turned"], n - 1)
                        dve.wait_ge(xn_st[par], (r * 2 + slot // 2) * 32)
                    nc.vector.tensor_scalar(xn[par], xb[slot], mv[par][:, 0:1], rstd[par], ALU.subtract,
                                            ALU.mult).then_inc(s["xn"], 1)

                self.pipeline(dve, [(0, stats), (1, norm)], NT, RX)
                dve.wait_ge(s["hist"], NT + 2)
                nc.vector.tensor_scalar(self.dinv[:, :], hist[0:P, 0:NT], 1.0, None, ALU.add).then_inc(s["counted"], 1)
                dve.wait_ge(s["counted"], 1)

            @block.tensor
            def _(pe):
                pe.wait_ge(s["zeroed"], 1)
                nc.tensor.matmul(hist[0:P, 0:NT], zer[:, 0:P], zer[:, 0:NT], start=True, stop=False, skip_group_check=True)

                def turned(n, par, r):
                    pe.wait_ge(s["xn"], n + 1)
                    for k in range(2):
                        mm = nc.tensor.transpose(turn[par][:, k * P:(k + 1) * P], xn[par][:, k * 128:(k + 1) * 128],
                                                 self.ident[0:P, 0:P])
                    mm.then_inc(s["xn_turned"], 1)

                def counts(n, par, r):
                    pe.wait_ge(s["hot"], n * 2 + 2)
                    for e in range(EPT):
                        mm = nc.tensor.matmul(hist[0:P, 0:NT], ohl[par][:, :, e], ohh[par][:, :, e], start=False,
                                              stop=False, skip_group_check=True)
                    mm.then_inc(s["hist"], 1)

                def h1(n, par, r):
                    pe.wait_ge(s["xnT"], n + 1)
                    for k in range(2):
                        mm = nc.tensor.matmul(hbank[par][0:P, 0:F], xnT[par][:, k, :], self.gW1[:, k, :],
                                              start=(k == 0), stop=(k == 1))
                    mm.then_inc(s["h"], 1)

                self.pipeline(pe, [(0, counts), (1, turned), (2, h1)], NT)

            @block.scalar
            def _(act):
                nc.scalar.preload_act_table_set("natural_log_exp_and_others")

                def inverse(n, par, r):
                    act.wait_ge(s["var"], n + 1)
                    self.inverse_std(act, rstd[par], mv[par][:, 1:2], s["ln"], n + 1, s["rstd"])

                def keep_turned(n, par, r):
                    act.wait_ge(s["xn_turned"], n + 1)
                    if not isinstance(n, int) or n > 1:
                        act.wait_ge(xT_st[par], r * 16)
                        act.wait_ge(s["h"], n - 1)
                    nc.scalar.activation(xnT[par], turn[par][:, 0:2 * P].rearrange("p (k n) -> p k n", k=2),
                                         ACT.Copy).then_inc(s["xnT"], 1)

                def keep_h1(n, par, r):
                    act.wait_ge(s["h"], n + 1)
                    nc.scalar.activation(self.nodes1[0:P, ds(n * F, F)], hbank[par][0:P, 0:F], ACT.Copy).then_inc(s["h1"], 1)

                self.pipeline(act, [(0, inverse), (1, keep_turned), (2, keep_h1)], NT)
                act.wait_ge(s["h1"], NT)

    def scale_nodes(self):
        nc, NT, F = self.nc, self.NT, self.F
        dinv_made, cleared, scaled, stored = self.sem("dinv_made"), self.sem("aggT_cleared"), self.sem("g1_scaled"), self.sem("g1_stored")
        CH = 10
        W = NT // CH
        g1 = self.nodes1[0:P, :].rearrange("p (n f) -> p n f", f=F)
        table = self.t_g1.rearrange("(n p) f -> p n f", p=P)

        def scale(eng, c):
            w = slice(c * W, (c + 1) * W)
            eng.tensor_tensor(g1[:, w, :], g1[:, w, :], spread(self.dinv[:, w], 2, F),
                              ALU.mult).then_inc(scaled, 1)

        with nc.Block() as block:
            @block.gpsimd
            def _(pool):
                nc.gpsimd.memset(self.aggT[:, :], 0.0).then_inc(cleared, 1)
                pool.wait_ge(cleared, 1)

            @block.scalar
            def _(act):
                nc.scalar.activation(self.dinv[:, :], self.dinv[:, :], ACT.Sqrt).then_inc(dinv_made, 1)

            @block.vector
            def _(dve):
                dve.wait_ge(dinv_made, 1)
                nc.vector.reciprocal(self.dinv[:, :], self.dinv[:, :]).then_inc(dinv_made, 1)
                dve.wait_ge(dinv_made, 2)
                for c in range(CH):
                    scale(nc.vector, c)

            @block.sync
            def _(sp):
                for c in range(CH):
                    w = slice(c * W, (c + 1) * W)
                    sp.wait_ge(scaled, c + 1)
                    for a, b in ((0, ROWS16), (ROWS16, P)):
                        sp.dma_start(table[a:b, w, :], g1[a:b, w, :]).then_inc(stored, 16)
                sp.wait_ge(stored, 32 * CH)

    def aggregate(self, name, table, beside=None):
        nc, NT, EPT = self.nc, self.NT, self.EPT
        SL, WB = self.SLOTS, 2
        idx, onehot, window = self.idx, self.onehot, self.bank[0:WB]
        got = [self.sem(f"{name}_row{k}") for k in range(SL)]
        indexed, hot, summed, added = (self.sem(f"{name}_{k}") for k in ("indexed", "hot", "summed", "added"))

        with self.nc.Block() as block:
            @block.gpsimd
            def _(pool):
                with pool.Fori(0, NT // 2) as i:
                    for par in range(2):
                        n = i * 2 + par
                        pool.wait_ge(summed, n * EPT + EPT)
                        nc.gpsimd.tensor_copy(idx[par][:, :], self.srcT[:, ds(n * EPT, EPT)]).then_inc(indexed, 1)
                        pool.wait_ge(indexed, n * 2 + 1)
                        nc.gpsimd.tensor_tensor(self.held[:, 0:1], self.held[:, 1:2], self.held[:, 1:2],
                                                ALU.add).then_inc(indexed, 1)
                        for e in range(EPT):
                            k = par * EPT + e
                            nc.gpsimd.indirect_dma_start(
                                self.rows[:, k, :], None, table,
                                bass.IndirectOffsetOnAxis(ap=idx[par][:, e:e + 1], axis=0)).then_inc(got[k], 16)

            @block.tensor
            def _(pe):
                if beside:
                    beside.pe_start(pe)

                def pair(i):
                    for par in range(2):
                        n = i * 2 + par
                        pe.wait_ge(hot, n + 1)
                        for e in range(EPT):
                            k = par * EPT + e
                            pe.wait_ge(got[k], (i + 1) * 16)
                            pe.wait_ge(added, n * EPT + (e + 1))
                            nc.tensor.matmul(window[k % WB][:, 0:P], self.rows[:, k, :], onehot[par][:, e, :],
                                             start=True, stop=True).then_inc(summed, 1)
                            if beside:
                                beside.pe(pe, n, par, i, e)
                pair(0)
                with pe.Fori(1, NT // 2) as i:
                    pair(i)
                if beside:
                    beside.pe_end(pe)

            @block.vector
            def _(dve):
                dve.sem_inc(summed, SL)
                dve.sem_inc(added, WB)

                def hots(n, par):
                    nc.vector.tensor_tensor(onehot[par][:, :, :], spread(self.iota[:, 0:P], 1, EPT),
                                            spread(self.dstT[:, ds(n * EPT, EPT)], 2, P),
                                            ALU.is_equal).then_inc(hot, 1)

                def group(n, par, r, more):
                    _, starts = nc.values_load_multi_w_load_instructions(
                        self.winstart[0:1, ds(n * self.DPAD, self.DPAD)], engines=DVE_ONLY, min_val=0, max_val=self.N,
                        skip_runtime_bounds_check_because="clamped to [0, N] when made")
                    if more:
                        dve.wait_ge(summed, n * EPT + SL)
                        hots(n + 1, 1 - par)
                    for e in range(EPT):
                        k = par * EPT + e
                        dve.wait_ge(summed, n * EPT + (e + 1 + SL))
                        dve.wait_ge(added, n * EPT + (e + WB))
                        at = self.aggT[:, ds(starts[e], P)]
                        nc.vector.tensor_tensor(at, at, window[k % WB][:, 0:P], ALU.add).then_inc(added, 1)
                        if beside:
                            beside.dve(dve, n, par, r, e)

                if beside:
                    beside.dve_start(dve)
                hots(0, 0)
                group(0, 0, 0, True)
                group(1, 1, 0, True)
                with dve.Fori(1, NT // 2 - 1) as i:
                    group(i * 2, 0, i, True)
                    group(i * 2 + 1, 1, i, True)
                group(NT - 2, 0, NT // 2 - 1, True)
                group(NT - 1, 1, NT // 2 - 1, False)
                dve.wait_ge(added, self.ET + WB)
                if beside:
                    beside.dve_end(dve)

            if beside:
                @block.sync
                def _(sp):
                    beside.sync(sp)

                @block.scalar
                def _(act):
                    beside.scalar(act)

    def load_experts(self, sp):
        t, NE, H, C = self.t, self.NE, self.H, self.C
        W = self.W1e.rearrange("p (e w) -> p e w", e=NE)
        sp.dma_start(W[:, :, 0:2 * H], t["ffn_W1"].rearrange("p e k h -> p e (k h)")).then_inc(self.W1_in, 16)
        sp.dma_start(W[:, :, 2 * H:self.WE], t["ffn_b1"]).then_inc(self.W1_in, 16)
        sp.dma_start(self.b2e, spread(t["ffn_b2"].rearrange("e c -> (e c)"), 0, P)).then_inc(self.W1_in, 16)

    def zero_slots(self, sp):
        self.zero_dmas = 4
        w = self.ST // self.zero_dmas
        rows = self.d_xs.rearrange("(j p) c -> p j c", p=P)
        sp.wait_ge(self.zeros_made, 1)
        for z in range(self.zero_dmas):
            sp.dma_start(rows[:, z * w:(z + 1) * w, :],
                         spread(self.zeros[0:P, :], 1, w)).then_inc(self.slots_zeroed, 16)

    def between(self):
        nc, NT, F = self.nc, self.NT, self.F
        G = 4
        joined, biased, ready, turned, kept, brought = (self.sem("p3_" + k) for k in (
            "joined", "biased", "ready", "turned", "kept", "brought"))
        stored = [self.sem(f"p3_stored{b}") for b in range(2)]
        chain = self.sem("p3_chain")
        flat = self.rows_flat[0:P, :]
        a1 = [flat[:, b * G * F:(b + 1) * G * F].rearrange("p (g f) -> p g f", g=G) for b in range(2)]
        g2 = [flat[:, (2 + b) * G * F:(3 + b) * G * F].rearrange("p (g f) -> p g f", g=G) for b in range(2)]
        take = self.carve(self.work)
        agg = [take(G * P) for _ in range(2)]
        table = self.t_g2.rearrange("(n p) f -> p n f", p=P)
        NG = NT // G
        sums, turns = self.bank[0:2], self.bank[2:4]

        def over(eng, A, B):
            A(0, 0, 0)
            with eng.Fori(0, (NG - 1) // 2) as i:
                A(i * 2 + 1, 1, i)
                B(i * 2, 0, i)
                A(i * 2 + 2, 0, i + 1)
                B(i * 2 + 1, 1, i)
            B(NG - 1, 0, (NG - 1) // 2)

        with nc.Block() as block:
            @block.tensor
            def _(pe):
                def A(g, par, r):
                    pe.wait_ge(biased, g + 1)
                    pe.wait_ge(brought, g + 1)
                    for k in range(G):
                        nc.tensor.matmul(sums[par][0:P, k * F:(k + 1) * F], agg[par][:, k * P:(k + 1) * P],
                                         self.ident[:, :], start=True, stop=False, skip_group_check=True)
                        mm = nc.tensor.matmul(sums[par][0:P, k * F:(k + 1) * F], self.ident[0:P, 0:P],
                                              self.nodes1[0:P, ds((g * G + k) * F, F)], start=False, stop=True,
                                              skip_group_check=True)
                    mm.then_inc(joined, 1)

                def B(g, par, r):
                    pe.wait_ge(ready, g + 1)
                    pe.wait_ge(kept, g + 1)
                    for k in range(G):
                        mm = nc.tensor.transpose(turns[par][:, k * P:(k + 1) * P], g2[par][:, k, :], self.ident[0:P, 0:P])
                    mm.then_inc(turned, 1)
                over(pe, A, B)

            @block.vector
            def _(dve):
                dve.sem_inc(biased, 2)
                dve.sem_inc(kept, 2)

                def group(g, par, r, first):
                    d = spread(self.dinv[:, ds(g * G, G)], 2, F)
                    dve.wait_ge(joined, g + 1)
                    nc.vector.tensor_tensor(a1[par], sums[par][0:P, 0:G * F].rearrange("p (g f) -> p g f", g=G), d,
                                            ALU.mult).then_inc(biased, 1)
                    dve.wait_ge(biased, g + 3)
                    nc.vector.tensor_tensor(a1[par], a1[par], spread(self.gb1[:, :], 1, G),
                                            ALU.add).then_inc(chain, 1)
                    dve.wait_ge(chain, g + 1)
                    if not first:
                        dve.wait_ge(stored[par], r * 32)
                        dve.wait_ge(turned, g - 1)
                    nc.vector.scalar_tensor_tensor(out=g2[par], in0=a1[par], scalar=0.0, in1=d, op0=ALU.max,
                                                   op1=ALU.mult).then_inc(ready, 1)
                group(0, 0, 0, True)
                group(1, 1, 0, True)
                with dve.Fori(1, (NG - 1) // 2) as i:
                    group(i * 2, 0, i, False)
                    group(i * 2 + 1, 1, i, False)
                group(NG - 1, 0, (NG - 1) // 2, False)

            @block.scalar
            def _(act):
                def bring(g, par, r):
                    if not isinstance(g, int) or g > 1:
                        act.wait_ge(joined, g - 1)
                    nc.scalar.activation(agg[par], self.aggT[:, ds(g * (G * P), G * P)], ACT.Copy).then_inc(brought, 1)

                def keep(g, par, r):
                    act.wait_ge(turned, g + 1)
                    act.wait_ge(brought, g + 1)
                    nc.scalar.activation(self.aggT[:, ds(g * (G * P), G * P)], turns[par][:, 0:G * P],
                                         ACT.Copy).then_inc(kept, 1)
                self.pipeline(act, [(0, bring), (2, keep)], NG)
                act.wait_ge(kept, NG + 2)

            @block.sync
            def _(sp):
                def store(g, par):
                    sp.wait_ge(ready, g + 1)
                    for a, b in ((0, ROWS16), (ROWS16, P)):
                        sp.dma_start(table[a:b, ds(g * G, G), :], g2[par][a:b, :, :]).then_inc(stored[par], 16)
                with sp.Fori(0, (NG - 1) // 2) as i:
                    for par in range(2):
                        store(i * 2 + par, par)
                store(NG - 1, 0)
                sp.wait_ge(stored[0], 32 * ((NG + 1) // 2))
                sp.wait_ge(stored[1], 32 * (NG // 2))


    def gate(self):
        nc, NT, C, NE = self.nc, self.NT, self.C, self.NE
        s = {k: self.sem("p5_" + k) for k in (
            "brought", "gnn", "x2", "stats", "var", "ln", "rstd", "xm", "xm_turned", "xmT", "score", "scored")}
        RX = 8
        x_in, x2_st, xm_st = ([self.sem(f"p5_{k}{b}") for b in range(RX // 2)] for k in ("x_in", "x2_stored", "xm_stored"))
        take = self.carve(self.work)
        spare = [self.carve(self.onehot[b][:, :, :].rearrange("p a b -> p (a b)")) for b in range(2)]
        xb2, x22, xm2 = ([piece(2 * C)[0:P].rearrange("p (b c) -> p b c", c=C) for _ in range(RX // 2)]
                         for piece in (take, spare[0], spare[1]))
        xb, x2, xm = ([buf[b // 2][:, b % 2, :] for b in range(RX)] for buf in (xb2, x22, xm2))
        agg = [take(P) for _ in range(2)]
        xmT = [take(2 * P).rearrange("p (k n) -> p k n", k=2) for _ in range(2)]
        small = take(40)[0:P]
        st = [small[:, 8 * b:8 * b + 6] for b in range(2)]
        mv = [small[:, 16 + 4 * b:18 + 4 * b] for b in range(2)]
        rstd = [small[:, 24 + b:25 + b] for b in range(2)]
        scratch = small[0:1, 26:27]
        gbank, turn, sbank = self.bank[0:2], self.bank[2:4], self.bank[4:6]

        with nc.Block() as block:
            @block.sync
            def _(sp):
                def load(n, slot, r):
                    if slot % 2 == 0:
                        if not isinstance(n, int) or n >= RX:
                            sp.wait_ge(s["x2"], n - (RX - 2))
                        move_rows(sp, xb2[slot // 2], self.pair_rows(self.d_xmix, n), x_in[slot // 2])

                def store(n, slot, r):
                    if slot % 2 == 0:
                        sp.wait_ge(s["x2"], n + 2)
                        move_rows(sp, self.pair_rows(self.d_x2, n), x22[slot // 2], x2_st[slot // 2])
                        sp.wait_ge(s["xm"], n + 2)
                        move_rows(sp, self.pair_rows(self.d_xm, n), xm2[slot // 2], xm_st[slot // 2])

                self.pipeline(sp, [(0, load), (5, store)], NT, RX)
                for b in range(RX // 2):
                    stores = len(range(2 * b, NT, RX))
                    sp.wait_ge(x2_st[b], 32 * stores)
                    sp.wait_ge(xm_st[b], 32 * stores)

            @block.scalar
            def _(act):
                nc.scalar.preload_act_table_set("natural_log_exp_and_others")

                def bring(n, par, r):
                    if not isinstance(n, int) or n > 1:
                        act.wait_ge(s["gnn"], n - 1)
                    nc.scalar.activation(agg[par], self.aggT[:, ds(n * P, P)], ACT.Copy).then_inc(s["brought"], 1)

                def inverse(n, par, r):
                    act.wait_ge(s["var"], n + 1)
                    self.inverse_std(act, rstd[par], mv[par][:, 1:2], s["ln"], n + 1, s["rstd"])

                def keep_turned(n, par, r):
                    act.wait_ge(s["xm_turned"], n + 1)
                    if not isinstance(n, int) or n > 1:
                        act.wait_ge(s["score"], n - 1)
                    nc.scalar.activation(xmT[par], turn[par][:, 0:2 * P].rearrange("p (k n) -> p k n", k=2),
                                         ACT.Copy).then_inc(s["xmT"], 1)
                self.pipeline(act, [(0, bring), (1, inverse), (3, keep_turned)], NT)

            @block.tensor
            def _(pe):
                def gnn(n, slot, r):
                    par = slot % 2
                    pe.wait_ge(s["brought"], n + 1)
                    if not isinstance(n, int) or n > 1:
                        pe.wait_ge(s["x2"], n - 1)
                    nc.tensor.matmul(gbank[par][0:P, 0:C], agg[par], self.gW2[:, :], start=True,
                                     stop=True).then_inc(s["gnn"], 1)

                def turned(n, slot, r):
                    par = slot % 2
                    pe.wait_ge(s["xm"], n + 1)
                    for k in range(2):
                        mm = nc.tensor.transpose(turn[par][:, k * P:(k + 1) * P], xm[slot][:, k * 128:(k + 1) * 128],
                                                 self.ident[0:P, 0:P])
                    mm.then_inc(s["xm_turned"], 1)

                def score(n, slot, r):
                    par = slot % 2
                    pe.wait_ge(s["xmT"], n + 1)
                    if not isinstance(n, int) or n > 1:
                        pe.wait_ge(s["scored"], n - 1)
                    for k in range(2):
                        mm = nc.tensor.matmul(sbank[par][0:P, 0:NE], xmT[par][:, k, :], self.Wg[:, k, :],
                                              start=(k == 0), stop=(k == 1))
                    mm.then_inc(s["score"], 1)
                self.pipeline(pe, [(0, gnn), (2, turned), (3, score)], NT, RX)

            @block.vector
            def _(dve):
                def x2_stats(n, slot, r):
                    par = slot % 2
                    dve.wait_ge(x_in[slot // 2], r * 32 + 32)
                    if not isinstance(n, int) or n >= RX:
                        dve.wait_ge(x2_st[slot // 2], r * 32)
                        dve.wait_ge(s["xm"], n - (RX - 1))
                    dve.wait_ge(s["gnn"], n + 1)
                    nc.vector.scalar_tensor_tensor(out=x2[slot], in0=gbank[par][0:P, 0:C], scalar=self.dinv[:, ds(n, 1)],
                                                   in1=xb[slot], op0=ALU.mult, op1=ALU.add).then_inc(s["x2"], 1)
                    dve.wait_ge(s["x2"], n + 1)
                    nc.vector.bn_stats(st[par], x2[slot]).then_inc(s["stats"], 1)
                    if not isinstance(n, int) or n > 1:
                        dve.wait_ge(s["xm"], n - 1)
                    dve.wait_ge(s["stats"], n + 1)
                    nc.vector.memset(scratch, 0.0)
                    nc.vector.bn_aggr(mv[par], st[par]).then_inc(s["var"], 1)

                def norm(n, slot, r):
                    par = slot % 2
                    dve.wait_ge(s["rstd"], n + 1)
                    if not isinstance(n, int) or n >= RX:
                        dve.wait_ge(s["xm_turned"], n - (RX - 1))
                        dve.wait_ge(xm_st[slot // 2], r * 32)
                    nc.vector.tensor_scalar(xm[slot], x2[slot], mv[par][:, 0:1], rstd[par], ALU.subtract,
                                            ALU.mult).then_inc(s["xm"], 1)

                def scored(n, slot, r):
                    dve.wait_ge(s["score"], n + 1)
                    nc.vector.tensor_tensor(self.gates[:, ds(n * NE, NE)], sbank[slot % 2][0:P, 0:NE], self.bg[:, :],
                                            ALU.add).then_inc(s["scored"], 1)
                self.pipeline(dve, [(0, x2_stats), (1, norm), (3, scored)], NT, RX)
                dve.wait_ge(s["scored"], NT)

    def route(self):
        nc, NT, NE, ST = self.nc, self.NT, self.NE, self.ST
        chain, made, counted, W2_in = (self.sem("p6_" + k) for k in ("chain", "made", "counted", "W2_in"))
        take = self.carve(self.rows_flat[0:P, :])
        grid = lambda flat: flat.rearrange("p (n e) -> p n e", e=NE)
        take(NT * NE)
        gates = grid(self.gates)
        first, second, upto, tmp = (grid(take(NT * NE)) for _ in range(4))
        best, ones8 = take(NT), take(NT)
        more = self.carve(self.work)
        mark = grid(more(NT * NE)[0:P])
        fits = more(NE * NT)[0:P].rearrange("p (e j) -> p e j", e=NE)
        past = more(ST * NE)[0:1]
        tile_no, tiles125 = more(ST)[0:1], more(NT)[0:P]
        rank8, per, total, ntile, upto8, base, own = (more(NE)[0:P] for _ in range(7))
        low, eidf = more(128), more(ST)[0:1]
        sums = self.bank[0]

        with nc.Block() as block:
            @block.sync
            def _(sp):
                sp.dma_start(self.W2e, self.t["ffn_W2"].rearrange("p e c d -> p (e c d)")).then_inc(W2_in, 16)
                sp.wait_ge(W2_in, 16)

            @block.gpsimd
            def _(pool):
                nc.gpsimd.affine_select(out=low, in_=self.ones[:, :], compare_op=ALU.is_gt, fill=0.0, base=0,
                                        pattern=[[1, 128]], channel_multiplier=-1).then_inc(made, 1)
                nc.gpsimd.iota(tile_no, pattern=[[1, ST]], base=0, channel_multiplier=0,
                               allow_small_or_imprecise_dtypes=True).then_inc(made, 1)
                nc.gpsimd.iota(tiles125, pattern=[[P, NT]], base=0, channel_multiplier=0,
                               allow_small_or_imprecise_dtypes=True).then_inc(made, 1)
                pool.wait_ge(made, 3)

            @block.tensor
            def _(pe):
                pe.wait_ge(made, 3)
                pe.wait_ge(counted, 1)
                nc.tensor.matmul(sums[0:P, 0:NE], low[0:P, 0:P], per, start=True, stop=True)
                nc.tensor.matmul(sums[0:P, NE:2 * NE], self.ones[0:P, 0:P], per, start=True, stop=True).then_inc(counted, 1)

            @block.vector
            def _(dve):
                c = Steps(dve, chain, 0, None)
                v = nc.vector

                def step(ins):
                    c.did(ins)
                    c.settle()
                step(v.tensor_scalar(rank8, self.iota[:, 0:NE], -1.0, float(NE), ALU.mult, ALU.add))
                step(v.memset(ones8, 1.0))

                def pick(scores, chosen):
                    step(v.tensor_reduce(best, scores, AX.X, ALU.max))
                    step(v.tensor_tensor(tmp, scores, spread(best, 2, NE), ALU.is_equal))
                    step(v.tensor_tensor(mark, tmp, spread(rank8, 1, NT), ALU.mult))
                    step(v.tensor_reduce(best, mark, AX.X, ALU.max))
                    step(v.tensor_tensor(chosen, mark, spread(best, 2, NE), ALU.is_equal))
                pick(gates, first)
                step(v.scalar_tensor_tensor(out=gates, in0=first, scalar=-3.0e38, in1=gates, op0=ALU.mult, op1=ALU.add))
                pick(gates, second)
                step(v.tensor_tensor(mark, first, second, ALU.add))
                for e in range(NE):
                    c.did(v.tensor_tensor_scan(out=upto[:, :, e], data0=ones8, data1=mark[:, :, e], initial=0.0,
                                               op0=ALU.mult, op1=ALU.add))
                c.settle()
                v.tensor_copy(per, upto[:, NT - 1, :]).then_inc(counted, 1)
                dve.wait_ge(counted, 2)
                step(v.tensor_copy(total, sums[0:P, NE:2 * NE]))
                step(v.tensor_copy(own, sums[0:P, 0:NE]))
                dve.wait_ge(made, 3)
                step(v.tensor_tensor(fits, spread(total, 2, NT), spread(tiles125, 1, NE), ALU.is_gt))
                step(v.tensor_reduce(ntile, fits, AX.X, ALU.add))
                step(v.tensor_tensor_scan(out=upto8, data0=ones8[:, 0:NE], data1=ntile, initial=0.0, op0=ALU.mult,
                                          op1=ALU.add))
                step(v.tensor_tensor(base, upto8, ntile, ALU.subtract))
                step(v.tensor_scalar(base, base, float(P), -1.0, ALU.mult, ALU.add))
                step(v.tensor_tensor(base, base, own, ALU.add))
                step(v.tensor_tensor(upto, upto, spread(base, 1, NT), ALU.add))
                for k, chosen in enumerate((first, second)):
                    step(v.tensor_tensor(tmp, upto, chosen, ALU.mult))
                    step(v.tensor_reduce(best, tmp, AX.X, ALU.add))
                    step(v.tensor_copy(self.slots[:, k, :], best))
                pastv = past.rearrange("a (j e) -> a j e", e=NE)
                step(v.tensor_tensor(pastv, spread(tile_no, 2, NE), spread(upto8[0:1, :], 1, ST), ALU.is_ge))
                step(v.tensor_reduce(eidf, pastv, AX.X, ALU.add))
                step(v.memset(self.eid[:, :], 0))
                step(v.tensor_scalar(self.eid[0:1, :].rearrange("a (j k) -> a j k", k=4)[:, :, 0:2],
                                     eidf.rearrange("a (j k) -> a j k", k=2), float(NE - 1), None, ALU.min))

    def scatter(self):
        nc, NT, C = self.nc, self.NT, self.C
        RX = 8
        x_in, sent = ([self.sem(f"p7_{k}{b}") for b in range(RX // 2)] for k in ("x_in", "sent"))
        indexed = self.sem("p7_indexed")
        take = self.carve(self.work)
        xm = [take(2 * C)[0:P].rearrange("p (b c) -> p b c", c=C) for _ in range(RX // 2)]
        idx = [take(4)[0:P].bitcast(I32).rearrange("p (k b) -> p k b", b=2) for _ in range(RX // 2)]

        with nc.Block() as block:
            @block.sync
            def _(sp):
                def load(n, slot, r):
                    if slot % 2 == 0:
                        if not isinstance(n, int) or n >= RX:
                            sp.wait_ge(sent[slot // 2], r * 64)
                        move_rows(sp, xm[slot // 2], self.pair_rows(self.d_xm, n), x_in[slot // 2])
                self.pipeline(sp, [(0, load)], NT, RX)

            @block.gpsimd
            def _(pool):
                def send(n, slot, r):
                    half = slot // 2
                    if slot % 2 == 0:
                        if not isinstance(n, int) or n >= RX:
                            pool.wait_ge(sent[half], r * 64)
                        nc.gpsimd.tensor_copy(idx[half], self.slots[:, :, ds(n, 2)]).then_inc(indexed, 1)
                        pool.wait_ge(indexed, n + 1)
                        pool.wait_ge(x_in[half], r * 32 + 32)
                        nc.gpsimd.tensor_tensor(self.held[:, 0:1], self.held[:, 1:2], self.held[:, 1:2],
                                                ALU.add).then_inc(indexed, 1)
                    for k in range(2):
                        nc.gpsimd.indirect_dma_start(
                            self.d_xs, bass.IndirectOffsetOnAxis(ap=idx[half][:, k, slot % 2:slot % 2 + 1], axis=0),
                            xm[half][:, slot % 2, :], None).then_inc(sent[half], 16)
                self.pipeline(pool, [(0, send)], NT, RX)
                for b in range(RX // 2):
                    pool.wait_ge(sent[b], 64 * len(range(2 * b, NT, RX)))

    def experts(self):
        nc, C, ST, NE, H = self.nc, self.C, self.ST, self.NE, self.H
        HC = H // 128
        s = {k: self.sem("p8_" + k) for k in ("turned", "xT", "W1", "h", "hT", "y", "kept")}
        RX = 8
        x_in, y_st = ([self.sem(f"p8_{k}{b}") for b in range(RX // 2)] for k in ("x_in", "y_stored"))
        take = self.carve(self.work)
        spare = self.carve(self.onehot[0][:, :, :].rearrange("p a b -> p (a b)"))
        xb2, yb2 = ([piece(2 * C)[0:P].rearrange("p (b c) -> p b c", c=C) for _ in range(RX // 2)]
                    for piece in (take, spare))
        xb, yb = ([buf[b // 2][:, b % 2, :] for b in range(RX)] for buf in (xb2, yb2))
        xT = [take(2 * P).rearrange("p (k n) -> p k n", k=2) for _ in range(2)]
        hT = [take(HC * P) for _ in range(2)]
        W1s = self.W1s
        turn, hbank, ybank = self.bank[0:2], self.bank[2:4], self.bank[4:6]
        WE = self.WE

        def expert_ids(engines, r):
            return nc.values_load_multi_w_load_instructions(
                self.eid[0:1, ds(r * 4, 4)], engines=engines, min_val=0, max_val=NE - 1,
                skip_runtime_bounds_check_because="a count of experts, held below their number when made")[1]

        with nc.Block() as block:
            @block.sync
            def _(sp):
                def load(n, slot, r):
                    if slot % 2 == 0:
                        if not isinstance(n, int) or n >= RX:
                            sp.wait_ge(s["turned"], n - (RX - 2))
                        move_rows(sp, xb2[slot // 2], self.pair_rows(self.d_xs, n), x_in[slot // 2])

                def store(n, slot, r):
                    if slot % 2 == 0:
                        sp.wait_ge(s["kept"], n + 2)
                        move_rows(sp, self.pair_rows(self.d_ys, n), yb2[slot // 2], y_st[slot // 2])
                self.pipeline(sp, [(0, load), (RX - 1, store)], ST, RX)
                for b in range(RX // 2):
                    sp.wait_ge(y_st[b], 32 * (ST // RX))

            @block.tensor
            def _(pe):
                def turned(n, slot, r):
                    par = slot % 2
                    pe.wait_ge(x_in[slot // 2], r * 32 + 32)
                    if not isinstance(n, int) or n > 1:
                        pe.wait_ge(s["xT"], n - 1)
                    for k in range(2):
                        mm = nc.tensor.transpose(turn[par][:, k * P:(k + 1) * P], xb[slot][:, k * 128:(k + 1) * 128],
                                                 self.ident[0:P, 0:P])
                    mm.then_inc(s["turned"], 1)

                def hidden(n, slot, r):
                    par = slot % 2
                    pe.wait_ge(s["xT"], n + 1)
                    pe.wait_ge(s["W1"], n + 1)
                    if not isinstance(n, int) or n > 1:
                        pe.wait_ge(s["hT"], (n - 1) * HC)
                    for c in range(HC):
                        for k in range(2):
                            mm = nc.tensor.matmul(hbank[par][:, c * P:(c + 1) * P],
                                                  W1s[par][:, k * H + c * 128:k * H + (c + 1) * 128], xT[par][:, k, :],
                                                  start=(k == 0), stop=(k == 1))
                    mm.then_inc(s["h"], 1)

                def output(n, slot, r):
                    par = slot % 2
                    if par == 0:
                        self.ids = expert_ids(PE_ONLY, r * (RX // 2) + slot // 2)
                    e = self.ids[par]
                    pe.wait_ge(s["hT"], (n + 1) * HC)
                    if not isinstance(n, int) or n > 1:
                        pe.wait_ge(s["kept"], n - 1)
                    out = ybank[par][0:P, 0:C]
                    for c in range(HC):
                        mm = nc.tensor.matmul(out, hT[par][:, c * P:(c + 1) * P], self.W2e[:, ds(e * (HC * C) + c * C, C)],
                                         start=(c == 0), stop=(c == HC - 1))
                    mm.then_inc(s["y"], 1)
                self.pipeline(pe, [(0, turned), (1, hidden), (2, output)], ST, RX)

            @block.scalar
            def _(act):
                def keep_turned(n, par, r):
                    act.wait_ge(s["turned"], n + 1)
                    if not isinstance(n, int) or n > 1:
                        act.wait_ge(s["h"], n - 1)
                    nc.scalar.activation(xT[par], turn[par][:, 0:2 * P].rearrange("p (k n) -> p k n", k=2),
                                         ACT.Copy).then_inc(s["xT"], 1)

                def gelu(n, par, r):
                    act.wait_ge(s["h"], n + 1)
                    if not isinstance(n, int) or n > 1:
                        act.wait_ge(s["y"], n - 1)
                    for c in range(HC):
                        nc.scalar.activation(hT[par][:, c * P:(c + 1) * P], hbank[par][:, c * P:(c + 1) * P], ACT.Gelu,
                                             bias=W1s[par][:, 2 * H + c:2 * H + c + 1]).then_inc(s["hT"], 1)
                nc.scalar.preload_act_table(ACT.Gelu)
                self.pipeline(act, [(0, keep_turned), (1, gelu)], ST)

            @block.vector
            def _(dve):
                def weights(n, slot, r):
                    par = slot % 2
                    if par == 0:
                        self.ids = expert_ids(DVE_ONLY, r * (RX // 2) + slot // 2)
                    if not isinstance(n, int) or n > 1:
                        dve.wait_ge(s["h"], n - 1)
                        dve.wait_ge(s["hT"], (n - 1) * HC)
                    nc.vector.tensor_copy(W1s[par], self.W1e[:, ds(self.ids[par] * WE, WE)]).then_inc(s["W1"], 1)

                def keep(n, slot, r):
                    par = slot % 2
                    if par == 0:
                        self.kept_ids = expert_ids(DVE_ONLY, r * (RX // 2) + slot // 2)
                    dve.wait_ge(s["y"], n + 1)
                    if not isinstance(n, int) or n >= RX:
                        dve.wait_ge(y_st[slot // 2], r * 32)
                    nc.vector.tensor_tensor(yb[slot], ybank[par][0:P, 0:C], self.b2e[:, ds(self.kept_ids[par] * C, C)],
                                            ALU.add).then_inc(s["kept"], 1)
                self.pipeline(dve, [(0, weights), (2, keep)], ST, RX)

    def combine(self, out):
        nc, NT, C = self.nc, self.NT, self.C
        RX = 8
        x_in, got, out_st = ([self.sem(f"p9_{k}{b}") for b in range(RX // 2)] for k in ("x_in", "got", "stored"))
        indexed, summed, done = (self.sem("p9_" + k) for k in ("indexed", "summed", "done"))
        pair = lambda take: [take(2 * C)[0:P].rearrange("p (b c) -> p b c", c=C) for _ in range(RX // 2)]
        take = self.carve(self.work)
        x2 = pair(take)
        ya, yb = (pair(self.carve(self.onehot[b][:, :, :].rearrange("p a b -> p (a b)"))) for b in range(2))
        idx = [take(4)[0:P].bitcast(I32).rearrange("p (k b) -> p k b", b=2) for _ in range(RX // 2)]

        with nc.Block() as block:
            @block.sync
            def _(sp):
                def load(n, slot, r):
                    if slot % 2 == 0:
                        if not isinstance(n, int) or n >= RX:
                            sp.wait_ge(out_st[slot // 2], r * 32)
                        move_rows(sp, x2[slot // 2], self.pair_rows(self.d_x2, n), x_in[slot // 2])

                def store(n, slot, r):
                    if slot % 2 == 0:
                        sp.wait_ge(done, n // 2 + 1 if isinstance(n, int) else r * (RX // 2) + (slot // 2 + 1))
                        move_rows(sp, self.pair_rows(out, n), x2[slot // 2], out_st[slot // 2])
                self.pipeline(sp, [(0, load), (4, store)], NT, RX)
                for b in range(RX // 2):
                    sp.wait_ge(out_st[b], 32 * len(range(2 * b, NT, RX)))

            @block.gpsimd
            def _(pool):
                def fetch(n, slot, r):
                    half = slot // 2
                    if slot % 2 == 0:
                        if not isinstance(n, int) or n >= RX:
                            pool.wait_ge(done, r * (RX // 2) + (half + 1 - RX // 2))
                        nc.gpsimd.tensor_copy(idx[half], self.slots[:, :, ds(n, 2)]).then_inc(indexed, 1)
                        pool.wait_ge(indexed, n + 1)
                        nc.gpsimd.tensor_tensor(self.held[:, 0:1], self.held[:, 1:2], self.held[:, 1:2],
                                                ALU.add).then_inc(indexed, 1)
                    for k, y in enumerate((ya, yb)):
                        nc.gpsimd.indirect_dma_start(
                            y[half][:, slot % 2, :], None, self.d_ys,
                            bass.IndirectOffsetOnAxis(ap=idx[half][:, k, slot % 2:slot % 2 + 1], axis=0))\
                            .then_inc(got[half], 16)
                self.pipeline(pool, [(0, fetch)], NT, RX)

            @block.vector
            def _(dve):
                def add(n, slot, r):
                    half = slot // 2
                    if slot % 2 == 0:
                        dve.wait_ge(got[half], r * 64 + 64)
                        nc.vector.tensor_tensor(ya[half], ya[half], yb[half], ALU.add).then_inc(summed, 1)
                        dve.wait_ge(x_in[half], r * 32 + 32)
                        dve.wait_ge(summed, r * (RX // 2) + (half + 1))
                        nc.vector.tensor_tensor(x2[half], x2[half], ya[half], ALU.add).then_inc(done, 1)
                self.pipeline(dve, [(0, add)], NT, RX)


class KeyValueSums:

    def __init__(self, k):
        self.k = k
        self.s = {n: k.sem("kv_" + n) for n in ("k", "v", "kmin", "kexp", "kf", "v_kept", "summed", "ready", "kept")}
        self.ins = [k.sem(f"kv_in{b}") for b in range(2)]
        take = k.carve(k.work)
        self.xnT = [take(2 * P).rearrange("p (a n) -> p a n", a=2) for _ in range(2)]
        self.kmin, self.kf = take(k.C)[0:P], take(k.C)[0:P]
        self.v = take(2 * 129)[0:P].rearrange("p (a m) -> p a m", a=2)
        self.zero = take(260)
        self.kb, self.vb, self.acc = k.bank[2:5]

    def sync(self, sp):
        k = self.k

        def load(n, par):
            sp.dma_start(self.xnT[par].rearrange("p a n -> p (a n)"),
                         k.d_xnT[ds(n, 1), :, :].rearrange("a p f -> (a p) f")).then_inc(self.ins[par], 16)
        load(0, 0)
        load(1, 1)
        k.zero_slots(sp)
        with sp.Fori(0, k.NT // 2 - 1) as i:
            for par in range(2):
                sp.wait_ge(self.s["v"], i * 2 + (par + 1))
                load(i * 2 + (par + 2), par)
        sp.wait_ge(k.slots_zeroed, 16 * k.zero_dmas)

    def pe_start(self, pe):
        pe.wait_ge(self.s["ready"], 2)
        self.k.nc.tensor.matmul(self.acc[:, 0:258], self.zero[:, 0:128], self.zero[:, 0:258], start=True, stop=False,
                                skip_group_check=True)

    def pe(self, pe, n, par, r, e):
        k, s, mm = self.k, self.s, self.k.nc.tensor.matmul
        if e == 1:
            pe.wait_ge(self.ins[par], r * 16 + 16)
            for w0, out, name in ((k.C, self.kb, "k"), (2 * k.C, self.vb, "v")):
                for c in range(2):
                    last = mm(out[0:P, 0:k.C], self.xnT[par][:, c, :], k.Wqkv[:, c, w0:w0 + k.C],
                              start=(c == 0), stop=(c == 1))
                last.then_inc(s[name], 1)
        if e == 9:
            pe.wait_ge(s["kf"], n + 1)
            pe.wait_ge(s["v_kept"], n + 1)
            for a in range(2):
                last = mm(self.acc[:, a * 129:(a + 1) * 129], self.kf[:, a * 128:(a + 1) * 128], self.v[:, a, :],
                          start=False, stop=False, skip_group_check=True)
            last.then_inc(s["summed"], 1)

    def scalar(self, act):
        k, s, nc = self.k, self.s, self.k.nc
        nc.scalar.preload_act_table_set("exp_and_others")
        act.wait_ge(s["ready"], 2)

        def tile(n):
            act.wait_ge(s["kmin"], n + 1)
            nc.scalar.activation(self.kmin, self.kmin, ACT.Exp).then_inc(s["kexp"], 1)
            act.wait_ge(s["v"], n + 1)
            if not isinstance(n, int):
                act.wait_ge(s["summed"], n)
            nc.scalar.activation(self.v[:, :, 0:128], self.vb[0:P, 0:k.C].rearrange("p (a m) -> p a m", a=2),
                                 ACT.Copy).then_inc(s["v_kept"], 1)
        tile(0)
        with act.Fori(1, k.NT) as n:
            tile(n)

    def dve(self, dve, n, par, r, e):
        k, s, nc = self.k, self.s, self.k.nc
        if e == 3:
            dve.wait_ge(s["k"], n + 1)
            nc.vector.tensor_scalar(self.kmin, self.kb[0:P, 0:k.C], 0.0, None, ALU.min).then_inc(s["kmin"], 1)
        if e == 6:
            dve.wait_ge(s["kexp"], n + 1)
            nc.vector.scalar_tensor_tensor(out=self.kf, in0=self.kb[0:P, 0:k.C], scalar=0.0, in1=self.kmin,
                                           op0=ALU.max, op1=ALU.add).then_inc(s["kf"], 1)

    def pe_end(self, pe):
        pass

    def dve_start(self, dve):
        self.k.nc.vector.memset(self.zero, 0.0).then_inc(self.s["ready"], 1)
        self.k.nc.vector.memset(self.v[:, :, 128:129], 1.0).then_inc(self.s["ready"], 1)

    def dve_end(self, dve):
        k, nc = self.k, self.k.nc
        dve.wait_ge(self.s["summed"], k.NT)
        for a in range(2):
            for h in range(4):
                q = slice(32 * h, 32 * h + 32)
                for to, of, w in ((32 * h, a * 129 + 32 * h, 32), (128 + h, a * 129 + 128, 1)):
                    nc.vector.tensor_copy(k.kvbd[q, a, to:to + w], self.acc[q, of:of + w]).then_inc(self.s["kept"], 1)
        dve.wait_ge(self.s["kept"], 16)


class Mixer:

    FIRST_STEPS, SECOND_STEPS = 6, 5

    def __init__(self, k):
        self.k = k
        nc, C = k.nc, k.C
        self.s = {n: k.sem("mix_" + n) for n in (
            "q", "qmin", "qexp", "qf", "t", "var1", "ln1", "std1", "x1", "x1_turned", "x1T", "h", "hT", "y", "var2",
            "ln2", "std2", "res", "chain1", "chain2")}
        self.ins = [k.sem(f"mix_in{b}") for b in range(2)]
        self.x_in = [k.sem(f"mix_x_in{b}") for b in range(2)]
        self.stored = [k.sem(f"mix_stored{b}") for b in range(2)]
        take = k.carve(k.work)
        rows = lambda: take(C)[0:P]
        cols = lambda: take(2 * P).rearrange("p (a n) -> p a n", a=2)
        self.x, self.xn = [rows() for _ in range(2)], [rows() for _ in range(2)]
        self.xnT = [cols() for _ in range(2)]
        self.res = [rows() for _ in range(2)]
        self.qm, self.qf, self.x1T, self.hT = cols(), cols(), cols(), cols()
        self.r1, self.r2, self.x1 = rows(), rows(), rows()
        small = take(40)[0:P]
        self.den, self.rden = (small[:, 8 * i:8 * i + 8].rearrange("p (a h) -> p a h", a=2) for i in range(2))
        self.st = [small[:, 16 + 6 * i:22 + 6 * i] for i in range(2)]
        self.mv = [small[:, 28 + 2 * i:30 + 2 * i] for i in range(2)]
        self.rstd = [small[:, 32 + i:33 + i] for i in range(2)]
        self.scratch = small[0:1, 34:35]
        self.qb, self.tb, self.turnb, self.hb, self.yb = k.bank[2:7]

    def sync(self, sp):
        k = self.k

        def load(n, par):
            move_rows(sp, self.xn[par], k.tile_rows(k.d_xn, n), self.ins[par])
            sp.dma_start(self.xnT[par].rearrange("p a n -> p (a n)"),
                         k.d_xnT[ds(n, 1), :, :].rearrange("a p f -> (a p) f")).then_inc(self.ins[par], 16)

        def load_x(n, par):
            move_rows(sp, self.x[par], k.tile_rows(k.t["x"], n), self.x_in[par])

        def store(n, par):
            sp.wait_ge(self.s["res"], n + 1)
            move_rows(sp, k.tile_rows(k.d_xmix, n), self.res[par], self.stored[par])

        for b in range(2):
            load(b, b)
            load_x(b, b)
        k.load_experts(sp)
        sp.wait_ge(self.s["x1"], 1)
        load(2, 0)
        with sp.Fori(0, k.NT // 2 - 2) as i:
            for par in range(2):
                n = i * 2 + par
                sp.wait_ge(self.s["x1"], n + 2)
                load(n + 3, 1 - par)
                store(n, par)
                load_x(n + 2, par)
        for n in range(k.NT - 4, k.NT):
            if n == k.NT - 4:
                sp.wait_ge(self.s["x1"], n + 2)
                load(n + 3, 1)
            store(n, n % 2)
            if n < k.NT - 2:
                load_x(n + 2, n % 2)
        for par in range(2):
            sp.wait_ge(self.stored[par], 32 * (k.NT // 2) + 32)
        sp.wait_ge(k.W1_in, 48)

    def pe_start(self, pe):
        pass

    def dve_start(self, dve):
        for par in range(2):
            dve.sem_inc(self.stored[par], 32)

    def pe(self, pe, n, par, r, e):
        k, s, mm = self.k, self.s, self.k.nc.tensor.matmul
        first = not isinstance(n, int) or n < k.NT
        second = not isinstance(n, int) or n > 0
        if e == 0 and second:
            pe.wait_ge(s["x1T"], n)
            for a in range(2):
                for c in range(2):
                    last = mm(self.hb[:, a * P:(a + 1) * P], k.mW1[:, c, a * 128:(a + 1) * 128], self.x1T[:, c, :],
                              start=(c == 0), stop=(c == 1))
            last.then_inc(s["h"], 1)
        if e == 1 and first:
            pe.wait_ge(self.ins[par], (r + 1) * 48)
            for a in range(2):
                for c in range(2):
                    last = mm(self.qb[:, a * P:(a + 1) * P], k.Wqkv[:, c, a * 128:(a + 1) * 128], self.xnT[par][:, c, :],
                              start=(c == 0), stop=(c == 1))
            last.then_inc(s["q"], 1)
        if e == 5 and second:
            pe.wait_ge(s["hT"], n * 2)
            for c in range(2):
                last = mm(self.yb[0:P, 0:k.C], self.hT[:, c, :], k.mW2[:, c, :], start=(c == 0), stop=(c == 1))
            last.then_inc(s["y"], 1)
        if e == 7 and first:
            pe.wait_ge(s["qf"], n + 1)
            for a in range(2):
                last = mm(self.tb[0:P, a * 132:(a + 1) * 132], self.qf[:, a, :], k.kvbd[:, a, :], start=True, stop=True)
            last.then_inc(s["t"], 1)
        if e == 15 and first:
            pe.wait_ge(s["x1"], n + 1)
            for a in range(2):
                last = k.nc.tensor.transpose(self.turnb[:, a * P:(a + 1) * P], self.x1[:, a * 128:(a + 1) * 128],
                                             k.ident[0:P, 0:P])
            last.then_inc(s["x1_turned"], 1)

    def scalar(self, act):
        k, s, nc = self.k, self.s, self.k.nc

        def group(n, first=True, second=True):
            if second:
                nc.scalar.preload_act_table_set("gelu_and_others")
                act.wait_ge(s["h"], n)
                for a in range(2):
                    nc.scalar.activation(self.hT[:, a, :], self.hb[:, a * P:(a + 1) * P], ACT.Gelu,
                                         bias=k.mb1[:, a:a + 1]).then_inc(s["hT"], 1)
            nc.scalar.preload_act_table_set("natural_log_exp_and_others")
            if first:
                act.wait_ge(s["qmin"], n + 1)
                nc.scalar.activation(self.qm, self.qm, ACT.Exp).then_inc(s["qexp"], 1)
            if second:
                act.wait_ge(s["var2"], n)
                k.inverse_std(act, self.rstd[1], self.mv[1][:, 1:2], s["ln2"], n, s["std2"])
            if first:
                act.wait_ge(s["var1"], n + 1)
                k.inverse_std(act, self.rstd[0], self.mv[0][:, 1:2], s["ln1"], n + 1, s["std1"])
                act.wait_ge(s["x1_turned"], n + 1)
                nc.scalar.activation(self.x1T, self.turnb[:, 0:2 * P].rearrange("p (a n) -> p a n", a=2),
                                     ACT.Copy).then_inc(s["x1T"], 1)
        group(0, second=False)
        with act.Fori(1, k.NT) as n:
            group(n)
        group(k.NT, first=False)

    def dve(self, dve, n, par, r, e):
        k, s, nc, C = self.k, self.s, self.k.nc, self.k.C
        first = not isinstance(n, int) or n < k.NT
        second = not isinstance(n, int) or n > 0
        if e == 0:
            self.c1 = Steps(dve, s["chain1"], n * self.FIRST_STEPS, self.FIRST_STEPS)
            self.c2 = Steps(dve, s["chain2"], (n - 1) * self.SECOND_STEPS, self.SECOND_STEPS)
        both = lambda b, w: b.rearrange("p (a n) -> p a n", a=2)

        def stats(c, half, r, var):
            c.did(nc.vector.bn_stats(self.st[half], r))
            c.settle()
            nc.vector.memset(self.scratch, 0.0)
            nc.vector.bn_aggr(self.mv[half], self.st[half]).then_inc(s[var], 1)

        def centred(c, half, r, g):
            c.did(nc.vector.scalar_tensor_tensor(out=r, in0=r, scalar=self.mv[half][:, 0:1], in1=k.brow[g][:, :],
                                                 op0=ALU.subtract, op1=ALU.mult))

        if e == 3 and first:
            dve.wait_ge(s["q"], n + 1)
            nc.vector.tensor_scalar(self.qm, both(self.qb[:, 0:2 * P], P), 0.0, None, ALU.min).then_inc(s["qmin"], 1)
        if e == 6 and first:
            dve.wait_ge(s["qexp"], n + 1)
            nc.vector.scalar_tensor_tensor(out=self.qf, in0=both(self.qb[:, 0:2 * P], P), scalar=0.0, in1=self.qm,
                                           op0=ALU.max, op1=ALU.add).then_inc(s["qf"], 1)
        if e == 7 and second:
            dve.wait_ge(s["y"], n)
            self.c2.did(nc.vector.tensor_tensor(self.r2, self.yb[0:P, 0:C], self.x1, ALU.add))
            self.c2.settle()
        if e == 8 and second:
            self.c2.did(nc.vector.tensor_tensor(self.r2, self.r2, k.brow["mix_b2"][:, :], ALU.add))
            self.c2.settle()
            stats(self.c2, 1, self.r2, "var2")
        if e == 9 and first:
            dve.wait_ge(s["t"], n + 1)
            t = self.tb[0:P, 0:264].rearrange("p (a m) -> p a m", a=2)
            self.c1.did(nc.vector.tensor_scalar(self.den, t[:, :, 128:132], EPS_ATTN, None, ALU.add))
            self.c1.settle()
            self.c1.did(nc.vector.reciprocal(self.rden, self.den))
            self.c1.settle()
            self.c1.did(nc.vector.tensor_tensor(self.r1.rearrange("p (a h m) -> p a h m", a=2, h=4),
                                                t[:, :, 0:128].rearrange("p a (h m) -> p a h m", h=4),
                                                spread(self.rden, 3, 32), ALU.mult))
            self.c1.settle()
        if e == 10 and first:
            self.c1.did(nc.vector.tensor_tensor(self.r1, self.r1, self.xn[par], ALU.add))
            self.c1.settle()
            stats(self.c1, 0, self.r1, "var1")
        if e == 11:
            if second:
                dve.wait_ge(s["var2"], n)
                centred(self.c2, 1, self.r2, "ln2_g")
                self.c2.settle()
                dve.wait_ge(s["std2"], n)
                self.c2.did(nc.vector.scalar_tensor_tensor(out=self.r2, in0=self.r2, scalar=self.rstd[1],
                                                           in1=k.brow["ln2_b"][:, :], op0=ALU.mult, op1=ALU.add))
            if first:
                dve.wait_ge(s["var1"], n + 1)
                centred(self.c1, 0, self.r1, "ln1_g")
        if e == 12 and second:
            self.c2.settle()
            dve.wait_ge(self.x_in[1 - par], r * 32 + 32 * par)
            dve.wait_ge(self.stored[1 - par], r * 32 + 32 * par)
            nc.vector.tensor_tensor(self.res[1 - par], self.r2, self.x[1 - par], ALU.add).then_inc(s["res"], 1)
            self.c2.end()
        if e == 13 and first:
            self.c1.settle()
            dve.wait_ge(s["std1"], n + 1)
            nc.vector.scalar_tensor_tensor(out=self.x1, in0=self.r1, scalar=self.rstd[0], in1=k.brow["ln1_b"][:, :],
                                           op0=ALU.mult, op1=ALU.add).then_inc(s["x1"], 1)
            self.c1.end()

    def pe_end(self, pe):
        for e in range(self.k.EPT):
            self.pe(pe, self.k.NT, 0, self.k.NT // 2, e)

    def dve_end(self, dve):
        for e in range(self.k.EPT):
            self.dve(dve, self.k.NT, 0, self.k.NT // 2, e)


def run_layer(nc, t, out):
    with ExitStack() as ctx:
        k = Kernel(nc, ctx, t)
        k.allocate()
        k.setup()
        k.end_phase()
        k.project()
        k.scale_nodes()
        k.end_phase()
        k.aggregate("agg1", k.t_g1, KeyValueSums(k))
        k.end_phase()
        k.between()
        k.aggregate("agg2", k.t_g2, Mixer(k))
        k.end_phase()
        k.gate()
        k.route()
        k.scatter()
        k.end_phase()
        k.experts()
        k.combine(out)


_NAMES = {"x": "x", "src": "src", "dst": "dst", "gnn_W1": "L0_gnn_W1", "gnn_b1": "L0_gnn_b1", "gnn_W2": "L0_gnn_W2",
          "gnn_b2": "L0_gnn_b2", "mix_WqkvT": "L0_mix_Wqkv", "ln1_g": "L0_mix_ln1_g", "ln1_b": "L0_mix_ln1_b",
          "mix_W1T": "L0_mix_W1", "mix_b1": "L0_mix_b1", "mix_W2T": "L0_mix_W2", "mix_b2": "L0_mix_b2",
          "ln2_g": "L0_mix_ln2_g", "ln2_b": "L0_mix_ln2_b", "ffn_Wg": "L0_ffn_Wg", "ffn_bg": "L0_ffn_bg",
          "ffn_W1": "L0_ffn_W1", "ffn_b1": "L0_ffn_b1", "ffn_W2": "L0_ffn_W2", "ffn_b2": "L0_ffn_b2"}


def _laid_out(name, a):
    if name in ("mix_WqkvT", "mix_W1T", "mix_W2T"):
        return a.T
    if name == "mix_b1":
        return a.reshape(-1, 128).T
    if name == "ffn_W1":
        e, d, h = a.shape
        return a.reshape(e, d // 128, 128, h).transpose(2, 0, 1, 3)
    if name == "ffn_W2":
        e, h, d = a.shape
        return a.reshape(e, h // 128, 128, d).transpose(2, 0, 1, 3)
    if name == "ffn_b1":
        return a.reshape(a.shape[0], -1, 128).transpose(2, 0, 1)
    return a


def kernel(**inputs):
    import numpy as _np
    import concourse.bacc as _bacc
    from concourse.bass_utils import run_bass_kernel_spmd as _run

    nc = _bacc.Bacc("TRN2", target_bir_lowering=False, num_devices=1)
    arrays, t = {}, {}
    for name, given in _NAMES.items():
        a = _np.ascontiguousarray(_laid_out(name, _np.asarray(inputs[given])))
        arrays[f"in_{name}"] = a
        t[name] = nc.dram_tensor(f"in_{name}", a.shape, mybir.dt.from_np(a.dtype), kind="ExternalInput").ap()
    out = nc.dram_tensor("out_0", arrays["in_x"].shape, F32, kind="ExternalOutput").ap()
    run_layer(nc, t, out)
    r = _run(nc, [arrays], core_ids=[0])
    return r.results[0]["out_0"]
```

```python
from contextlib import ExitStack

import concourse.bass as bass
from concourse import mybir

F32 = mybir.dt.float32
BF16 = mybir.dt.bfloat16
I32 = mybir.dt.int32
ALU = mybir.AluOpType
ACT = mybir.ActivationFunctionType
AX = mybir.AxisListType
DVE_ONLY = (mybir.EngineType.DVE,)
PE_ONLY = (mybir.EngineType.PE,)
ds = bass.ds

P = 125
ROWS16 = 112
EPS_LN = 1e-5
EPS_ATTN = 1e-6


class Steps:

    def __init__(self, eng, sem, base, per_body):
        self.eng, self.sem, self.base, self.n, self.per_body = eng, sem, base, 0, per_body

    def did(self, ins):
        ins.then_inc(self.sem, 1)
        self.n += 1

    def settle(self):
        self.eng.wait_ge(self.sem, self.base + self.n)

    def end(self):
        assert self.per_body is None or self.n == self.per_body, (self.n, self.per_body)


def spread(ap, dim, n):
    ap = ap.unsqueeze(dim)
    return ap.broadcast_to(tuple(n if i == dim else d for i, d in enumerate(ap.shape)))


def row_pieces(dst, src):
    yield dst[0:ROWS16], src[0:ROWS16]
    yield dst[ROWS16:P], src[ROWS16:P]


def move_rows(eng, dst, src, sem):
    for d, s in row_pieces(dst, src):
        eng.dma_start(d, s).then_inc(sem, 16)


class Kernel:
    def __init__(self, nc, ctx, t):
        self.nc, self.ctx, self.t, self.phase_sems = nc, ctx, t, []
        self.N, self.C = t["x"].shape
        self.NT = self.N // P
        self.E = t["src"].shape[0]
        self.ET = self.E // P
        self.EPT = self.ET // self.NT
        self.F = t["gnn_W1"].shape[1]
        assert self.N == self.NT * P and self.ET == self.EPT * self.NT and self.NT % 4 == 0
        assert self.F == 128 and self.C == 256

    def sb(self, name, shape, dt=F32):
        return self.ctx.enter_context(self.nc.sbuf_tensor(name, shape, dt))

    def sem(self, name):
        self.phase_sems.append(self.nc.alloc_semaphore(name=name))
        return self.phase_sems[-1]

    def end_phase(self):
        self.nc.all_engine_barrier()
        self.nc.clear_and_free_semaphores(self.phase_sems)
        self.nc.all_engine_barrier()
        self.phase_sems = []

    def dram(self, name, shape, dt=F32):
        return self.nc.dram_tensor(name, shape, dt, kind="Internal").ap()

    def carve(self, flat):
        at = [0]

        def take(n):
            at[0] += n
            assert at[0] <= flat.shape[1], (at[0], flat.shape)
            return flat[:, at[0] - n:at[0]]
        return take

    def inverse_std(self, act, out, var, ln_done, count, done):
        self.nc.scalar.activation(out, var, ACT.Ln, bias=self.epsc[:, 0:1]).then_inc(ln_done, 1)
        act.wait_ge(ln_done, count)
        self.nc.scalar.activation(out, out, ACT.Exp, scale=-0.5).then_inc(done, 1)

    def pipeline(self, eng, stages, tiles, ring=2, last=None):
        deepest = max(lag for lag, _ in stages)
        first = -(-(deepest + ring) // ring) * ring
        last = tiles - tiles % ring if last is None else last

        def step(i, h):
            for lag, stage in stages:
                n = ring * i + h - lag if isinstance(i, int) else i * ring + (h - lag)
                if isinstance(n, int) and not 0 <= n < tiles:
                    continue
                stage(n, (h - lag) % ring, i + (h - lag) // ring)
        for k in range(first):
            step(k // ring, k % ring)
        with eng.Fori(first // ring, last // ring) as i:
            for h in range(ring):
                step(i, h)
        for k in range(last, tiles + deepest):
            step(k // ring, k % ring)

    def allocate(self):
        NT, ET, EPT, F, C = self.NT, self.ET, self.EPT, self.F, self.C
        self.bank = [self.ctx.enter_context(self.nc.psum_tensor(f"bank{i}", [128, 512], F32)) for i in range(8)]
        self.nodes1 = self.sb("nodes1", [128, NT * F])
        self.aggT = self.sb("aggT", [128, (NT + 1) * P])
        self.SLOTS = 2 * EPT
        self.rows_flat = self.sb("gathered_rows", [128, self.SLOTS * F])
        self.rows = self.rows_flat[0:P, :].rearrange("p (a f) -> p a f", f=F)
        self.srcT = self.sb("srcT", [P, ET], I32)
        self.dstT = self.sb("dstT", [P, ET])
        self.DPAD = 20
        self.winstart = self.sb("window_start", [1, NT * self.DPAD], I32)
        self.stray_count = self.sb("stray_count", [1, 4], I32)
        self.d_stray = self.dram("stray_dst", [P, ET])
        self.dinv = self.sb("dinv", [P, NT])
        self.ident = self.sb("ident", [128, 128])
        self.iota = self.sb("iota", [P, 128])
        self.ones = self.sb("ones", [128, 128])
        self.kvbd = self.sb("kv_blockdiag", [128, 2, 132])
        self.gW1 = self.sb("gnn_W1", [128, 2, F])
        self.Wqkv = self.sb("Wqkv", [128, 2, 3 * C])
        self.mW1 = self.sb("mix_W1", [128, 2, C])
        self.mW2 = self.sb("mix_W2", [128, 2, C])
        self.gW2 = self.sb("gnn_W2", [128, C])
        self.mb1 = self.sb("mix_b1", [128, 2])
        self.brow = {k: self.sb("row_" + k, [P, C]) for k in ("mix_b2", "ln1_g", "ln1_b", "ln2_g", "ln2_b", "gnn_b2")}
        self.gb1 = self.sb("gnn_b1", [P, F])
        NE, H = self.t["ffn_W1"].shape[1], self.t["ffn_W1"].shape[3]
        self.NE, self.H = NE, H
        self.Wg, self.bg = self.sb("ffn_Wg", [128, 2, NE]), self.sb("ffn_bg", [P, NE])
        self.slots = self.sb("slots", [P, 2, NT], I32)
        self.WE = 2 * H + H // 128
        self.W1e = self.nodes1[:, 0:NE * self.WE]
        self.b2e = self.nodes1[0:P, NE * self.WE:NE * (self.WE + C)]
        self.W2e = self.aggT[:, 0:NE * (H // 128) * C]
        self.W2_early = (NT // 2 * P) // (H // 128 * C)
        self.W2_in = self.sem("W2_in")
        self.gates = self.rows_flat[0:P, :][:, 0:NT * NE]
        self.W1s = [self.rows_flat[:, b * self.WE:(b + 1) * self.WE] for b in range(2)]
        self.W1_in = self.sem("W1_in")
        self.idx = [self.sb(f"idx{b}", [P, EPT], I32) for b in range(2)]
        self.onehot = [self.sb(f"onehot{b}", [P, EPT, P]) for b in range(2)]
        self.zeros = self.sb("zeros", [P, C])
        self.held = self.sb("held", [1, 2])
        self.zeros_made, self.slots_zeroed = self.sem("zeros_made"), self.sem("slots_zeroed")
        self.epsc = self.sb("eps_ln", [P, 1])
        self.work = self.sb("work", [128, 4200])
        self.t_g1 = self.dram("g1_table", [self.N, F])
        self.t_g2 = self.dram("g2_table", [self.N, F])
        self.d_xn = self.dram("xn_rows", [self.N, C])
        self.d_xnT = self.dram("xnT_tiles", [NT, 128, 2 * P])
        self.d_xmix = self.dram("xmix_rows", [self.N, C])
        self.d_x2 = self.dram("x2_rows", [self.N, C])
        self.d_xm = self.dram("xm_rows", [self.N, C])
        self.PARTS = 2
        self.NTP = NT // self.PARTS
        self.STP = 2 * self.NTP + NE
        assert self.NTP % 2 == 0 and self.STP % 4 == 0
        self.eid = self.sb("tile_expert", [1, self.PARTS * (self.STP // 2) * 4], I32)
        self.d_xs = [self.dram(f"expert_in_rows{k}", [self.STP * P, C]) for k in range(self.PARTS)]
        self.d_ys = [self.dram(f"expert_out_rows{k}", [self.STP * P, C]) for k in range(self.PARTS)]
        self.phase_sems = []

    def pair_rows(self, ap, n):
        return ap[ds(n * P, 2 * P), :].rearrange("(b p) c -> p b c", p=P)

    def tile_rows(self, ap, n):
        return ap[ds(n * P, P), :]

    def setup(self):
        nc, t, NT, ET, EPT = self.nc, self.t, self.NT, self.ET, self.EPT
        weights_in, raw_in = self.sem("weights_in"), self.sem("raw_in")
        made, idn = self.sem("constants_made"), self.sem("identity_made")
        floated, turned, taken = self.sem("raw_floated"), self.sem("blocks_turned"), self.sem("blocks_taken")
        starts_out, chain = self.sem("starts_spread"), self.sem("setup_chain")
        strays, counted, stray_out = self.sem("strays_found"), self.sem("strays_counted"), self.sem("strays_stored")
        NBLK = ET // 100
        raw = self.nodes1[0:100, 0:2 * NBLK * P].bitcast(I32).rearrange("p (a b e) -> p a b e", a=2, b=NBLK)
        flt = self.nodes1[0:100, 2 * NBLK * P:4 * NBLK * P].rearrange("p (a b e) -> p a b e", a=2, b=NBLK)
        take = self.carve(self.aggT)
        exact = lambda *shape: take(-(-shape[0] * shape[1] // 2))[0:P].bitcast(BF16)[:, 0:shape[0] * shape[1]]
        self.lo, self.hi = exact(NT, EPT), exact(NT, EPT)
        self.lo_is = exact(P, EPT).rearrange("p (m e) -> p m e", e=EPT)
        self.hi_is = exact(NT, EPT).rearrange("p (m e) -> p m e", e=EPT)
        self.ohl = [exact(P, EPT).rearrange("p (m e) -> p m e", e=EPT) for _ in range(2)]
        self.ohh = [exact(NT, EPT).rearrange("p (m e) -> p m e", e=EPT) for _ in range(2)]
        self.xnT = [take(2 * P).rearrange("p (k n) -> p k n", k=2) for _ in range(2)]
        self.zer = take(260)
        whole, tmp, found = take(ET)[0:P], take(ET)[0:P], take(1)[0:P]
        loads = [
            (self.gW1[:, :, :], t["gnn_W1"].rearrange("(k p) f -> p k f", p=128)),
            (self.Wqkv[:, :, :], t["mix_WqkvT"].rearrange("(k p) f -> p k f", p=128)),
            (self.mW1[:, :, :], t["mix_W1T"].rearrange("(k p) f -> p k f", p=128)),
            (self.mW2[:, :, :], t["mix_W2T"].rearrange("(k p) f -> p k f", p=128)),
            (self.gW2[:, :], t["gnn_W2"]),
            (self.mb1[:, :], t["mix_b1"]),
            (self.gb1[:, :], spread(t["gnn_b1"], 0, P)),
            (self.Wg[:, :, :], t["ffn_Wg"].rearrange("(k p) e -> p k e", p=128)),
            (self.bg[:, :], spread(t["ffn_bg"], 0, P)),
        ] + [(self.brow[k][:, :], spread(t[k], 0, P)) for k in self.brow]

        with nc.Block() as block:
            @block.sync
            def _(sp):
                for a, name in enumerate(("src", "dst")):
                    sp.dma_start(raw[:, a, :, :], t[name].rearrange("(b p e) -> p b e", p=100, e=P)).then_inc(raw_in, 16)
                for dst, src in loads:
                    sp.dma_start(dst, src).then_inc(weights_in, 16)
                sp.wait_ge(weights_in, 16 * len(loads))
                sp.wait_ge(strays, 5)
                sp.dma_start(self.d_stray, whole).then_inc(stray_out, 16)
                sp.wait_ge(stray_out, 16)

            @block.gpsimd
            def _(pool):
                nc.gpsimd.memset(self.ident[:, :], 0.0).then_inc(idn, 1)
                pool.wait_ge(idn, 1)
                nc.gpsimd.affine_select(out=self.ident[:, :], in_=self.ident[:, :], compare_op=ALU.not_equal, fill=1.0,
                                        base=0, pattern=[[-1, 128]], channel_multiplier=1).then_inc(idn, 1)
                nc.gpsimd.iota(self.iota[:, :], pattern=[[1, 128]], base=0, channel_multiplier=0,
                               allow_small_or_imprecise_dtypes=True).then_inc(made, 1)
                for out, m in ((self.lo_is, P), (self.hi_is, NT)):
                    nc.gpsimd.iota(out, pattern=[[1, m], [0, EPT]], base=0, channel_multiplier=0,
                                   allow_small_or_imprecise_dtypes=True).then_inc(made, 1)
                nc.gpsimd.memset(self.ones[:, :], 1.0).then_inc(made, 1)
                nc.gpsimd.memset(self.kvbd[:, :, :], 0.0).then_inc(made, 1)
                pool.wait_ge(idn, 2)
                nc.gpsimd.memset(self.held[:, :], 0.0).then_inc(made, 1)
                pool.wait_ge(made, 6)

            @block.tensor
            def _(pe):
                pe.wait_ge(idn, 2)
                pe.wait_ge(floated, 2)
                n = 0
                for a in range(2):
                    for b0 in range(0, NBLK, 4):
                        if n >= 4:
                            pe.wait_ge(taken, n - 3)
                        for b in range(b0, min(b0 + 4, NBLK)):
                            mm = nc.tensor.transpose(self.bank[n % 4][0:P, (b - b0) * 100:(b - b0 + 1) * 100],
                                                     flt[:, a, b, :], self.ident[0:100, 0:100])
                        mm.then_inc(turned, 1)
                        n += 1
                pe.wait_ge(made, 5)
                pe.wait_ge(taken, n)
                for c in range(4):
                    w = ET // 4
                    mm = nc.tensor.matmul(self.bank[4 + c][0:P, 0:w], self.ones[0:1, 0:P],
                                          self.dstT[0:1, c * w:(c + 1) * w], start=True, stop=True)
                    mm.then_inc(starts_out, 1)
                pe.wait_ge(strays, 5)
                nc.tensor.matmul(self.bank[0][0:1, 0:1], found, self.ones[0:P, 0:1], start=True,
                                 stop=True).then_inc(counted, 1)

            @block.vector
            def _(dve):
                dve.wait_ge(raw_in, 32)
                for a in range(2):
                    nc.vector.tensor_copy(flt[:, a, :, :], raw[:, a, :, :]).then_inc(floated, 1)
                n = 0
                for a, out in enumerate((self.srcT, self.dstT)):
                    for b0 in range(0, NBLK, 4):
                        k = min(4, NBLK - b0) * 100
                        dve.wait_ge(turned, n + 1)
                        nc.vector.tensor_copy(out[:, b0 * 100:b0 * 100 + k], self.bank[n % 4][0:P, 0:k]).then_inc(taken, 1)
                        n += 1
                dve.wait_ge(taken, n)
                c = Steps(dve, chain, 0, 8)
                c.did(nc.vector.tensor_scalar(tmp, self.dstT[:, :], 1.0 / P, 0.5 / P - 0.5, ALU.mult, ALU.add))
                c.settle()
                c.did(nc.vector.tensor_scalar(whole, tmp, 12582912.0, None, ALU.add))
                c.settle()
                c.did(nc.vector.tensor_scalar(tmp, whole, 12582912.0, None, ALU.subtract))
                c.settle()
                c.did(nc.vector.tensor_copy(self.hi, tmp))
                c.did(nc.vector.scalar_tensor_tensor(out=self.lo, in0=tmp, scalar=-float(P), in1=self.dstT[:, :],
                                                     op0=ALU.mult, op1=ALU.add))
                c.settle()
                c.did(nc.vector.tensor_copy(whole, self.dstT[:, :]))
                start = self.winstart[0:1, :].rearrange("a (n d) -> a n d", d=self.DPAD)
                c.did(nc.vector.memset(self.winstart[0:1, :], 0))
                c.settle()
                c.did(nc.vector.tensor_scalar(start[:, :, 0:EPT], self.dstT[0:1, :].rearrange("a (n e) -> a n e", e=EPT),
                                              0.0, float(self.N), ALU.max, ALU.min))
                c.settle()
                c.end()
                nc.vector.memset(self.epsc[:, :], EPS_LN).then_inc(taken, 1)
                nc.vector.memset(self.zeros[:, :], 0.0).then_inc(self.zeros_made, 1)
                dve.wait_ge(weights_in, 16 * len(loads))
                nc.vector.tensor_tensor(self.brow["ln2_b"][:, :], self.brow["ln2_b"][:, :], self.brow["gnn_b2"][:, :],
                                        ALU.add).then_inc(taken, 1)
                n += 2
                for k in range(4):
                    w = ET // 4
                    dve.wait_ge(starts_out, 4)
                    nc.vector.tensor_tensor(self.dstT[:, k * w:(k + 1) * w], self.dstT[:, k * w:(k + 1) * w],
                                            self.bank[4 + k][0:P, 0:w], ALU.subtract).then_inc(taken, 1)
                dve.wait_ge(taken, n + 4)
                v = Steps(dve, strays, 0, 5)
                v.did(nc.vector.tensor_scalar(tmp, self.dstT[:, :], 0.0, None, ALU.is_lt))
                v.settle()
                v.did(nc.vector.scalar_tensor_tensor(out=tmp, in0=self.dstT[:, :], scalar=P - 1.0, in1=tmp, op0=ALU.is_gt,
                                                     op1=ALU.add))
                v.settle()
                v.did(nc.vector.scalar_tensor_tensor(out=whole, in0=whole, scalar=1.0, in1=tmp, op0=ALU.add,
                                                     op1=ALU.mult))
                v.settle()
                v.did(nc.vector.tensor_scalar(whole, whole, 1.0, None, ALU.subtract))
                v.did(nc.vector.tensor_reduce(found, tmp, AX.X, ALU.add))
                v.end()
                nc.vector.memset(self.stray_count[:, :], 0).then_inc(counted, 1)
                dve.wait_ge(counted, 2)
                nc.vector.tensor_copy(self.stray_count[0:1, 0:1], self.bank[0][0:1, 0:1]).then_inc(counted, 1)
                dve.wait_ge(counted, 3)

    def project(self):
        nc, t, NT, EPT, F, C = self.nc, self.t, self.NT, self.EPT, self.F, self.C
        s = {k: self.sem("p1_" + k) for k in (
            "stats", "var", "ln", "rstd", "scaled", "shift", "xn", "xn_turned", "xnT", "h", "h1", "hot", "hist",
            "zeroed", "counted")}
        RX = 8
        x_in, xn_st = ([self.sem(f"p1_{k}{b}") for b in range(RX // 2)] for k in ("x_in", "xn_stored"))
        xT_st = [self.sem(f"p1_xnT_stored{b}") for b in range(2)]
        take = self.carve(self.work)
        xb2, xn2 = ([take(2 * C)[0:P].rearrange("p (b c) -> p b c", c=C) for _ in range(RX // 2)] for _ in range(2))
        xb, xn = ([buf[b // 2][:, b % 2, :] for b in range(RX)] for buf in (xb2, xn2))
        small = take(40)[0:P]
        st = [small[:, 8 * b:8 * b + 6] for b in range(2)]
        mv = [small[:, 16 + 4 * b:18 + 4 * b] for b in range(2)]
        rstd, scaled, shift = ([small[:, 24 + 2 * a + b:25 + 2 * a + b] for b in range(2)] for a in range(3))
        xnT, zer, ohl, ohh = self.xnT, self.zer, self.ohl, self.ohh
        turn, hbank, hist = self.bank[0:2], self.bank[2:4], self.bank[4]

        with nc.Block() as block:
            @block.sync
            def _(sp):
                def load(n, slot, r):
                    if slot % 2 == 0:
                        if not isinstance(n, int) or n >= RX:
                            sp.wait_ge(s["xn"], n - (RX - 2))
                        move_rows(sp, xb2[slot // 2], self.pair_rows(t["x"], n), x_in[slot // 2])

                def store(n, slot, r):
                    if slot % 2 == 0:
                        sp.wait_ge(s["xn"], n + 2)
                        move_rows(sp, self.pair_rows(self.d_xn, n), xn2[slot // 2], xn_st[slot // 2])

                def store_turned(n, slot, r):
                    sp.wait_ge(s["xnT"], n + 1)
                    sp.dma_start(self.d_xnT[ds(n, 1), :, :].rearrange("a p f -> (a p) f"),
                                 xnT[slot % 2].rearrange("p k n -> p (k n)")).then_inc(xT_st[slot % 2], 16)

                self.pipeline(sp, [(0, load), (5, store), (5, store_turned)], NT, RX)
                for b in range(RX // 2):
                    sp.wait_ge(xn_st[b], 32 * len(range(2 * b, NT, RX)))
                for par in range(2):
                    sp.wait_ge(xT_st[par], 16 * (NT // 2))

            @block.vector
            def _(dve):
                nc.vector.memset(zer, 0.0).then_inc(s["zeroed"], 1)
                dve.sem_inc(s["hist"], 2)

                def stats(n, slot, r):
                    par = slot % 2
                    dve.wait_ge(x_in[slot // 2], r * 32 + 32)
                    nc.vector.bn_stats(st[par], xb[slot]).then_inc(s["stats"], 1)
                    dve.wait_ge(s["hist"], n + 1)
                    nc.vector.tensor_tensor(ohl[par], spread(self.lo[:, ds(n * EPT, EPT)], 1, P), self.lo_is,
                                            ALU.is_equal).then_inc(s["hot"], 1)
                    dve.wait_ge(s["stats"], n + 1)
                    nc.vector.tensor_tensor(ohh[par], spread(self.hi[:, ds(n * EPT, EPT)], 1, NT), self.hi_is,
                                            ALU.is_equal).then_inc(s["hot"], 1)
                    if not isinstance(n, int) or n > 1:
                        dve.wait_ge(s["scaled"], n - 1)
                        nc.vector.memset(small[0:1, 32:33], 0.0)
                    nc.vector.bn_aggr(mv[par], st[par]).then_inc(s["var"], 1)

                self.pipeline(dve, [(0, stats)], NT, RX)
                dve.wait_ge(s["hist"], NT + 2)
                nc.vector.tensor_scalar(self.dinv[:, :], hist[0:P, 0:NT], 1.0, None, ALU.add).then_inc(s["counted"], 1)
                dve.wait_ge(s["counted"], 1)

            @block.gpsimd
            def _(pool):
                def shift_of(n, par, r):
                    pool.wait_ge(s["rstd"], n + 1)
                    nc.gpsimd.tensor_tensor(scaled[par], mv[par][:, 0:1], rstd[par], ALU.mult).then_inc(s["scaled"], 1)
                    pool.wait_ge(s["scaled"], n + 1)
                    if not isinstance(n, int) or n > 1:
                        pool.wait_ge(s["xn"], n - 1)
                    nc.gpsimd.tensor_tensor(shift[par], self.zeros[:, 0:1], scaled[par],
                                            ALU.subtract).then_inc(s["shift"], 1)
                self.pipeline(pool, [(0, shift_of)], NT)

            @block.tensor
            def _(pe):
                pe.wait_ge(s["zeroed"], 1)
                nc.tensor.matmul(hist[0:P, 0:NT], zer[:, 0:P], zer[:, 0:NT], start=True, stop=False, skip_group_check=True)

                def turned(n, slot, r):
                    par = slot % 2
                    pe.wait_ge(s["xn"], n + 1)
                    for k in range(2):
                        mm = nc.tensor.transpose(turn[par][:, k * P:(k + 1) * P], xn[slot][:, k * 128:(k + 1) * 128],
                                                 self.ident[0:P, 0:P])
                    mm.then_inc(s["xn_turned"], 1)

                def counts(n, slot, r):
                    par = slot % 2
                    pe.wait_ge(s["hot"], n * 2 + 2)
                    for e in range(EPT):
                        mm = nc.tensor.matmul(hist[0:P, 0:NT], ohl[par][:, :, e], ohh[par][:, :, e], start=False,
                                              stop=False, skip_group_check=True)
                    mm.then_inc(s["hist"], 1)

                def h1(n, slot, r):
                    par = slot % 2
                    pe.wait_ge(s["xnT"], n + 1)
                    for k in range(2):
                        mm = nc.tensor.matmul(hbank[par][0:P, 0:F], xnT[par][:, k, :], self.gW1[:, k, :],
                                              start=(k == 0), stop=(k == 1))
                    mm.then_inc(s["h"], 1)

                self.pipeline(pe, [(0, counts), (1, turned), (2, h1)], NT, RX)

            @block.scalar
            def _(act):
                nc.scalar.preload_act_table_set("natural_log_exp_and_others")

                def inverse(n, slot, r):
                    par = slot % 2
                    act.wait_ge(s["var"], n + 1)
                    if not isinstance(n, int) or n > 1:
                        act.wait_ge(s["xn"], n - 1)
                    self.inverse_std(act, rstd[par], mv[par][:, 1:2], s["ln"], n + 1, s["rstd"])

                def norm(n, slot, r):
                    par = slot % 2
                    act.wait_ge(s["shift"], n + 1)
                    act.wait_ge(s["rstd"], n + 1)
                    act.wait_ge(x_in[slot // 2], r * 32 + 32)
                    if not isinstance(n, int) or n >= RX:
                        act.wait_ge(s["xn_turned"], n - (RX - 1))
                        act.wait_ge(xn_st[slot // 2], r * 32)
                    nc.scalar.activation(xn[slot], xb[slot], ACT.Identity, scale=rstd[par],
                                         bias=shift[par]).then_inc(s["xn"], 1)

                def keep_turned(n, slot, r):
                    par = slot % 2
                    act.wait_ge(s["xn_turned"], n + 1)
                    if not isinstance(n, int) or n > 1:
                        act.wait_ge(xT_st[par], (r * (RX // 2) + slot // 2) * 16)
                        act.wait_ge(s["h"], n - 1)
                    nc.scalar.activation(xnT[par], turn[par][:, 0:2 * P].rearrange("p (k n) -> p k n", k=2),
                                         ACT.Copy).then_inc(s["xnT"], 1)

                def keep_h1(n, slot, r):
                    par = slot % 2
                    act.wait_ge(s["h"], n + 1)
                    nc.scalar.activation(self.nodes1[0:P, ds(n * F, F)], hbank[par][0:P, 0:F], ACT.Copy).then_inc(s["h1"], 1)

                self.pipeline(act, [(0, inverse), (1, norm), (2, keep_turned), (3, keep_h1)], NT, RX)
                act.wait_ge(s["h1"], NT)

    def scale_nodes(self):
        nc, NT, F = self.nc, self.NT, self.F
        dinv_made, cleared, scaled, stored = (self.sem(n) for n in ("dinv_made", "aggT_cleared", "g1_scaled", "g1_stored"))
        CH = 10
        W = NT // CH
        g1 = self.nodes1[0:P, :].rearrange("p (n f) -> p n f", f=F)
        table = self.t_g1.rearrange("(n p) f -> p n f", p=P)

        def scale(eng, c):
            w = slice(c * W, (c + 1) * W)
            eng.tensor_tensor(g1[:, w, :], g1[:, w, :], spread(self.dinv[:, w], 2, F),
                              ALU.mult).then_inc(scaled, 1)

        with nc.Block() as block:
            @block.gpsimd
            def _(pool):
                nc.gpsimd.memset(self.aggT[:, :], 0.0).then_inc(cleared, 1)
                pool.wait_ge(cleared, 1)

            @block.scalar
            def _(act):
                nc.scalar.activation(self.dinv[:, :], self.dinv[:, :], ACT.Sqrt).then_inc(dinv_made, 1)

            @block.vector
            def _(dve):
                dve.wait_ge(dinv_made, 1)
                nc.vector.reciprocal(self.dinv[:, :], self.dinv[:, :]).then_inc(dinv_made, 1)
                dve.wait_ge(dinv_made, 2)
                for c in range(CH):
                    scale(nc.vector, c)

            @block.sync
            def _(sp):
                for c in range(CH):
                    w = slice(c * W, (c + 1) * W)
                    sp.wait_ge(scaled, c + 1)
                    for a, b in ((0, ROWS16), (ROWS16, P)):
                        sp.dma_start(table[a:b, w, :], g1[a:b, w, :]).then_inc(stored, 16)
                sp.wait_ge(stored, 32 * CH)

    def aggregate(self, name, table, beside=None):
        nc, NT, EPT = self.nc, self.NT, self.EPT
        SL, WB = self.SLOTS, 2
        idx, onehot, window = self.idx, self.onehot, self.bank[0:WB]
        got = [self.sem(f"{name}_row{k}") for k in range(SL)]
        indexed, held, hot, summed, added = (self.sem(f"{name}_{k}") for k in (
            "indexed", "held", "hot", "summed", "added"))

        with self.nc.Block() as block:
            @block.gpsimd
            def _(pool):
                with pool.Fori(0, NT // 2) as i:
                    for par in range(2):
                        n = i * 2 + par
                        pool.wait_ge(indexed, n + 1)
                        pool.wait_ge(held, n + 1)
                        nc.gpsimd.tensor_tensor(self.held[:, 0:1], self.held[:, 1:2], self.held[:, 1:2],
                                                ALU.add).then_inc(held, 1)
                        for e in range(EPT):
                            k = par * EPT + e
                            nc.gpsimd.indirect_dma_start(
                                self.rows[:, k, :], None, table,
                                bass.IndirectOffsetOnAxis(ap=idx[par][:, e:e + 1], axis=0)).then_inc(got[k], 16)

            @block.tensor
            def _(pe):
                if beside:
                    beside.pe_start(pe)

                def pair(i):
                    for par in range(2):
                        n = i * 2 + par
                        pe.wait_ge(hot, n + 1)
                        for e in range(EPT):
                            k = par * EPT + e
                            pe.wait_ge(got[k], (i + 1) * 16)
                            pe.wait_ge(added, n * EPT + (e + 1))
                            nc.tensor.matmul(window[k % WB][:, 0:P], self.rows[:, k, :], onehot[par][:, e, :],
                                             start=True, stop=True).then_inc(summed, 1)
                            if beside:
                                beside.pe(pe, n, par, i, e)
                pair(0)
                with pe.Fori(1, NT // 2) as i:
                    pair(i)
                if beside:
                    beside.pe_end(pe)

            @block.vector
            def _(dve):
                dve.sem_inc(held, 1)
                dve.sem_inc(summed, SL)
                dve.sem_inc(added, WB)

                def hots(n, par):
                    nc.vector.tensor_tensor(onehot[par][:, :, :], spread(self.iota[:, 0:P], 1, EPT),
                                            spread(self.dstT[:, ds(n * EPT, EPT)], 2, P),
                                            ALU.is_equal).then_inc(hot, 1)

                def indices(n, par):
                    nc.vector.tensor_copy(idx[par][:, :], self.srcT[:, ds(n * EPT, EPT)]).then_inc(indexed, 1)

                def group(n, par, r, more):
                    _, starts = nc.values_load_multi_w_load_instructions(
                        self.winstart[0:1, ds(n * self.DPAD, self.DPAD)], engines=DVE_ONLY, min_val=0, max_val=self.N,
                        skip_runtime_bounds_check_because="clamped to [0, N] when made")
                    if more:
                        dve.wait_ge(summed, n * EPT + SL)
                        indices(n + 1, 1 - par)
                        hots(n + 1, 1 - par)
                    for e in range(EPT):
                        k = par * EPT + e
                        dve.wait_ge(summed, n * EPT + (e + 1 + SL))
                        dve.wait_ge(added, n * EPT + (e + WB))
                        at = self.aggT[:, ds(starts[e], P)]
                        nc.vector.tensor_tensor(at, at, window[k % WB][:, 0:P], ALU.add).then_inc(added, 1)
                        if beside:
                            beside.dve(dve, n, par, r, e)

                if beside:
                    beside.dve_start(dve)
                indices(0, 0)
                hots(0, 0)
                group(0, 0, 0, True)
                group(1, 1, 0, True)
                with dve.Fori(1, NT // 2 - 1) as i:
                    group(i * 2, 0, i, True)
                    group(i * 2 + 1, 1, i, True)
                group(NT - 2, 0, NT // 2 - 1, True)
                group(NT - 1, 1, NT // 2 - 1, False)
                dve.wait_ge(added, self.ET + WB)
                if beside:
                    beside.dve_end(dve)

            if beside:
                @block.sync
                def _(sp):
                    beside.sync(sp)

                @block.scalar
                def _(act):
                    beside.scalar(act)

    def strays(self, name, table):
        nc, NT, ET = self.nc, self.NT, self.ET
        W = 4 * P
        NQ = NT // 4
        hot_flat, dst = (self.onehot[b][:, :, :].rearrange("p a b -> p (a b)") for b in range(2))
        take = self.carve(hot_flat)
        hot, column, rel = take(W), take(W), take(1)
        dst_in, ready, row, indexed, chain, hots, summed, added = (self.sem(f"{name}_{k}") for k in (
            "dst_in", "columns", "row", "indexed", "chain", "hot", "summed", "added"))

        def if_any(eng, engine):
            count = nc.values_load_multi_w_load_instructions(
                self.stray_count[0:1, 0:4], engines=(engine,), min_val=0, max_val=self.E,
                skip_runtime_bounds_check_because="a count of edges")[1][0]
            return eng.If(count > 0)

        with nc.Block() as block:
            @block.sync
            def _(sp):
                with if_any(sp, mybir.EngineType.SP):
                    sp.dma_start(dst[:, 0:ET], self.d_stray).then_inc(dst_in, 16)
                    sp.wait_ge(dst_in, 16)

            @block.gpsimd
            def _(pool):
                with if_any(pool, mybir.EngineType.Pool):
                    nc.gpsimd.iota(column, pattern=[[1, W]], base=0, channel_multiplier=0,
                                   allow_small_or_imprecise_dtypes=True).then_inc(ready, 1)
                    with pool.Fori(0, ET) as j:
                        pool.wait_ge(summed, j * NQ + 1)
                        nc.gpsimd.tensor_copy(self.idx[0][:, 0:1], self.srcT[:, ds(j, 1)]).then_inc(indexed, 1)
                        pool.wait_ge(indexed, j * 2 + 1)
                        nc.gpsimd.tensor_tensor(self.held[:, 0:1], self.held[:, 1:2], self.held[:, 1:2],
                                                ALU.add).then_inc(indexed, 1)
                        nc.gpsimd.indirect_dma_start(
                            self.rows[:, 0, :], None, table,
                            bass.IndirectOffsetOnAxis(ap=self.idx[0][:, 0:1], axis=0)).then_inc(row, 16)

            @block.tensor
            def _(pe):
                with if_any(pe, mybir.EngineType.PE):
                    with pe.Fori(0, ET) as j:
                        with pe.Fori(0, NQ) as q:
                            pe.wait_ge(row, j * 16 + 16)
                            pe.wait_ge(hots, j * NQ + q + 1)
                            nc.tensor.matmul(self.bank[0][:, 0:W], self.rows[:, 0, :], hot, start=True,
                                             stop=True).then_inc(summed, 1)

            @block.vector
            def _(dve):
                for sem in (summed, chain, added):
                    dve.sem_inc(sem, 1)
                with if_any(dve, mybir.EngineType.DVE):
                    dve.wait_ge(dst_in, 16)
                    dve.wait_ge(ready, 1)
                    with dve.Fori(0, ET) as j:
                        dve.wait_ge(chain, j * (NQ + 1) + 1)
                        nc.vector.tensor_copy(rel, dst[:, ds(j, 1)]).then_inc(chain, 1)
                        with dve.Fori(0, NQ) as q:
                            n = j * NQ + q
                            dve.wait_ge(chain, n + j + 2)
                            nc.vector.tensor_tensor(hot, column, rel.broadcast_to((P, W)), ALU.is_equal).then_inc(hots, 1)
                            dve.wait_ge(hots, n + 1)
                            nc.vector.tensor_scalar(rel, rel, float(W), None, ALU.subtract).then_inc(chain, 1)
                            dve.wait_ge(summed, n + 2)
                            dve.wait_ge(added, n + 1)
                            at = self.aggT[:, ds(q * W, W)]
                            nc.vector.tensor_tensor(at, at, self.bank[0][:, 0:W], ALU.add).then_inc(added, 1)

    def load_experts(self, sp, step):
        t, NE, H = self.t, self.NE, self.H
        W = self.W1e.rearrange("p (e w) -> p e w", e=NE)
        e = slice(step * NE // 4, (step + 1) * NE // 4)
        sp.dma_start(W[:, e, 0:2 * H], t["ffn_W1"][:, e, :, :].rearrange("p e k h -> p e (k h)")).then_inc(self.W1_in, 16)
        if step == 3:
            sp.dma_start(W[:, :, 2 * H:self.WE], t["ffn_b1"]).then_inc(self.W1_in, 16)
            sp.dma_start(self.b2e, spread(t["ffn_b2"].rearrange("e c -> (e c)"), 0, P)).then_inc(self.W1_in, 16)

    def load_W2(self, sp, e0, e1):
        w = self.H // 128 * self.C
        sp.dma_start(self.W2e[:, e0 * w:e1 * w], self.t["ffn_W2"].rearrange("p e c d -> p (e c d)")[:, e0 * w:e1 * w])\
            .then_inc(self.W2_in, 16)

    def zero_slots(self, sp, part, first, tiles):
        rows = self.d_xs[part][ds(first * P, tiles * P), :].rearrange("(j p) c -> p j c", p=P)
        sp.dma_start(rows, spread(self.zeros[0:P, :], 1, tiles)).then_inc(self.slots_zeroed, 16)

    def between(self):
        nc, NT, F = self.nc, self.NT, self.F
        G = 4
        joined, biased, ready, turned, kept, brought = (self.sem("p3_" + k) for k in (
            "joined", "biased", "ready", "turned", "kept", "brought"))
        stored = [self.sem(f"p3_stored{b}") for b in range(2)]
        flat = self.rows_flat[0:P, :]
        a1 = [flat[:, b * G * F:(b + 1) * G * F].rearrange("p (g f) -> p g f", g=G) for b in range(2)]
        g2 = [flat[:, (2 + b) * G * F:(3 + b) * G * F].rearrange("p (g f) -> p g f", g=G) for b in range(2)]
        take = self.carve(self.work)
        agg = [take(G * P) for _ in range(2)]
        table = self.t_g2.rearrange("(n p) f -> p n f", p=P)
        NG = NT // G
        sums, turns = self.bank[0:2], self.bank[2:4]

        def over(eng, A, B):
            A(0, 0, 0)
            with eng.Fori(0, (NG - 1) // 2) as i:
                A(i * 2 + 1, 1, i)
                B(i * 2, 0, i)
                A(i * 2 + 2, 0, i + 1)
                B(i * 2 + 1, 1, i)
            B(NG - 1, 0, (NG - 1) // 2)

        with nc.Block() as block:
            @block.tensor
            def _(pe):
                def A(g, par, r):
                    pe.wait_ge(biased, g + 1)
                    pe.wait_ge(brought, g + 1)
                    for k in range(G):
                        nc.tensor.matmul(sums[par][0:P, k * F:(k + 1) * F], agg[par][:, k * P:(k + 1) * P],
                                         self.ident[:, :], start=True, stop=False, skip_group_check=True)
                        mm = nc.tensor.matmul(sums[par][0:P, k * F:(k + 1) * F], self.ident[0:P, 0:P],
                                              self.nodes1[0:P, ds((g * G + k) * F, F)], start=False, stop=True,
                                              skip_group_check=True)
                    mm.then_inc(joined, 1)

                def B(g, par, r):
                    pe.wait_ge(ready, g + 1)
                    pe.wait_ge(kept, g + 1)
                    for k in range(G):
                        mm = nc.tensor.transpose(turns[par][:, k * P:(k + 1) * P], g2[par][:, k, :], self.ident[0:P, 0:P])
                    mm.then_inc(turned, 1)
                over(pe, A, B)

            @block.vector
            def _(dve):
                dve.sem_inc(biased, 2)
                dve.sem_inc(kept, 2)

                def group(g, par, r, first):
                    d = spread(self.dinv[:, ds(g * G, G)], 2, F)
                    dve.wait_ge(joined, g + 1)
                    for k in range(G):
                        ins = nc.vector.scalar_tensor_tensor(
                            out=a1[par][:, k, :], in0=sums[par][0:P, k * F:(k + 1) * F],
                            scalar=self.dinv[:, ds(g * G + k, 1)], in1=self.gb1[:, :], op0=ALU.mult, op1=ALU.add)
                    ins.then_inc(biased, 1)
                    dve.wait_ge(biased, g + 3)
                    if not first:
                        dve.wait_ge(stored[par], r * 32)
                        dve.wait_ge(turned, g - 1)
                    nc.vector.scalar_tensor_tensor(out=g2[par], in0=a1[par], scalar=0.0, in1=d, op0=ALU.max,
                                                   op1=ALU.mult).then_inc(ready, 1)
                group(0, 0, 0, True)
                group(1, 1, 0, True)
                with dve.Fori(1, (NG - 1) // 2) as i:
                    group(i * 2, 0, i, False)
                    group(i * 2 + 1, 1, i, False)
                group(NG - 1, 0, (NG - 1) // 2, False)

            @block.scalar
            def _(act):
                def bring(g, par, r):
                    if not isinstance(g, int) or g > 1:
                        act.wait_ge(joined, g - 1)
                    nc.scalar.activation(agg[par], self.aggT[:, ds(g * (G * P), G * P)], ACT.Copy).then_inc(brought, 1)

                def keep(g, par, r):
                    act.wait_ge(turned, g + 1)
                    act.wait_ge(brought, g + 1)
                    nc.scalar.activation(self.aggT[:, ds(g * (G * P), G * P)], turns[par][:, 0:G * P],
                                         ACT.Copy).then_inc(kept, 1)
                self.pipeline(act, [(0, bring), (2, keep)], NG)
                act.wait_ge(kept, NG + 2)

            @block.sync
            def _(sp):
                def store(g, par):
                    sp.wait_ge(ready, g + 1)
                    for a, b in ((0, ROWS16), (ROWS16, P)):
                        sp.dma_start(table[a:b, ds(g * G, G), :], g2[par][a:b, :, :]).then_inc(stored[par], 16)
                with sp.Fori(0, (NG - 1) // 2) as i:
                    for par in range(2):
                        store(i * 2 + par, par)
                store(NG - 1, 0)
                sp.wait_ge(stored[0], 32 * ((NG + 1) // 2))
                sp.wait_ge(stored[1], 32 * (NG // 2))


    def gate(self, part, mover=None):
        nc, NT, C, NE = self.nc, self.NTP, self.C, self.NE
        n0 = part * NT
        s = {k: self.sem(f"p5_{part}_{k}") for k in (
            "brought", "gnn", "x2", "stats", "var", "ln", "rstd", "xm", "xm_turned", "xmT", "score", "scored")}
        RX = 8
        x_in, x2_st, xm_st = ([self.sem(f"p5_{part}_{k}{b}") for b in range(RX // 2)] for k in (
            "x_in", "x2_stored", "xm_stored"))
        take = self.carve(self.work)
        spare = [self.carve(self.onehot[b][:, :, :].rearrange("p a b -> p (a b)")) for b in range(2)]
        xb2, x22, xm2 = ([piece(2 * C)[0:P].rearrange("p (b c) -> p b c", c=C) for _ in range(RX // 2)]
                         for piece in (take, spare[0], spare[1]))
        xb, x2, xm = ([buf[b // 2][:, b % 2, :] for b in range(RX)] for buf in (xb2, x22, xm2))
        agg = [take(P) for _ in range(2)]
        xmT = [take(2 * P).rearrange("p (k n) -> p k n", k=2) for _ in range(2)]
        small = take(48)[0:P]
        RS = 4
        st = [small[:, 8 * b:8 * b + 6] for b in range(RS)]
        mv = [small[:, 32 + 2 * b:34 + 2 * b] for b in range(RS)]
        rstd = [small[:, 40 + b:41 + b] for b in range(RS)]
        scratch = small[0:1, 44:45]
        gbank, turn, sbank = self.bank[0:2], self.bank[2:4], self.bank[4:6]

        with nc.Block() as block:
            @block.sync
            def _(sp):
                if mover:
                    self.load_W2(sp, 0, self.W2_early)
                def load(n, slot, r):
                    if slot % 2 == 0:
                        if not isinstance(n, int) or n >= RX:
                            sp.wait_ge(s["x2"], n - (RX - 2))
                        move_rows(sp, xb2[slot // 2], self.pair_rows(self.d_xmix, n + n0), x_in[slot // 2])

                def store(n, slot, r):
                    if slot % 2 == 0:
                        sp.wait_ge(s["x2"], n + 2)
                        move_rows(sp, self.pair_rows(self.d_x2, n + n0), x22[slot // 2], x2_st[slot // 2])
                        sp.wait_ge(s["xm"], n + 2)
                        move_rows(sp, self.pair_rows(self.d_xm, n + n0), xm2[slot // 2], xm_st[slot // 2])

                beside = mover.sync_stages(2, RX) if mover else []
                self.pipeline(sp, beside + [(0, load), (5, store)], NT, RX)
                for b in range(RX // 2):
                    stores = len(range(2 * b, NT, RX))
                    sp.wait_ge(x2_st[b], 32 * stores)
                    sp.wait_ge(xm_st[b], 32 * stores)
                if mover:
                    mover.sync_end(sp)
                    sp.wait_ge(self.W2_in, 16)

            if mover:
                @block.gpsimd
                def _(pool):
                    mover.gpsimd(pool)

            @block.scalar
            def _(act):
                nc.scalar.preload_act_table_set("natural_log_exp_and_others")

                def bring(n, slot, r):
                    par = slot % 2
                    if not isinstance(n, int) or n > 1:
                        act.wait_ge(s["gnn"], n - 1)
                    nc.scalar.activation(agg[par], self.aggT[:, ds((n + n0) * P, P)], ACT.Copy).then_inc(s["brought"], 1)

                def inverse(n, slot, r):
                    act.wait_ge(s["var"], n + 1)
                    self.inverse_std(act, rstd[slot], mv[slot][:, 1:2], s["ln"], n + 1, s["rstd"])

                def keep_turned(n, slot, r):
                    par = slot % 2
                    act.wait_ge(s["xm_turned"], n + 1)
                    if not isinstance(n, int) or n > 1:
                        act.wait_ge(s["score"], n - 1)
                    nc.scalar.activation(xmT[par], turn[par][:, 0:2 * P].rearrange("p (k n) -> p k n", k=2),
                                         ACT.Copy).then_inc(s["xmT"], 1)
                self.pipeline(act, [(0, bring), (2, inverse), (5, keep_turned)], NT, RS)

            @block.tensor
            def _(pe):
                def gnn(n, slot, r):
                    par = slot % 2
                    pe.wait_ge(s["brought"], n + 1)
                    if not isinstance(n, int) or n > 1:
                        pe.wait_ge(s["x2"], n - 1)
                    nc.tensor.matmul(gbank[par][0:P, 0:C], agg[par], self.gW2[:, :], start=True,
                                     stop=True).then_inc(s["gnn"], 1)

                def turned(n, slot, r):
                    par = slot % 2
                    pe.wait_ge(s["xm"], n + 1)
                    if not isinstance(n, int) or n > 1:
                        pe.wait_ge(s["xmT"], n - 1)
                    for k in range(2):
                        mm = nc.tensor.transpose(turn[par][:, k * P:(k + 1) * P], xm[slot][:, k * 128:(k + 1) * 128],
                                                 self.ident[0:P, 0:P])
                    mm.then_inc(s["xm_turned"], 1)

                def score(n, slot, r):
                    par = slot % 2
                    pe.wait_ge(s["xmT"], n + 1)
                    if not isinstance(n, int) or n > 1:
                        pe.wait_ge(s["scored"], n - 1)
                    for k in range(2):
                        mm = nc.tensor.matmul(sbank[par][0:P, 0:NE], xmT[par][:, k, :], self.Wg[:, k, :],
                                              start=(k == 0), stop=(k == 1))
                    mm.then_inc(s["score"], 1)
                self.pipeline(pe, [(0, gnn), (4, turned), (6, score)], NT, RX)

            @block.vector
            def _(dve):
                def x2_stats(n, slot, r):
                    par = slot % 2
                    dve.wait_ge(x_in[slot // 2], r * 32 + 32)
                    if not isinstance(n, int) or n >= RX:
                        dve.wait_ge(x2_st[slot // 2], r * 32)
                        dve.wait_ge(s["xm"], n - (RX - 1))
                    dve.wait_ge(s["gnn"], n + 1)
                    nc.vector.scalar_tensor_tensor(out=x2[slot], in0=gbank[par][0:P, 0:C], scalar=self.dinv[:, ds(n + n0, 1)],
                                                   in1=xb[slot], op0=ALU.mult, op1=ALU.add).then_inc(s["x2"], 1)
                    dve.wait_ge(s["x2"], n + 1)
                    nc.vector.bn_stats(st[slot % RS], x2[slot]).then_inc(s["stats"], 1)
                    if not isinstance(n, int) or n >= RS:
                        dve.wait_ge(s["xm"], n - (RS - 1))
                    dve.wait_ge(s["stats"], n + 1)
                    nc.vector.memset(scratch, 0.0)
                    nc.vector.bn_aggr(mv[slot % RS], st[slot % RS]).then_inc(s["var"], 1)

                def norm(n, slot, r):
                    dve.wait_ge(s["rstd"], n + 1)
                    if not isinstance(n, int) or n >= RX:
                        dve.wait_ge(s["xm_turned"], n - (RX - 1))
                        dve.wait_ge(xm_st[slot // 2], r * 32)
                    nc.vector.tensor_scalar(xm[slot], x2[slot], mv[slot % RS][:, 0:1], rstd[slot % RS], ALU.subtract,
                                            ALU.mult).then_inc(s["xm"], 1)

                def scored(n, slot, r):
                    dve.wait_ge(s["score"], n + 1)
                    nc.vector.tensor_tensor(self.gates[:, ds((n + n0) * NE, NE)], sbank[slot % 2][0:P, 0:NE], self.bg[:, :],
                                            ALU.add).then_inc(s["scored"], 1)
                self.pipeline(dve, [(0, x2_stats), (2, norm), (6, scored)], NT, RX)
                dve.wait_ge(s["scored"], NT)

    def route(self, part):
        nc, NE, NT, ST = self.nc, self.NE, self.NTP, self.STP
        nodes = slice(part * NT, (part + 1) * NT)
        chain, made, counted = (self.sem(f"p6_{part}_{k}") for k in ("chain", "made", "counted"))
        take = self.carve(self.rows_flat[0:P, :])
        grid = lambda flat: flat.rearrange("p (n e) -> p n e", e=NE)
        take(self.NT * NE)
        gates = grid(self.gates)[:, nodes, :]
        first, second, upto, tmp, mark = (grid(take(NT * NE)) for _ in range(5))
        best, ones8 = take(NT), take(NT)
        more = self.carve(self.work)
        fits = more(NE * NT)[0:P].rearrange("p (e j) -> p e j", e=NE)
        past = more(ST * NE)[0:1]
        tile_no, tiles125 = more(ST)[0:1], more(NT)[0:P]
        rank8, per, total, ntile, upto8, base, own = (more(NE)[0:P] for _ in range(7))
        low, eidf = more(128), more(ST)[0:1]
        sums = self.bank[0]

        with nc.Block() as block:
            if part == self.PARTS - 1:
                @block.sync
                def _(sp):
                    self.load_W2(sp, self.W2_early, NE)
                    sp.wait_ge(self.W2_in, 32)

            @block.gpsimd
            def _(pool):
                nc.gpsimd.affine_select(out=low, in_=self.ones[:, :], compare_op=ALU.is_gt, fill=0.0, base=0,
                                        pattern=[[1, 128]], channel_multiplier=-1).then_inc(made, 1)
                nc.gpsimd.iota(tile_no, pattern=[[1, ST]], base=0, channel_multiplier=0,
                               allow_small_or_imprecise_dtypes=True).then_inc(made, 1)
                nc.gpsimd.iota(tiles125, pattern=[[P, NT]], base=0, channel_multiplier=0,
                               allow_small_or_imprecise_dtypes=True).then_inc(made, 1)
                pool.wait_ge(made, 3)

            @block.tensor
            def _(pe):
                pe.wait_ge(made, 3)
                pe.wait_ge(counted, 1)
                nc.tensor.matmul(sums[0:P, 0:NE], low[0:P, 0:P], per, start=True, stop=True)
                nc.tensor.matmul(sums[0:P, NE:2 * NE], self.ones[0:P, 0:P], per, start=True,
                                 stop=True).then_inc(counted, 1)

            @block.vector
            def _(dve):
                c = Steps(dve, chain, 0, None)
                v = nc.vector

                def step(ins):
                    c.did(ins)
                    c.settle()
                step(v.tensor_scalar(rank8, self.iota[:, 0:NE], -1.0, float(NE), ALU.mult, ALU.add))
                step(v.memset(ones8, 1.0))

                def pick(scores, chosen):
                    step(v.tensor_reduce(best, scores, AX.X, ALU.max))
                    step(v.tensor_tensor(tmp, scores, spread(best, 2, NE), ALU.is_equal))
                    step(v.tensor_tensor(mark, tmp, spread(rank8, 1, NT), ALU.mult))
                    step(v.tensor_reduce(best, mark, AX.X, ALU.max))
                    step(v.tensor_tensor(chosen, mark, spread(best, 2, NE), ALU.is_equal))
                pick(gates, first)
                step(v.scalar_tensor_tensor(out=gates, in0=first, scalar=-3.0e38, in1=gates, op0=ALU.mult, op1=ALU.add))
                pick(gates, second)
                step(v.tensor_tensor(mark, first, second, ALU.add))
                for e in range(NE):
                    c.did(v.tensor_tensor_scan(out=upto[:, :, e], data0=ones8, data1=mark[:, :, e], initial=0.0,
                                               op0=ALU.mult, op1=ALU.add))
                c.settle()
                v.tensor_copy(per, upto[:, NT - 1, :]).then_inc(counted, 1)
                dve.wait_ge(counted, 2)
                step(v.tensor_copy(total, sums[0:P, NE:2 * NE]))
                step(v.tensor_copy(own, sums[0:P, 0:NE]))
                dve.wait_ge(made, 3)
                step(v.tensor_tensor(fits, spread(total, 2, NT), spread(tiles125, 1, NE), ALU.is_gt))
                step(v.tensor_reduce(ntile, fits, AX.X, ALU.add))
                step(v.tensor_tensor_scan(out=upto8, data0=ones8[:, 0:NE], data1=ntile, initial=0.0, op0=ALU.mult,
                                          op1=ALU.add))
                step(v.tensor_tensor(base, upto8, ntile, ALU.subtract))
                step(v.tensor_scalar(base, base, float(P), -1.0, ALU.mult, ALU.add))
                step(v.tensor_tensor(base, base, own, ALU.add))
                step(v.tensor_tensor(upto, upto, spread(base, 1, NT), ALU.add))
                for k, chosen in enumerate((first, second)):
                    step(v.tensor_tensor(tmp, upto, chosen, ALU.mult))
                    step(v.tensor_reduce(best, tmp, AX.X, ALU.add))
                    step(v.tensor_copy(self.slots[:, k, nodes], best))
                pastv = past.rearrange("a (j e) -> a j e", e=NE)
                step(v.tensor_tensor(pastv, spread(tile_no, 2, NE), spread(upto8[0:1, :], 1, ST), ALU.is_ge))
                step(v.tensor_reduce(eidf, pastv, AX.X, ALU.add))
                eid = self.eid[0:1, part * (ST // 2) * 4:(part + 1) * (ST // 2) * 4]
                step(v.memset(eid, 0))
                step(v.tensor_scalar(eid.rearrange("a (j k) -> a j k", k=4)[:, :, 0:2],
                                     eidf.rearrange("a (j k) -> a j k", k=2), float(NE - 1), None, ALU.min))

    def move_alone(self, mover):
        with self.nc.Block() as block:
            @block.sync
            def _(sp):
                self.pipeline(sp, mover.sync_stages(1, 2), mover.pairs, 2)
                mover.sync_end(sp)

            @block.gpsimd
            def _(pool):
                mover.gpsimd(pool)

            @block.vector
            def _(dve):
                if stages := mover.vector_stages(1, 2):
                    self.pipeline(dve, stages, mover.pairs, 2)

    def experts(self, part, mover):
        nc, C, ST, NE, H = self.nc, self.C, self.STP, self.NE, self.H
        PER = 4
        HC = H // 128
        s = {k: self.sem(f"p8_{part}_{k}") for k in ("turned", "xT", "W1", "h", "hT", "y", "kept")}
        RX = 8
        x_in, y_st = ([self.sem(f"p8_{part}_{k}{b}") for b in range(RX // 2)] for k in ("x_in", "y_stored"))
        take = self.carve(self.work)
        spare = self.carve(self.onehot[0][:, :, :].rearrange("p a b -> p (a b)"))
        xb2, yb2 = ([piece(2 * C)[0:P].rearrange("p (b c) -> p b c", c=C) for _ in range(RX // 2)]
                    for piece in (take, spare))
        xb, yb = ([buf[b // 2][:, b % 2, :] for b in range(RX)] for buf in (xb2, yb2))
        xT = [take(2 * P).rearrange("p (k n) -> p k n", k=2) for _ in range(2)]
        hT = [take(HC * P) for _ in range(2)]
        W1s = self.W1s
        turn, hbank, ybank = self.bank[0:2], self.bank[2:4], self.bank[4:6]
        WE = self.WE

        last = (mover.pairs * PER) // RX * RX

        def expert_ids(engines, r):
            return nc.values_load_multi_w_load_instructions(
                self.eid[0:1, ds((r + part * (ST // 2)) * 4, 4)], engines=engines, min_val=0, max_val=NE - 1,
                skip_runtime_bounds_check_because="a count of experts, held below their number when made")[1]

        with nc.Block() as block:
            @block.sync
            def _(sp):
                def load(n, slot, r):
                    if slot % 2 == 0:
                        if not isinstance(n, int) or n >= RX:
                            sp.wait_ge(s["turned"], n - (RX - 2))
                        move_rows(sp, xb2[slot // 2], self.pair_rows(self.d_xs[part], n), x_in[slot // 2])

                def store(n, slot, r):
                    if slot % 2 == 0:
                        sp.wait_ge(s["kept"], n + 2)
                        move_rows(sp, self.pair_rows(self.d_ys[part], n), yb2[slot // 2], y_st[slot // 2])
                self.pipeline(sp, mover.sync_stages(PER, RX) + [(0, load), (RX - 1, store)], ST, RX, last)
                for b in range(RX // 2):
                    sp.wait_ge(y_st[b], 32 * len(range(2 * b, ST, RX)))
                mover.sync_end(sp)

            @block.gpsimd
            def _(pool):
                mover.gpsimd(pool)

            @block.tensor
            def _(pe):
                def turned(n, slot, r):
                    par = slot % 2
                    pe.wait_ge(x_in[slot // 2], r * 32 + 32)
                    if not isinstance(n, int) or n > 1:
                        pe.wait_ge(s["xT"], n - 1)
                    for k in range(2):
                        mm = nc.tensor.transpose(turn[par][:, k * P:(k + 1) * P], xb[slot][:, k * 128:(k + 1) * 128],
                                                 self.ident[0:P, 0:P])
                    mm.then_inc(s["turned"], 1)

                def hidden(n, slot, r):
                    par = slot % 2
                    pe.wait_ge(s["xT"], n + 1)
                    pe.wait_ge(s["W1"], n + 1)
                    if not isinstance(n, int) or n > 1:
                        pe.wait_ge(s["hT"], (n - 1) * HC)
                    for c in range(HC):
                        for k in range(2):
                            mm = nc.tensor.matmul(hbank[par][:, c * P:(c + 1) * P],
                                                  W1s[par][:, k * H + c * 128:k * H + (c + 1) * 128], xT[par][:, k, :],
                                                  start=(k == 0), stop=(k == 1))
                    mm.then_inc(s["h"], 1)

                def output(n, slot, r):
                    par = slot % 2
                    if par == 0:
                        self.ids = expert_ids(PE_ONLY, r * (RX // 2) + slot // 2)
                    e = self.ids[par]
                    pe.wait_ge(s["hT"], (n + 1) * HC)
                    if not isinstance(n, int) or n > 1:
                        pe.wait_ge(s["kept"], n - 1)
                    out = ybank[par][0:P, 0:C]
                    for c in range(HC):
                        mm = nc.tensor.matmul(out, hT[par][:, c * P:(c + 1) * P], self.W2e[:, ds(e * (HC * C) + c * C, C)],
                                         start=(c == 0), stop=(c == HC - 1))
                    mm.then_inc(s["y"], 1)
                self.pipeline(pe, [(0, turned), (1, hidden), (2, output)], ST, RX)

            @block.scalar
            def _(act):
                def keep_turned(n, par, r):
                    act.wait_ge(s["turned"], n + 1)
                    if not isinstance(n, int) or n > 1:
                        act.wait_ge(s["h"], n - 1)
                    nc.scalar.activation(xT[par], turn[par][:, 0:2 * P].rearrange("p (k n) -> p k n", k=2),
                                         ACT.Copy).then_inc(s["xT"], 1)

                def gelu(n, par, r):
                    act.wait_ge(s["h"], n + 1)
                    if not isinstance(n, int) or n > 1:
                        act.wait_ge(s["y"], n - 1)
                    for c in range(HC):
                        nc.scalar.activation(hT[par][:, c * P:(c + 1) * P], hbank[par][:, c * P:(c + 1) * P], ACT.Gelu,
                                             bias=W1s[par][:, 2 * H + c:2 * H + c + 1]).then_inc(s["hT"], 1)
                nc.scalar.preload_act_table(ACT.Gelu)
                self.pipeline(act, [(0, keep_turned), (1, gelu)], ST)

            @block.vector
            def _(dve):
                def weights(n, slot, r):
                    par = slot % 2
                    if par == 0:
                        self.ids = expert_ids(DVE_ONLY, r * (RX // 2) + slot // 2)
                    if not isinstance(n, int) or n > 1:
                        dve.wait_ge(s["h"], n - 1)
                        dve.wait_ge(s["hT"], (n - 1) * HC)
                    nc.vector.tensor_copy(W1s[par], self.W1e[:, ds(self.ids[par] * WE, WE)]).then_inc(s["W1"], 1)

                def keep(n, slot, r):
                    par = slot % 2
                    if par == 0:
                        self.kept_ids = expert_ids(DVE_ONLY, r * (RX // 2) + slot // 2)
                    dve.wait_ge(s["y"], n + 1)
                    if not isinstance(n, int) or n >= RX:
                        dve.wait_ge(y_st[slot // 2], r * 32)
                    nc.vector.tensor_tensor(yb[slot], ybank[par][0:P, 0:C], self.b2e[:, ds(self.kept_ids[par] * C, C)],
                                            ALU.add).then_inc(s["kept"], 1)
                self.pipeline(dve, [(0, weights), (2, keep)] + mover.vector_stages(PER, RX), ST, RX, last)

class Mover:

    def __init__(self, k, part, name):
        self.k, self.part, self.name = k, part, name
        self.pairs = k.NTP // 2
        self.first = part * k.NTP
        self.x_in, self.indirect, self.stored = ([k.sem(f"{name}_{n}{b}") for b in range(2)] for n in (
            "x_in", "indirect", "stored"))
        self.indexed = k.sem(name + "_indexed")
        self.take = k.carve(k.onehot[1][:, :, :].rearrange("p a b -> p (a b)"))
        self.take_more = k.carve(k.rows_flat[:, 2 * k.WE:])
        small = k.carve(k.work[:, 4000:4200])
        self.idx = [small(4)[0:P].bitcast(I32).rearrange("p (k b) -> p k b", b=2) for _ in range(2)]

    def pair(self, take):
        return take(2 * self.k.C)[0:P].rearrange("p (b c) -> p b c", c=self.k.C)

    def every(self, per, ring, step):
        def stage(n, slot, r):
            if slot % per == 0 and not (isinstance(n, int) and n // per >= self.pairs):
                h, w = slot // per, ring // per
                step(n // per if isinstance(n, int) else r * w + h, h % 2, r * (w // 2) + h // 2)
        return stage

    def slots_of(self, pool, m, b):
        k = self.k
        k.nc.gpsimd.tensor_copy(self.idx[b], k.slots[:, :, ds(m * 2 + self.first, 2)]).then_inc(self.indexed, 1)
        pool.wait_ge(self.indexed, m * 2 + 1)

    def hold(self):
        k = self.k
        k.nc.gpsimd.tensor_tensor(k.held[:, 0:1], k.held[:, 1:2], k.held[:, 1:2], ALU.add).then_inc(self.indexed, 1)

    def by_slot(self, b, k, h):
        return bass.IndirectOffsetOnAxis(ap=self.idx[b][:, k, h:h + 1], axis=0)

    def uses(self, b):
        return len(range(b, self.pairs, 2))


class Scatter(Mover):

    def __init__(self, k, part):
        super().__init__(k, part, f"scatter{part}")
        self.xm = [self.pair(self.take_more) for _ in range(2)]

    def sync_stages(self, per, ring):
        k = self.k

        def load(m, b, r):
            if not isinstance(m, int) or m > 1:
                k.nc.sync.wait_ge(self.indirect[b], r * 64)
            move_rows(k.nc.sync, self.xm[b], k.pair_rows(k.d_xm, m * 2 + self.first), self.x_in[b])
        return [(0, self.every(per, ring, load))]

    def sync_end(self, sp):
        pass

    def vector_stages(self, per, ring):
        return []

    def gpsimd(self, pool):
        def send(m, b, r):
            if not isinstance(m, int) or m > 1:
                pool.wait_ge(self.indirect[b], r * 64)
            self.slots_of(pool, m, b)
            pool.wait_ge(self.x_in[b], r * 32 + 32)
            self.hold()
            for h in range(2):
                for c in range(2):
                    self.k.nc.gpsimd.indirect_dma_start(self.k.d_xs[self.part], self.by_slot(b, c, h),
                                                        self.xm[b][:, h, :], None).then_inc(self.indirect[b], 16)
        self.k.pipeline(pool, [(0, send)], self.pairs, 2)
        for b in range(2):
            pool.wait_ge(self.indirect[b], 64 * self.uses(b))


class Combine(Mover):

    def __init__(self, k, part, out):
        super().__init__(k, part, f"combine{part}")
        self.out = out
        self.summed, self.done = k.sem(f"combine{part}_summed"), k.sem(f"combine{part}_done")
        self.ya, self.yb = ([self.pair(self.take) for _ in range(2)] for _ in range(2))
        self.x2 = [self.pair(self.take_more) for _ in range(2)]

    def sync_stages(self, per, ring):
        k = self.k

        def store(m, b, r):
            k.nc.sync.wait_ge(self.done, m + 1)
            move_rows(k.nc.sync, k.pair_rows(self.out, m * 2 + self.first), self.x2[b], self.stored[b])

        def load(m, b, r):
            if not isinstance(m, int) or m > 1:
                k.nc.sync.wait_ge(self.stored[b], r * 32)
            move_rows(k.nc.sync, self.x2[b], k.pair_rows(k.d_x2, m * 2 + self.first), self.x_in[b])
        return [(2 * per, self.every(per, ring, store)), (0, self.every(per, ring, load))]

    def sync_end(self, sp):
        for b in range(2):
            sp.wait_ge(self.stored[b], 32 * self.uses(b))

    def vector_stages(self, per, ring):
        k = self.k

        def add(m, b, r):
            k.nc.vector.wait_ge(self.indirect[b], r * 64 + 64)
            k.nc.vector.tensor_tensor(self.ya[b], self.ya[b], self.yb[b], ALU.add).then_inc(self.summed, 1)
            k.nc.vector.wait_ge(self.x_in[b], r * 32 + 32)
            k.nc.vector.wait_ge(self.summed, m + 1)
            k.nc.vector.tensor_tensor(self.x2[b], self.x2[b], self.ya[b], ALU.add).then_inc(self.done, 1)
        return [(per, self.every(per, ring, add))]

    def gpsimd(self, pool):
        def fetch(m, b, r):
            if not isinstance(m, int) or m > 1:
                pool.wait_ge(self.done, m - 1)
            self.slots_of(pool, m, b)
            self.hold()
            for h in range(2):
                for c, y in enumerate((self.ya, self.yb)):
                    self.k.nc.gpsimd.indirect_dma_start(y[b][:, h, :], None, self.k.d_ys[self.part],
                                                        self.by_slot(b, c, h)).then_inc(self.indirect[b], 16)
        self.k.pipeline(pool, [(0, fetch)], self.pairs, 2)


class KeyValueSums:

    def __init__(self, k):
        self.k = k
        self.s = {n: k.sem("kv_" + n) for n in ("k", "v", "kmin", "kexp", "kf", "v_kept", "summed", "ready", "kept")}
        self.ins = [k.sem(f"kv_in{b}") for b in range(2)]
        take = k.carve(k.work)
        self.xnT = [take(2 * P).rearrange("p (a n) -> p a n", a=2) for _ in range(2)]
        self.kmin, self.kf = take(k.C)[0:P], take(k.C)[0:P]
        self.v = take(2 * 129)[0:P].rearrange("p (a m) -> p a m", a=2)
        self.zero = take(260)
        self.kb, self.vb, self.acc = k.bank[2:5]

    def sync(self, sp):
        k = self.k

        def load(n, par):
            sp.dma_start(self.xnT[par].rearrange("p a n -> p (a n)"),
                         k.d_xnT[ds(n, 1), :, :].rearrange("a p f -> (a p) f")).then_inc(self.ins[par], 16)
        load(0, 0)
        load(1, 1)
        sp.wait_ge(k.zeros_made, 1)
        loops, w = k.NT // 2 - 1, 2
        with sp.Fori(0, loops) as i:
            for par in range(2):
                sp.wait_ge(self.s["v"], i * 2 + (par + 1))
                load(i * 2 + (par + 2), par)
                k.zero_slots(sp, par, i * w, w)
        for part in range(k.PARTS):
            k.zero_slots(sp, part, loops * w, k.STP - loops * w)
        sp.wait_ge(k.slots_zeroed, 16 * k.PARTS * (loops + 1))

    def pe_start(self, pe):
        pe.wait_ge(self.s["ready"], 2)
        self.k.nc.tensor.matmul(self.acc[:, 0:258], self.zero[:, 0:128], self.zero[:, 0:258], start=True, stop=False,
                                skip_group_check=True)

    def pe(self, pe, n, par, r, e):
        k, s, mm = self.k, self.s, self.k.nc.tensor.matmul
        if e == 1:
            pe.wait_ge(self.ins[par], r * 16 + 16)
            for w0, out, name in ((k.C, self.kb, "k"), (2 * k.C, self.vb, "v")):
                for c in range(2):
                    last = mm(out[0:P, 0:k.C], self.xnT[par][:, c, :], k.Wqkv[:, c, w0:w0 + k.C],
                              start=(c == 0), stop=(c == 1))
                last.then_inc(s[name], 1)
        if e == 9:
            pe.wait_ge(s["kf"], n + 1)
            pe.wait_ge(s["v_kept"], n + 1)
            for a in range(2):
                last = mm(self.acc[:, a * 129:(a + 1) * 129], self.kf[:, a * 128:(a + 1) * 128], self.v[:, a, :],
                          start=False, stop=False, skip_group_check=True)
            last.then_inc(s["summed"], 1)

    def scalar(self, act):
        k, s, nc = self.k, self.s, self.k.nc
        nc.scalar.preload_act_table_set("exp_and_others")
        act.wait_ge(s["ready"], 2)

        def tile(n):
            act.wait_ge(s["kmin"], n + 1)
            nc.scalar.activation(self.kmin, self.kmin, ACT.Exp).then_inc(s["kexp"], 1)
            act.wait_ge(s["v"], n + 1)
            if not isinstance(n, int):
                act.wait_ge(s["summed"], n)
            nc.scalar.activation(self.v[:, :, 0:128], self.vb[0:P, 0:k.C].rearrange("p (a m) -> p a m", a=2),
                                 ACT.Copy).then_inc(s["v_kept"], 1)
        tile(0)
        with act.Fori(1, k.NT) as n:
            tile(n)

    def dve(self, dve, n, par, r, e):
        k, s, nc = self.k, self.s, self.k.nc
        if e == 3:
            dve.wait_ge(s["k"], n + 1)
            nc.vector.tensor_scalar(self.kmin, self.kb[0:P, 0:k.C], 0.0, None, ALU.min).then_inc(s["kmin"], 1)
        if e == 6:
            dve.wait_ge(s["kexp"], n + 1)
            nc.vector.scalar_tensor_tensor(out=self.kf, in0=self.kb[0:P, 0:k.C], scalar=0.0, in1=self.kmin,
                                           op0=ALU.max, op1=ALU.add).then_inc(s["kf"], 1)

    def pe_end(self, pe):
        pass

    def dve_start(self, dve):
        self.k.nc.vector.memset(self.zero, 0.0).then_inc(self.s["ready"], 1)
        self.k.nc.vector.memset(self.v[:, :, 128:129], 1.0).then_inc(self.s["ready"], 1)

    def dve_end(self, dve):
        k, nc = self.k, self.k.nc
        dve.wait_ge(self.s["summed"], k.NT)
        for a in range(2):
            for h in range(4):
                q = slice(32 * h, 32 * h + 32)
                for to, of, w in ((32 * h, a * 129 + 32 * h, 32), (128 + h, a * 129 + 128, 1)):
                    nc.vector.tensor_copy(k.kvbd[q, a, to:to + w], self.acc[q, of:of + w]).then_inc(self.s["kept"], 1)
        dve.wait_ge(self.s["kept"], 16)


class Mixer:

    FIRST_STEPS, SECOND_STEPS = 6, 5

    def __init__(self, k):
        self.k = k
        C = k.C
        self.s = {n: k.sem("mix_" + n) for n in (
            "q", "qmin", "qexp", "qf", "t", "var1", "ln1", "std1", "x1", "x1_turned", "x1T", "h", "hT", "y", "var2",
            "ln2", "std2", "res", "chain1", "chain2")}
        self.ins = [k.sem(f"mix_in{b}") for b in range(2)]
        self.x_in = [k.sem(f"mix_x_in{b}") for b in range(2)]
        self.stored = [k.sem(f"mix_stored{b}") for b in range(2)]
        take = k.carve(k.work)
        rows = lambda: take(C)[0:P]
        cols = lambda: take(2 * P).rearrange("p (a n) -> p a n", a=2)
        self.x, self.xn = [rows() for _ in range(2)], [rows() for _ in range(2)]
        self.xnT = [cols() for _ in range(2)]
        self.res = [rows() for _ in range(2)]
        self.qm, self.qf, self.x1T, self.hT = cols(), cols(), cols(), cols()
        self.r1, self.r2, self.x1 = rows(), rows(), rows()
        small = take(40)[0:P]
        self.den, self.rden = (small[:, 8 * i:8 * i + 8].rearrange("p (a h) -> p a h", a=2) for i in range(2))
        self.st = [small[:, 16 + 6 * i:22 + 6 * i] for i in range(2)]
        self.mv = [small[:, 28 + 2 * i:30 + 2 * i] for i in range(2)]
        self.rstd = [small[:, 32 + i:33 + i] for i in range(2)]
        self.scratch = small[0:1, 34:35]
        self.qb, self.tb, self.turnb, self.hb, self.yb = k.bank[2:7]

    def sync(self, sp):
        k = self.k

        def load(n, par):
            move_rows(sp, self.xn[par], k.tile_rows(k.d_xn, n), self.ins[par])
            sp.dma_start(self.xnT[par].rearrange("p a n -> p (a n)"),
                         k.d_xnT[ds(n, 1), :, :].rearrange("a p f -> (a p) f")).then_inc(self.ins[par], 16)

        def load_x(n, par):
            move_rows(sp, self.x[par], k.tile_rows(k.t["x"], n), self.x_in[par])

        def store(n, par):
            sp.wait_ge(self.s["res"], n + 1)
            move_rows(sp, k.tile_rows(k.d_xmix, n), self.res[par], self.stored[par])

        for b in range(2):
            load(b, b)
            load_x(b, b)
        sp.wait_ge(self.s["x1"], 1)
        load(2, 0)
        with sp.Fori(0, k.NT // 2 - 2) as i:
            for par in range(2):
                n = i * 2 + par
                sp.wait_ge(self.s["x1"], n + 2)
                load(n + 3, 1 - par)
                store(n, par)
                load_x(n + 2, par)
        for n in range(k.NT - 4, k.NT):
            if n == k.NT - 4:
                sp.wait_ge(self.s["x1"], n + 2)
                load(n + 3, 1)
            store(n, n % 2)
            if n < k.NT - 2:
                load_x(n + 2, n % 2)
            k.load_experts(sp, n - (k.NT - 4))
        for par in range(2):
            sp.wait_ge(self.stored[par], 32 * (k.NT // 2) + 32)
        sp.wait_ge(k.W1_in, 16 * 6)

    def pe_start(self, pe):
        pass

    def dve_start(self, dve):
        for par in range(2):
            dve.sem_inc(self.stored[par], 32)

    def pe(self, pe, n, par, r, e):
        k, s, mm = self.k, self.s, self.k.nc.tensor.matmul
        first = not isinstance(n, int) or n < k.NT
        second = not isinstance(n, int) or n > 0
        if e == 0 and second:
            pe.wait_ge(s["x1T"], n)
            for a in range(2):
                for c in range(2):
                    last = mm(self.hb[:, a * P:(a + 1) * P], k.mW1[:, c, a * 128:(a + 1) * 128], self.x1T[:, c, :],
                              start=(c == 0), stop=(c == 1))
            last.then_inc(s["h"], 1)
        if e == 1 and first:
            pe.wait_ge(self.ins[par], (r + 1) * 48)
            for a in range(2):
                for c in range(2):
                    last = mm(self.qb[:, a * P:(a + 1) * P], k.Wqkv[:, c, a * 128:(a + 1) * 128], self.xnT[par][:, c, :],
                              start=(c == 0), stop=(c == 1))
            last.then_inc(s["q"], 1)
        if e == 5 and second:
            pe.wait_ge(s["hT"], n * 2)
            for c in range(2):
                last = mm(self.yb[0:P, 0:k.C], self.hT[:, c, :], k.mW2[:, c, :], start=(c == 0), stop=(c == 1))
            last.then_inc(s["y"], 1)
        if e == 7 and first:
            pe.wait_ge(s["qf"], n + 1)
            for a in range(2):
                last = mm(self.tb[0:P, a * 132:(a + 1) * 132], self.qf[:, a, :], k.kvbd[:, a, :], start=True, stop=True)
            last.then_inc(s["t"], 1)
        if e == 15 and first:
            pe.wait_ge(s["x1"], n + 1)
            for a in range(2):
                last = k.nc.tensor.transpose(self.turnb[:, a * P:(a + 1) * P], self.x1[:, a * 128:(a + 1) * 128],
                                             k.ident[0:P, 0:P])
            last.then_inc(s["x1_turned"], 1)

    def scalar(self, act):
        k, s, nc = self.k, self.s, self.k.nc

        def group(n, first=True, second=True):
            if second:
                nc.scalar.preload_act_table_set("gelu_and_others")
                act.wait_ge(s["h"], n)
                for a in range(2):
                    nc.scalar.activation(self.hT[:, a, :], self.hb[:, a * P:(a + 1) * P], ACT.Gelu,
                                         bias=k.mb1[:, a:a + 1]).then_inc(s["hT"], 1)
            nc.scalar.preload_act_table_set("natural_log_exp_and_others")
            if first:
                act.wait_ge(s["qmin"], n + 1)
                nc.scalar.activation(self.qm, self.qm, ACT.Exp).then_inc(s["qexp"], 1)
            if second:
                act.wait_ge(s["var2"], n)
                k.inverse_std(act, self.rstd[1], self.mv[1][:, 1:2], s["ln2"], n, s["std2"])
            if first:
                act.wait_ge(s["var1"], n + 1)
                k.inverse_std(act, self.rstd[0], self.mv[0][:, 1:2], s["ln1"], n + 1, s["std1"])
                act.wait_ge(s["x1_turned"], n + 1)
                nc.scalar.activation(self.x1T, self.turnb[:, 0:2 * P].rearrange("p (a n) -> p a n", a=2),
                                     ACT.Copy).then_inc(s["x1T"], 1)
        group(0, second=False)
        with act.Fori(1, k.NT) as n:
            group(n)
        group(k.NT, first=False)

    def dve(self, dve, n, par, r, e):
        k, s, nc, C = self.k, self.s, self.k.nc, self.k.C
        first = not isinstance(n, int) or n < k.NT
        second = not isinstance(n, int) or n > 0
        if e == 0:
            self.c1 = Steps(dve, s["chain1"], n * self.FIRST_STEPS, self.FIRST_STEPS)
            self.c2 = Steps(dve, s["chain2"], (n - 1) * self.SECOND_STEPS, self.SECOND_STEPS)
        both = lambda b, w: b.rearrange("p (a n) -> p a n", a=2)

        def stats(c, half, r, var):
            c.did(nc.vector.bn_stats(self.st[half], r))
            c.settle()
            nc.vector.memset(self.scratch, 0.0)
            nc.vector.bn_aggr(self.mv[half], self.st[half]).then_inc(s[var], 1)

        def centred(c, half, r, g):
            c.did(nc.vector.scalar_tensor_tensor(out=r, in0=r, scalar=self.mv[half][:, 0:1], in1=k.brow[g][:, :],
                                                 op0=ALU.subtract, op1=ALU.mult))

        if e == 3 and first:
            dve.wait_ge(s["q"], n + 1)
            nc.vector.tensor_scalar(self.qm, both(self.qb[:, 0:2 * P], P), 0.0, None, ALU.min).then_inc(s["qmin"], 1)
        if e == 6 and first:
            dve.wait_ge(s["qexp"], n + 1)
            nc.vector.scalar_tensor_tensor(out=self.qf, in0=both(self.qb[:, 0:2 * P], P), scalar=0.0, in1=self.qm,
                                           op0=ALU.max, op1=ALU.add).then_inc(s["qf"], 1)
        if e == 7 and second:
            dve.wait_ge(s["y"], n)
            self.c2.did(nc.vector.tensor_tensor(self.r2, self.yb[0:P, 0:C], self.x1, ALU.add))
            self.c2.settle()
        if e == 8 and second:
            self.c2.did(nc.vector.tensor_tensor(self.r2, self.r2, k.brow["mix_b2"][:, :], ALU.add))
            self.c2.settle()
            stats(self.c2, 1, self.r2, "var2")
        if e == 9 and first:
            dve.wait_ge(s["t"], n + 1)
            t = self.tb[0:P, 0:264].rearrange("p (a m) -> p a m", a=2)
            self.c1.did(nc.vector.tensor_scalar(self.den, t[:, :, 128:132], EPS_ATTN, None, ALU.add))
            self.c1.settle()
            self.c1.did(nc.vector.reciprocal(self.rden, self.den))
            self.c1.settle()
            self.c1.did(nc.vector.tensor_tensor(self.r1.rearrange("p (a h m) -> p a h m", a=2, h=4),
                                                t[:, :, 0:128].rearrange("p a (h m) -> p a h m", h=4),
                                                spread(self.rden, 3, 32), ALU.mult))
            self.c1.settle()
        if e == 10 and first:
            self.c1.did(nc.vector.tensor_tensor(self.r1, self.r1, self.xn[par], ALU.add))
            self.c1.settle()
            stats(self.c1, 0, self.r1, "var1")
        if e == 11:
            if second:
                dve.wait_ge(s["var2"], n)
                centred(self.c2, 1, self.r2, "ln2_g")
                self.c2.settle()
                dve.wait_ge(s["std2"], n)
                self.c2.did(nc.vector.scalar_tensor_tensor(out=self.r2, in0=self.r2, scalar=self.rstd[1],
                                                           in1=k.brow["ln2_b"][:, :], op0=ALU.mult, op1=ALU.add))
            if first:
                dve.wait_ge(s["var1"], n + 1)
                centred(self.c1, 0, self.r1, "ln1_g")
        if e == 12 and second:
            self.c2.settle()
            dve.wait_ge(self.x_in[1 - par], r * 32 + 32 * par)
            dve.wait_ge(self.stored[1 - par], r * 32 + 32 * par)
            nc.vector.tensor_tensor(self.res[1 - par], self.r2, self.x[1 - par], ALU.add).then_inc(s["res"], 1)
            self.c2.end()
        if e == 13 and first:
            self.c1.settle()
            dve.wait_ge(s["std1"], n + 1)
            nc.vector.scalar_tensor_tensor(out=self.x1, in0=self.r1, scalar=self.rstd[0], in1=k.brow["ln1_b"][:, :],
                                           op0=ALU.mult, op1=ALU.add).then_inc(s["x1"], 1)
            self.c1.end()

    def pe_end(self, pe):
        for e in range(self.k.EPT):
            self.pe(pe, self.k.NT, 0, self.k.NT // 2, e)

    def dve_end(self, dve):
        for e in range(self.k.EPT):
            self.dve(dve, self.k.NT, 0, self.k.NT // 2, e)


def run_layer(nc, t, out):
    with ExitStack() as ctx:
        k = Kernel(nc, ctx, t)
        k.allocate()
        k.setup()
        k.end_phase()
        k.project()
        k.scale_nodes()
        k.end_phase()
        k.aggregate("agg1", k.t_g1, KeyValueSums(k))
        k.strays("strays1", k.t_g1)
        k.end_phase()
        k.between()
        k.aggregate("agg2", k.t_g2, Mixer(k))
        k.strays("strays2", k.t_g2)
        k.end_phase()
        k.gate(0)
        k.route(0)
        k.end_phase()
        k.gate(1, Scatter(k, 0))
        k.route(1)
        k.end_phase()
        k.experts(0, Scatter(k, 1))
        k.end_phase()
        k.experts(1, Combine(k, 0, out))
        k.end_phase()
        k.move_alone(Combine(k, 1, out))


_NAMES = {"x": "x", "src": "src", "dst": "dst", "gnn_W1": "L0_gnn_W1", "gnn_b1": "L0_gnn_b1", "gnn_W2": "L0_gnn_W2",
          "gnn_b2": "L0_gnn_b2", "mix_WqkvT": "L0_mix_Wqkv", "ln1_g": "L0_mix_ln1_g", "ln1_b": "L0_mix_ln1_b",
          "mix_W1T": "L0_mix_W1", "mix_b1": "L0_mix_b1", "mix_W2T": "L0_mix_W2", "mix_b2": "L0_mix_b2",
          "ln2_g": "L0_mix_ln2_g", "ln2_b": "L0_mix_ln2_b", "ffn_Wg": "L0_ffn_Wg", "ffn_bg": "L0_ffn_bg",
          "ffn_W1": "L0_ffn_W1", "ffn_b1": "L0_ffn_b1", "ffn_W2": "L0_ffn_W2", "ffn_b2": "L0_ffn_b2"}


def _laid_out(name, a):
    if name in ("mix_WqkvT", "mix_W1T", "mix_W2T"):
        return a.T
    if name == "mix_b1":
        return a.reshape(-1, 128).T
    if name == "ffn_W1":
        e, d, h = a.shape
        return a.reshape(e, d // 128, 128, h).transpose(2, 0, 1, 3)
    if name == "ffn_W2":
        e, h, d = a.shape
        return a.reshape(e, h // 128, 128, d).transpose(2, 0, 1, 3)
    if name == "ffn_b1":
        return a.reshape(a.shape[0], -1, 128).transpose(2, 0, 1)
    return a


def kernel(**inputs):
    import numpy as _np
    import concourse.bacc as _bacc
    from concourse.bass_utils import run_bass_kernel_spmd as _run

    nc = _bacc.Bacc("TRN2", target_bir_lowering=False, num_devices=1)
    arrays, t = {}, {}
    for name, given in _NAMES.items():
        a = _np.ascontiguousarray(_laid_out(name, _np.asarray(inputs[given])))
        arrays[f"in_{name}"] = a
        t[name] = nc.dram_tensor(f"in_{name}", a.shape, mybir.dt.from_np(a.dtype), kind="ExternalInput").ap()
    out = nc.dram_tensor("out_0", arrays["in_x"].shape, F32, kind="ExternalOutput").ap()
    run_layer(nc, t, out)
    r = _run(nc, [arrays], core_ids=[0])
    return r.results[0]["out_0"]
```
